# Optimizing a Trainium2 kernel written in Bass

```python
import numpy as np
import jax
import jax.numpy as jnp

def _softmax(x, axis=-1):
    return jax.nn.softmax(x, axis=axis)

def _gelu(x):
    return jax.nn.gelu(x, approximate=True)

def _silu(x):
    return jax.nn.silu(x)

def _sigmoid(x):
    return jax.nn.sigmoid(x)

def _layernorm(x, axis=-1, eps=1e-05):
    m = jnp.mean(x, axis=axis, keepdims=True)
    v = jnp.var(x, axis=axis, keepdims=True)
    return (x - m) / jnp.sqrt(v + eps)

def _scatter_add(tgt, idx, src, axis=0):
    return tgt.at[idx].add(src)

def _segment_sum(src, seg, n):
    return jax.ops.segment_sum(src, seg, n)
kernel_name = 'mk_gps_d2_gnn_r8_2fac3e'

def setup_inputs(seed: int=0):
    np.random.seed(seed)
    _w = jnp.asarray

    def _rec_inputs():
        import jax
        import jax.numpy as jnp
        _gk = jax.random.key(seed)
        x = -0.0003713 + 1 * jax.random.normal(jax.random.fold_in(_gk, 1), (6250, 256), jnp.float32)
        _s = jax.random.randint(jax.random.fold_in(_gk, 2), (50000,), 0, 6250, jnp.int32)
        _d = jax.random.randint(jax.random.fold_in(_gk, 3), (50000,), 0, 6250, jnp.int32)
        _loop = jnp.arange(6250, dtype=jnp.int32)
        src = jnp.concatenate([_s, _d, _loop])
        dst = jnp.concatenate([_d, _s, _loop])
        _o = jnp.argsort(dst, stable=True)
        src = src[_o]
        dst = dst[_o]
        return (x, src, dst)
    x, src, dst = _rec_inputs()

    def _L0_gnn_setup():
        import jax, jax.numpy as jnp
        import numpy as np
        N_NODES = 6250
        N_EDGES = 100000
        D_IN = 256
        D_OUT = 256
        key = jax.random.key(seed)
        k1, k2, k3, k4, k5, k6 = jax.random.split(key, 6)
        nodes = jax.random.normal(k1, (N_NODES, D_IN), dtype=jnp.float32)
        senders = jax.random.randint(k2, (N_EDGES,), 0, N_NODES, dtype=jnp.int32)
        receivers = jax.random.randint(k3, (N_EDGES,), 0, N_NODES, dtype=jnp.int32)
        W_left = jax.random.normal(k4, (2 * D_IN, D_OUT), dtype=jnp.float32) / np.sqrt(2 * D_IN)
        b_left = jnp.zeros((D_OUT,), dtype=jnp.float32)
        W_right = jax.random.normal(k5, (D_IN, D_OUT), dtype=jnp.float32) / np.sqrt(D_IN)
        return {'nodes': nodes, 'senders': senders, 'receivers': receivers, 'W_left': W_left, 'b_left': b_left, 'W_right': W_right}
    _L0_gnn_all = _L0_gnn_setup()
    _L0_gnn_in = {k: v for k, v in _L0_gnn_all.items() if k in ('W_left', 'b_left', 'W_right')}
    del _L0_gnn_all

    def _L0_mix_setup():
        import jax, jax.numpy as jnp
        import numpy as np
        HEADS, DIM_HEAD = (8, 64)
        EPS = 1e-05

        def instance_norm(t):
            mu = jnp.mean(t, axis=-1, keepdims=True)
            var = jnp.mean((t - mu) ** 2, axis=-1, keepdims=True)
            return (t - mu) * jax.lax.rsqrt(var + EPS)
        key = jax.random.key(seed)
        k1, k2, k3, k4 = jax.random.split(key, 4)
        B, N, D = (8, 1024, 256)
        inner = HEADS * DIM_HEAD
        x = jax.random.normal(k1, (B, N, D), jnp.float32)
        w_qkv = jax.random.normal(k2, (3 * inner, D), jnp.float32) / np.sqrt(D).astype(np.float32)
        w_out = jax.random.normal(k3, (D, inner), jnp.float32) / np.sqrt(inner).astype(np.float32)
        b_out = 0.01 * jax.random.normal(k4, (D,), jnp.float32)
        return {'x': x, 'w_qkv': w_qkv, 'w_out': w_out, 'b_out': b_out}
    _L0_mix_all = _L0_mix_setup()
    _L0_mix_in = {k: v for k, v in _L0_mix_all.items() if k in ('w_qkv', 'w_out', 'b_out')}
    del _L0_mix_all

    def _L0_ffn_setup():
        import jax, jax.numpy as jnp
        import numpy as np
        BN_EPS = 0.001

        def _bn(h, g, b, m, v):
            return g * (h - m) * jax.lax.rsqrt(v + BN_EPS) + b
        key = jax.random.key(seed)
        ks = jax.random.split(key, 8)
        B, F, Df = (256, 64, 256)
        E, H, D = (8, 256, 256)
        s1 = 1.0 / np.sqrt(Df)
        s2 = 1.0 / np.sqrt(H)
        return {'x': jax.random.normal(ks[0], (B, F, Df), jnp.float32), 'Wr': jax.random.normal(ks[1], (Df, E), jnp.float32) * s1, 'br': jnp.zeros((E,), jnp.float32), 'W1': jax.random.normal(ks[2], (E, Df, H), jnp.float32) * s1, 'b1': jnp.zeros((E, H), jnp.float32), 'g1': jnp.ones((E, H), jnp.float32), 'be1': jnp.zeros((E, H), jnp.float32), 'm1': jnp.zeros((E, H), jnp.float32), 'v1': jnp.ones((E, H), jnp.float32), 'W2': jax.random.normal(ks[3], (E, H, H), jnp.float32) * s2, 'b2': jnp.zeros((E, H), jnp.float32), 'g2': jnp.ones((E, H), jnp.float32), 'be2': jnp.zeros((E, H), jnp.float32), 'm2': jnp.zeros((E, H), jnp.float32), 'v2': jnp.ones((E, H), jnp.float32), 'Wo': jax.random.normal(ks[4], (E, H, D), jnp.float32) * s2, 'bo': jnp.zeros((E, D), jnp.float32)}
    _L0_ffn_all = _L0_ffn_setup()
    _L0_ffn_in = {k: v for k, v in _L0_ffn_all.items() if k in ('Wr', 'br', 'W1', 'b1', 'g1', 'be1', 'm1', 'v1', 'W2', 'b2', 'g2', 'be2', 'm2', 'v2', 'Wo', 'bo')}
    del _L0_ffn_all

    def _L1_gnn_setup():
        import jax, jax.numpy as jnp
        import numpy as np
        N_NODES = 1250
        N_EDGES = 40000
        D_IN = 256
        D_OUT = 256
        MAX_NORM = 0.95

        def _expmap0(u):
            un = jnp.linalg.norm(u, axis=-1, keepdims=True)
            un_c = jnp.maximum(un, 1e-15)
            return jnp.tanh(un_c) * u / un_c
        key = jax.random.key(seed)
        ks = jax.random.split(key, 7)
        x = jax.random.normal(ks[0], (N_NODES, D_IN), dtype=jnp.float32)
        edge_index = jax.random.randint(ks[1], (2, N_EDGES), 0, N_NODES, dtype=jnp.int64)
        W = jax.random.normal(ks[2], (D_OUT, D_IN), dtype=jnp.float32) * (1.0 / np.sqrt(D_IN))
        b = jax.random.normal(ks[3], (D_OUT,), dtype=jnp.float32) * 0.02
        mag_w = jax.random.normal(ks[4], (1, D_IN), dtype=jnp.float32) * 0.02
        mag_b = jax.random.normal(ks[5], (1,), dtype=jnp.float32) * 0.02
        attn_w = jax.random.normal(ks[6], (1, 2 * D_OUT), dtype=jnp.float32) * (1.0 / np.sqrt(2 * D_OUT))
        return {'x': x, 'edge_index': edge_index, 'W': W, 'b': b, 'mag_w': mag_w, 'mag_b': mag_b, 'attn_w': attn_w}
    _L1_gnn_all = _L1_gnn_setup()
    _L1_gnn_in = {k: v for k, v in _L1_gnn_all.items() if k in ('W', 'b', 'mag_w', 'mag_b', 'attn_w')}
    del _L1_gnn_all

    def _L1_mix_setup():
        import jax, jax.numpy as jnp
        import numpy as np
        HEADS = 4
        DIM_HEAD = 32
        key = jax.random.key(seed)
        k1, k2, k3 = jax.random.split(key, 3)
        B, L, D = (16, 1024, 256)
        hidden = HEADS * DIM_HEAD
        x = jax.random.normal(k1, (B, L, D), dtype=jnp.float32)
        W_qkv = jax.random.normal(k2, (D, 3 * hidden), dtype=jnp.float32) * D ** (-0.5)
        W_out = jax.random.normal(k3, (hidden, D), dtype=jnp.float32) * hidden ** (-0.5)
        b_out = jnp.zeros((D,), dtype=jnp.float32)
        return {'x': x, 'W_qkv': W_qkv, 'W_out': W_out, 'b_out': b_out}
    _L1_mix_all = _L1_mix_setup()
    _L1_mix_in = {k: v for k, v in _L1_mix_all.items() if k in ('W_qkv', 'W_out', 'b_out')}
    del _L1_mix_all

    def _L1_ffn_setup():
        import jax, jax.numpy as jnp
        import numpy as np
        NUM_EXPERTS = 8
        TOP_K = 2
        B, S, D = (8, 1024, 256)

        def _moe(tokens, router_w, w1, b1, w2, b2):
            N = tokens.shape[0]
            E = router_w.shape[0]
            logits = tokens.astype(jnp.float32) @ router_w.astype(jnp.float32).T
            probs = jax.nn.softmax(logits, axis=-1)
            rw, re = jax.lax.top_k(probs, TOP_K)
            if TOP_K > 1:
                rw = rw / jnp.maximum(rw.sum(-1, keepdims=True), 1e-12)
            rw = rw.astype(tokens.dtype)
            combine = jnp.zeros((N, E), tokens.dtype).at[jnp.arange(N)[:, None], re].set(rw)
            out = tokens
            for e in range(E):
                h = jax.nn.gelu(tokens @ w1[e] + b1[e], approximate=False)
                y = h @ w2[e] + b2[e]
                out = out + combine[:, e:e + 1] * y
            return out
        key = jax.random.key(seed)
        ks = jax.random.split(key, 4)
        scale = 1.0 / np.sqrt(D).astype(np.float32)
        return {'input_embeddings': jax.random.normal(ks[0], (B, S, D), jnp.float32), 'router_w': jax.random.normal(ks[1], (NUM_EXPERTS, D), jnp.float32) * scale, 'w1': jax.random.normal(ks[2], (NUM_EXPERTS, D, D), jnp.float32) * scale, 'b1': jnp.zeros((NUM_EXPERTS, D), jnp.float32), 'w2': jax.random.normal(ks[3], (NUM_EXPERTS, D, D), jnp.float32) * scale, 'b2': jnp.zeros((NUM_EXPERTS, D), jnp.float32)}
    _L1_ffn_all = _L1_ffn_setup()
    _L1_ffn_in = {k: v for k, v in _L1_ffn_all.items() if k in ('router_w', 'w1', 'b1', 'w2', 'b2')}
    del _L1_ffn_all
    return {'x': x, 'src': src, 'dst': dst, 'L0_gnn_W_left': _L0_gnn_in['W_left'], 'L0_gnn_b_left': _L0_gnn_in['b_left'], 'L0_gnn_W_right': _L0_gnn_in['W_right'], 'L0_mix_w_qkv': _L0_mix_in['w_qkv'], 'L0_mix_w_out': _L0_mix_in['w_out'], 'L0_mix_b_out': _L0_mix_in['b_out'], 'L0_ffn_Wr': _L0_ffn_in['Wr'], 'L0_ffn_br': _L0_ffn_in['br'], 'L0_ffn_W1': _L0_ffn_in['W1'], 'L0_ffn_b1': _L0_ffn_in['b1'], 'L0_ffn_g1': _L0_ffn_in['g1'], 'L0_ffn_be1': _L0_ffn_in['be1'], 'L0_ffn_m1': _L0_ffn_in['m1'], 'L0_ffn_v1': _L0_ffn_in['v1'], 'L0_ffn_W2': _L0_ffn_in['W2'], 'L0_ffn_b2': _L0_ffn_in['b2'], 'L0_ffn_g2': _L0_ffn_in['g2'], 'L0_ffn_be2': _L0_ffn_in['be2'], 'L0_ffn_m2': _L0_ffn_in['m2'], 'L0_ffn_v2': _L0_ffn_in['v2'], 'L0_ffn_Wo': _L0_ffn_in['Wo'], 'L0_ffn_bo': _L0_ffn_in['bo'], 'L1_gnn_W': _L1_gnn_in['W'], 'L1_gnn_b': _L1_gnn_in['b'], 'L1_gnn_mag_w': _L1_gnn_in['mag_w'], 'L1_gnn_mag_b': _L1_gnn_in['mag_b'], 'L1_gnn_attn_w': _L1_gnn_in['attn_w'], 'L1_mix_W_qkv': _L1_mix_in['W_qkv'], 'L1_mix_W_out': _L1_mix_in['W_out'], 'L1_mix_b_out': _L1_mix_in['b_out'], 'L1_ffn_router_w': _L1_ffn_in['router_w'], 'L1_ffn_w1': _L1_ffn_in['w1'], 'L1_ffn_b1': _L1_ffn_in['b1'], 'L1_ffn_w2': _L1_ffn_in['w2'], 'L1_ffn_b2': _L1_ffn_in['b2']}

def reference(x, src, dst, L0_gnn_W_left, L0_gnn_b_left, L0_gnn_W_right, L0_mix_w_qkv, L0_mix_w_out, L0_mix_b_out, L0_ffn_Wr, L0_ffn_br, L0_ffn_W1, L0_ffn_b1, L0_ffn_g1, L0_ffn_be1, L0_ffn_m1, L0_ffn_v1, L0_ffn_W2, L0_ffn_b2, L0_ffn_g2, L0_ffn_be2, L0_ffn_m2, L0_ffn_v2, L0_ffn_Wo, L0_ffn_bo, L1_gnn_W, L1_gnn_b, L1_gnn_mag_w, L1_gnn_mag_b, L1_gnn_attn_w, L1_mix_W_qkv, L1_mix_W_out, L1_mix_b_out, L1_ffn_router_w, L1_ffn_w1, L1_ffn_b1, L1_ffn_w2, L1_ffn_b2):
    import jax
    import jax.numpy as jnp

    def _L0_gnn_ref(nodes, senders, receivers, W_left, b_left, W_right):
        import jax, jax.numpy as jnp
        import numpy as np
        N_NODES = 6250
        N_EDGES = 100000
        D_IN = 256
        D_OUT = 256
        num_nodes = nodes.shape[0]
        seg_sum = jax.ops.segment_sum(nodes[senders], receivers, num_segments=num_nodes)
        counts = jax.ops.segment_sum(jnp.ones_like(receivers, dtype=nodes.dtype), receivers, num_segments=num_nodes)
        h_neigh = seg_sum / jnp.maximum(counts, 1.0)[:, None]
        h = jnp.concatenate((nodes, h_neigh), axis=1)
        out = h @ W_left + b_left
        out = out + nodes @ W_right
        return out

    def _L0_mix_ref(x, w_qkv, w_out, b_out):
        import jax, jax.numpy as jnp
        import numpy as np
        HEADS, DIM_HEAD = (8, 64)
        EPS = 1e-05

        def instance_norm(t):
            mu = jnp.mean(t, axis=-1, keepdims=True)
            var = jnp.mean((t - mu) ** 2, axis=-1, keepdims=True)
            return (t - mu) * jax.lax.rsqrt(var + EPS)
        B, N, _ = x.shape
        H, Dh = (HEADS, DIM_HEAD)
        qkv = jnp.einsum('bnd,ed->bne', x, w_qkv)
        q, k, v = jnp.split(qkv, 3, axis=-1)

        def to_heads(t):
            return t.reshape(B, N, H, Dh).transpose(0, 2, 1, 3)
        q, k, v = (to_heads(q), to_heads(k), to_heads(v))
        k = instance_norm(k)
        v = instance_norm(v)
        dots = jnp.einsum('bhnd,bhne->bhde', k, v)
        out = jnp.einsum('bhnd,bhde->bhne', q, dots) / N
        out = out.transpose(0, 2, 1, 3).reshape(B, N, H * Dh)
        return jnp.einsum('bne,de->bnd', out, w_out) + b_out

    def _L0_ffn_ref(x, Wr, br, W1, b1, g1, be1, m1, v1, W2, b2, g2, be2, m2, v2, Wo, bo):
        import jax, jax.numpy as jnp
        import numpy as np
        BN_EPS = 0.001

        def _bn(h, g, b, m, v):
            return g * (h - m) * jax.lax.rsqrt(v + BN_EPS) + b
        feat = jnp.mean(x, axis=0)
        w = jax.nn.softmax(feat @ Wr + br, axis=-1)
        h = jnp.einsum('bfd,edh->bfeh', x, W1) + b1
        h = jax.nn.relu(_bn(h, g1, be1, m1, v1))
        h = jnp.einsum('bfeh,ehk->bfek', h, W2) + b2
        h = jax.nn.relu(_bn(h, g2, be2, m2, v2))
        y = jnp.einsum('bfeh,ehd->bfed', h, Wo) + bo
        return jnp.einsum('bfed,fe->bfd', y, w)

    def _L1_gnn_ref(x, edge_index, W, b, mag_w, mag_b, attn_w):
        import jax, jax.numpy as jnp
        import numpy as np
        N_NODES = 1250
        N_EDGES = 40000
        D_IN = 256
        D_OUT = 256
        MAX_NORM = 0.95

        def _expmap0(u):
            un = jnp.linalg.norm(u, axis=-1, keepdims=True)
            un_c = jnp.maximum(un, 1e-15)
            return jnp.tanh(un_c) * u / un_c
        N = x.shape[0]
        F_out = W.shape[0]
        h_raw = x @ W.T + b
        h_dir = h_raw / jnp.maximum(jnp.linalg.norm(h_raw, axis=-1, keepdims=True), 1e-12)
        h_mag = jax.nn.sigmoid(x @ mag_w.T + mag_b) * 1.5
        h = h_dir * h_mag
        src, tgt = (edge_index[0], edge_index[1])
        h_src = h[src]
        h_tgt = h[tgt]
        a_s, a_t = (attn_w[0, :F_out], attn_w[0, F_out:])
        scores = h_src @ a_s + h_tgt @ a_t
        mx = jnp.maximum(jax.ops.segment_max(scores, tgt, num_segments=N), -1000000000.0)
        ex = jnp.exp(scores - mx[tgt])
        se = jax.ops.segment_sum(ex, tgt, num_segments=N)
        attn_weights = ex / (se[tgt] + 1e-10)
        agg = jax.ops.segment_sum(h_src * attn_weights[:, None], tgt, num_segments=N)
        h_combined = h + agg
        h_poincare = _expmap0(h_combined)
        norms = jnp.linalg.norm(h_poincare, axis=1, keepdims=True)
        return jnp.where(norms > MAX_NORM, h_poincare * (MAX_NORM / (norms + 1e-08)), h_poincare)

    def _L1_mix_ref(x, W_qkv, W_out, b_out):
        import jax, jax.numpy as jnp
        import numpy as np
        HEADS = 4
        DIM_HEAD = 32
        B, L, D = x.shape
        scale = DIM_HEAD ** (-0.5)
        qkv = jnp.einsum('bld,df->blf', x, W_qkv)
        qkv = qkv.reshape(B, L, 3, HEADS, DIM_HEAD)
        q = jnp.transpose(qkv[:, :, 0], (0, 2, 1, 3)) * scale
        k = jax.nn.softmax(jnp.transpose(qkv[:, :, 1], (0, 2, 1, 3)), axis=2)
        v = jnp.transpose(qkv[:, :, 2], (0, 2, 1, 3))
        context = jnp.einsum('bhld,bhle->bhde', k, v)
        out = jnp.einsum('bhde,bhld->bhle', context, q)
        out = jnp.transpose(out, (0, 2, 1, 3)).reshape(B, L, HEADS * DIM_HEAD)
        return jnp.einsum('blf,fd->bld', out, W_out) + b_out

    def _L1_ffn_ref(input_embeddings, router_w, w1, b1, w2, b2):
        import jax, jax.numpy as jnp
        import numpy as np
        NUM_EXPERTS = 8
        TOP_K = 2
        B, S, D = (8, 1024, 256)

        def _moe(tokens, router_w, w1, b1, w2, b2):
            N = tokens.shape[0]
            E = router_w.shape[0]
            logits = tokens.astype(jnp.float32) @ router_w.astype(jnp.float32).T
            probs = jax.nn.softmax(logits, axis=-1)
            rw, re = jax.lax.top_k(probs, TOP_K)
            if TOP_K > 1:
                rw = rw / jnp.maximum(rw.sum(-1, keepdims=True), 1e-12)
            rw = rw.astype(tokens.dtype)
            combine = jnp.zeros((N, E), tokens.dtype).at[jnp.arange(N)[:, None], re].set(rw)
            out = tokens
            for e in range(E):
                h = jax.nn.gelu(tokens @ w1[e] + b1[e], approximate=False)
                y = h @ w2[e] + b2[e]
                out = out + combine[:, e:e + 1] * y
            return out
        b, s, d = input_embeddings.shape
        tokens = input_embeddings.reshape(b * s, d)
        return _moe(tokens, router_w, w1, b1, w2, b2).reshape(b, s, d)
    edge_index = jnp.stack([src, dst])
    xn = _layernorm(x, axis=-1)
    x = x + _L0_gnn_ref(xn, src, dst, L0_gnn_W_left, L0_gnn_b_left, L0_gnn_W_right) + _L0_mix_ref(xn[None], L0_mix_w_qkv, L0_mix_w_out, L0_mix_b_out)[0]
    x = x + _L0_ffn_ref(_layernorm(x, axis=-1)[None], L0_ffn_Wr, L0_ffn_br, L0_ffn_W1, L0_ffn_b1, L0_ffn_g1, L0_ffn_be1, L0_ffn_m1, L0_ffn_v1, L0_ffn_W2, L0_ffn_b2, L0_ffn_g2, L0_ffn_be2, L0_ffn_m2, L0_ffn_v2, L0_ffn_Wo, L0_ffn_bo)[0]
    xn = _layernorm(x, axis=-1)
    x = x + _L1_gnn_ref(xn, edge_index, L1_gnn_W, L1_gnn_b, L1_gnn_mag_w, L1_gnn_mag_b, L1_gnn_attn_w) + _L1_mix_ref(xn[None], L1_mix_W_qkv, L1_mix_W_out, L1_mix_b_out)[0]
    x = x + _L1_ffn_ref(_layernorm(x, axis=-1)[None], L1_ffn_router_w, L1_ffn_w1, L1_ffn_b1, L1_ffn_w2, L1_ffn_b2)[0]
    return x

_drawn_inputs = setup_inputs


def setup_inputs(seed=0):
    import zlib

    import numpy as np

    out = dict(_drawn_inputs(seed))
    spreads = {'L0_gnn_b_left': (0.0, 0.1),
     'L0_ffn_br': (0.0, 0.1),
     'L0_ffn_b1': (0.0, 0.335),
     'L0_ffn_g1': (1.0, 0.2),
     'L0_ffn_be1': (0.0, 0.336),
     'L0_ffn_m1': (0.0, 0.33),
     'L0_ffn_v1': (1.0, 0.6),
     'L0_ffn_b2': (0.0, 0.1),
     'L0_ffn_g2': (1.0, 0.2),
     'L0_ffn_be2': (0.0, 0.1),
     'L0_ffn_m2': (0.0, 0.1),
     'L0_ffn_v2': (1.0, 0.586),
     'L0_ffn_bo': (0.0, 0.1),
     'L1_mix_b_out': (0.0, 0.1),
     'L1_ffn_b1': (0.0, 0.42),
     'L1_ffn_b2': (0.0, 0.293)}
    factors = {'L0_mix_b_out': 4.96, 'L1_gnn_b': 38.165, 'L1_gnn_mag_w': 22.924, 'L1_gnn_attn_w': 160.311}
    for name, (base, spread) in spreads.items():
        noise = np.random.default_rng([zlib.crc32(name.encode()), seed]).standard_normal(out[name].shape)
        drawn = base * np.exp(spread * noise) if base else spread * noise
        out[name] = jnp.asarray(drawn.astype(out[name].dtype))
    for name, factor in factors.items():
        out[name] = (out[name] * factor).astype(out[name].dtype)
    return out
```

```python
from contextlib import ExitStack

import concourse.bass as bass
from concourse import mybir

F32 = mybir.dt.float32
F16 = mybir.dt.float16
I32 = mybir.dt.int32
ALU = mybir.AluOpType
ACT = mybir.ActivationFunctionType
AX = mybir.AxisListType.X

P = 128
N = 6250
E = 106250
D = 256
KD = D // P
T = 125
NT = N // T
PAIRS = NT // 2
TP = 2 * T
CH = 18
WIN = CH * P
SWEEP_CH = 17
SWEEP = SWEEP_CH * T
SWEEPS = E // SWEEP
SAMPLE = 10
EX = 8
HEADS0 = 8
HD0 = 64
KV0 = 2 * HEADS0 * HD0
HEADS1 = 4
HD1 = 32
HID1 = HEADS1 * HD1
ROW1 = D + 2
LN_EPS = 1e-5
BN_EPS = 1e-3
MAX_NORM = 0.95
FAR = 9.0


def col(ap, n):
    return ap.unsqueeze(2).to_broadcast([ap.shape[0], ap.shape[1], n])


def mid(ap, n):
    return ap.unsqueeze(1).to_broadcast([ap.shape[0], n, ap.shape[1]])


ROOT_STEPS = 11


def inverse_root(dve, step, y, x, t):
    step(dve.tensor_scalar(t.bitcast(I32), x.bitcast(I32), 1, None, ALU.logical_shift_right))
    step(dve.tensor_scalar(y.bitcast(I32), t.bitcast(I32), -1.0, float(0x5F3759DF), ALU.mult, ALU.add))
    for _ in range(3):
        step(dve.tensor_tensor(t, y, y, ALU.mult))
        step(dve.scalar_tensor_tensor(t, t, -0.5, x, ALU.mult, ALU.mult))
        step(dve.scalar_tensor_tensor(y, t, 1.5, y, ALU.add, ALU.mult))


def gps_kernel(nc, a, out):
    ctx = ExitStack()
    with ctx:
        def sb(name, shape, dt=F32):
            return ctx.enter_context(nc.sbuf_tensor(name, shape, dt))

        def sem(name):
            return ctx.enter_context(nc.semaphore(name))

        ctx.enter_context(nc.allow_non_contiguous_dma(reason="columns of small vectors"))

        xtab = nc.dram_tensor("xtab", (N, 2 * D), F16).ap()
        xnT_d = nc.dram_tensor("xnT_d", (P, KD, N), F32).ap()
        xn2T_d = nc.dram_tensor("xn2T_d", (P, KD, N), F32).ap()
        x2_d = nc.dram_tensor("x2_d", (N, D), F32).ap()
        htab = nc.dram_tensor("htab", (N, ROW1), F32).ap()
        hbase_d = nc.dram_tensor("hbase_d", (N, D), F32).ap()
        nslow_d = nc.dram_tensor("nslow_d", (N, D), F32).ap()

        def pair_rows(t, i):
            return t[bass.ds(i * TP, TP), :].rearrange("(u p) d -> p u d", u=2)

        W1 = sb("W1", [P, EX, KD, D])
        W2 = sb("W2", [P, EX, KD, D])
        Wo = sb("Wo", [P, EX, KD, D])
        kT_all = sb("kT_all", [P, N])
        v_all = sb("v_all", [T, NT, HID1])
        ring = sb("ring", [P, 2, CH, ROW1])
        ring16 = ring[:, :, :, :].rearrange("p u c d -> p (u c d)").bitcast(F16)\
            .rearrange("p (u c d) -> p u c d", u=2, c=CH)
        hot = sb("hot", [P, 2, CH, T], F16)
        big = kT_all[:, 0:2 * CH * T].rearrange("p (u c d) -> p u c d", u=2, c=CH)
        srcw = sb("srcw", [P, NT * CH], I32)
        relw = sb("relw", [P, NT * CH])
        idx = sb("idx", [P, 2, CH], I32)
        ident = sb("ident", [P, P])
        ones = sb("ones", [P, P])
        ones16 = sb("ones16", [P, 1], F16)
        zeros = sb("zeros", [P, 512])
        iota = sb("iota", [P, T])
        thr = sb("thr", [P, NT])
        thr1 = sb("thr1", [P, NT])
        cols = sb("cols", [P, 448])
        bn = sb("bn", [P, 2, 2, 2 * EX])
        wg = sb("wg", [P, KD, D])
        wg3 = sb("wg3", [P, KD, 3])
        c3 = sb("c3", [T, 3])
        hbound = sb("hbound", [P, 1])
        nbound = sb("nbound", [P, 1])
        Wr = sb("Wr", [P, KD, EX])
        br = sb("br", [T, EX])
        bo = sb("bo", [EX, D])
        b2 = sb("b2", [EX, D])
        bias0 = sb("bias0", [T, D])
        gb = sb("gb", [T, D])
        bias1 = sb("bias1", [T, D])
        bl = sb("bl", [T, D])
        WL = sb("WL", [P, 2 * KD, D])
        M1 = sb("M1", [P, KD, D])
        wqkv1 = sb("wqkv1", [P, KD, 3 * HID1])
        wout1 = sb("wout1", [HID1, D])
        flag = sb("flag", [1, 1], I32)
        ht_all = sb("ht_all", [T, NT])
        iota8 = sb("iota8", [T, EX])
        fl = sb("fl", [P, 4])
        nothing = sb("nothing", [1, 16])
        xin = sb("xin", [T, 2, D])
        xT = sb("xT", [P, KD, TP])
        base = sb("base", [T, 2, D])
        st = sb("st", [T, 2, 6])
        mv = sb("mv", [T, 2, 2])
        rs = sb("rs", [T, 2])
        nb = sb("nb", [T, 2])
        xn = sb("xn", [T, 2, D])
        acc = sb("acc", [T, 2, D])
        uT = sb("uT", [P, KD, TP])
        h1 = sb("h1", [P, KD, TP])
        h2 = sb("h2", [P, KD, TP])
        tmp = sb("tmp", [T, 2, D])
        hn = sb("hn", [T, 2, D])
        hnT = sb("hnT", [P, KD, TP])
        sm = sb("sm", [T, 24, 2])
        lg = sb("lg", [T, 8, 2, EX])
        wT = sb("wT", [EX, TP])
        hrow = sb("hrow", [T, 2, ROW1])
        ps = [ctx.enter_context(nc.psum_tensor(f"ps{i}", [P, 512], F32)) for i in range(8)]

        f1 = W1[:, :, :, :].rearrange("p e k d -> p (e k d)")
        f2 = W2[:, :, :, :].rearrange("p e k d -> p (e k d)")
        wqkv0 = f1[:, 0:12 * D].rearrange("p (r d) -> p r d", r=12)
        wout0 = f2[:, 0:2 * 512].rearrange("p (r d) -> p r d", r=2)
        woutT = f2[:, 1024:1024 + 4 * D].rearrange("p (r d) -> p r d", r=4)
        wkvT = f2[:, 2048:2048 + 2 * KV0].rearrange("p (k d) -> p k d", k=KD)
        gnnW = f1[:, 3072:3072 + 2 * D].rearrange("p (r d) -> p r d", r=2)

        setup_loads = []
        uses = []
        load_setup = sem("load_setup")
        load_edges = sem("load_edges")
        load_experts0 = sem("load_experts0")
        load_experts1 = sem("load_experts1")

        rows = kT_all[0:80, 0:2 * P].rearrange("p (l d) -> p l d", l=2)
        rows_b1 = kT_all[0:16, 256:256 + P]
        rwrow = kT_all[0:EX, 384:384 + D]
        acol = kT_all[:, 640:644].rearrange("p (s t) -> p s t", s=2)
        bcol = kT_all[:, 644:646]
        asq = kT_all[:, 646:648]
        asum = kT_all[:, 648:649]
        bfull = kT_all[:, 656:656 + 2 * T].rearrange("p (t n) -> p t n", t=2)
        magb = kT_all[0:T, 910:911]
        wright = kT_all[:, 1024:1024 + 2 * D].rearrange("p (k d) -> p k d", k=KD)
        wmean = kT_all[:, 1600:1632]
        bnt = kT_all[:, 1664:1664 + 64].rearrange("p (l v n) -> p l v n", l=2, v=2)
        dst_all = v_all[:, :, :].rearrange("p t d -> p (t d)")[:, 0:850].bitcast(I32)
        dstf = v_all[:, :, :].rearrange("p t d -> p (t d)")[:, 900:985]
        cnt = v_all[:, :, :].rearrange("p t d -> p (t d)")[:, 1000:1050]
        startf = v_all[:, :, :].rearrange("p t d -> p (t d)")[0:1, 1100:1150]
        starti = v_all[:, :, :].rearrange("p t d -> p (t d)")[0:1, 1200:1250].bitcast(I32)
        dstw = ring[:, 0, :, :].rearrange("p c d -> p (c d)")[:, 0:NT * CH].bitcast(I32)
        ge = ring[:, 0, :, :].rearrange("p c d -> p (c d)")[:, 1000:1000 + NT * CH]
        lt = ring[:, 0, :, :].rearrange("p c d -> p (c d)")[:, 2000:2000 + NT * CH]
        cmp = ring[0:T, :, :, :].rearrange("p u c d -> p (u c d)")[:, 0:NT * 85]\
            .rearrange("p (t s) -> p t s", t=NT)

        turns = []
        for k in range(KD):
            for g in range(2):
                turns.append((wkvT[:, k, 512 * g:512 * g + 512],
                              [(wqkv0[:, 4 + 4 * g + r, k * P:k * P + P], P) for r in range(4)]))
        for g in range(2):
            turns.append((woutT[:, 2 * g:2 * g + 2, :].rearrange("p r d -> p (r d)"),
                          [(wout0[:, o, (2 * g + q) * P:(2 * g + q) * P + P], P) for q in range(2) for o in range(2)]))
        turns.append((wg[:, :, :].rearrange("p k d -> p (k d)"),
                      [(gnnW[:, o, k * P:k * P + P], P) for k in range(KD) for o in range(2)]))
        turns.append((cols[:, :],
                      [(wqkv1[:, 0, 0:P], P), (wqkv1[:, 1, 0:P], P)]
                      + [(rwrow[:, k * P:k * P + P], EX) for k in range(KD)]
                      + [(rows[:, l, :], 80) for l in range(2)] + [(rows_b1, 16)]))
        wq1T = cols[:, 0:2 * P].rearrange("p (k i) -> p k i", k=KD)
        rwT = cols[:, 256:272].rearrange("p (k e) -> p k e", k=KD)
        bnc = cols[:, 272:432].rearrange("p (l v n) -> p l v n", l=2, v=5)
        b1c = cols[:, 432:448]

        def wait_apart(engine, semaphore, value):
            engine.wait_ge(semaphore, value)
            at = len(uses)
            uses.append(at)
            target = nothing[0:1, 2 + at:3 + at]
            if engine.engine == nc.gpsimd.engine:
                engine.tensor_tensor(target, nothing[0:1, 0:1], nothing[0:1, 1:2], ALU.add)
            else:
                engine.memset(target, 0.0)

        made = sem("made")
        zeroed = sem("zeroed")
        turned = sem("turned")
        turned_copied = sem("turned_copied")
        s_dve = sem("setup_dve")
        s_count = sem("setup_counted")
        s_start = sem("setup_starts")
        s_a = sem("setup_through_w")
        s_norm = sem("setup_before_summed")
        s_match = sem("setup_matches")
        windows = sem("windows_loaded")
        nslow_zero = sem("nslow_zero")

        with nc.Block() as block:
            @block.sync
            def _(sp):
                sp.dma_start(dst_all, a["dst"].rearrange("(p n) -> p n", p=T)).then_inc(load_edges, 16)

                def put(dst, src):
                    sp.dma_start(dst, src).then_inc(load_setup, 16)
                    put.n += 1
                put.n = 0
                put(wqkv0, a["L0_mix_w_qkv"].rearrange("(r p) d -> p r d", p=P))
                put(wout0, a["L0_mix_w_out"].rearrange("(r p) d -> p r d", p=P))
                put(gnnW, a["L1_gnn_W"].rearrange("(r p) d -> p r d", p=P))
                put(wqkv1[:, :, :], a["L1_mix_W_qkv"].rearrange("(k p) d -> p k d", p=P))
                put(rwrow, a["L1_ffn_router_w"])
                for l, names in enumerate((("g1", "b1", "be1", "m1", "v1"), ("g2", "b2", "be2", "m2", "v2"))):
                    for v, name in enumerate(names):
                        put(rows[16 * v:16 * v + 16, l, :], a["L0_ffn_" + name].rearrange("e (k p) -> (e k) p", p=P))
                put(rows_b1, a["L1_ffn_b1"].rearrange("e (k p) -> (e k) p", p=P))
                put(acol, a["L1_gnn_attn_w"].rearrange("o (s t p) -> p (o s) t", s=2, p=P))
                put(bcol, a["L1_gnn_b"].rearrange("(t p) -> p t", p=P))
                put(magb, a["L1_gnn_mag_b"].rearrange("(o n) -> o n", o=1).to_broadcast([T, 1]))
                put(wg3[:, :, 0:1], a["L1_gnn_mag_w"].rearrange("o (k p) -> p k o", p=P))
                put(WL[:, :, :], a["L0_gnn_W_left"].rearrange("(k p) d -> p k d", p=P))
                put(wright, a["L0_gnn_W_right"].rearrange("(k p) d -> p k d", p=P))
                put(Wr[:, :, :], a["L0_ffn_Wr"].rearrange("(k p) e -> p k e", p=P))
                put(wout1[:, :], a["L1_mix_W_out"])
                put(bo[:, :], a["L0_ffn_bo"])
                put(b2[:, :], a["L1_ffn_b2"])

                def row(t, name, n):
                    put(t[:, :], a[name].rearrange("(o n) -> o n", o=1).to_broadcast([T, n]))
                row(br, "L0_ffn_br", EX)
                row(bl, "L0_gnn_b_left", D)
                row(bias0, "L0_mix_b_out", D)
                row(gb, "L1_gnn_b", D)
                row(bias1, "L1_mix_b_out", D)
                setup_loads.append(put.n)
                sp.dma_start(Wo[:, :, :, :], a["L0_ffn_Wo"].rearrange("e (k p) d -> p e k d", p=P)).then_inc(load_experts0, 16)
                sp.wait_ge(zeroed, 1)
                for k in range(PAIRS):
                    sp.dma_start(nslow_d[k * TP:k * TP + TP, :].rearrange("(u p) d -> p u d", u=2), zeros[0:T, :].rearrange("p (u d) -> p u d", u=2))\
                        .then_inc(nslow_zero, 16)
                sp.wait_ge(s_start, 1)
                with sp.Fori(0, NT) as t:
                    start = sp.value_load(starti[0:1, bass.ds(t, 1)], min_val=0, max_val=E - WIN)
                    sp.dma_start(srcw[:, bass.ds(t * CH, CH)],
                                 a["src"][bass.ds(start, WIN)].rearrange("(p c) -> p c", p=P)).then_inc(windows, 16)
                    sp.dma_start(dstw[:, bass.ds(t * CH, CH)],
                                 a["dst"][bass.ds(start, WIN)].rearrange("(p c) -> p c", p=P)).then_inc(windows, 16)
                sp.wait_ge(nslow_zero, 16 * PAIRS)

            @block.gpsimd
            def _(pool):
                pool.memset(ident[:, :], 0.0).then_inc(made, 1)
                pool.memset(ones[:, :], 1.0).then_inc(made, 1)
                pool.memset(nothing[:, 0:2], 0.0).then_inc(made, 1)
                pool.memset(ones16[:, :], 1.0).then_inc(made, 1)
                pool.memset(hrow[:, :, D:D + 1], 1.0).then_inc(made, 1)
                pool.iota(idx[:, 0, 0:1], pattern=[[0, 1]], base=0, channel_multiplier=0).then_inc(made, 1)
                pool.iota(kT_all[:, 2000:2000 + T].bitcast(I32), pattern=[[1, T]], base=0, channel_multiplier=0).then_inc(made, 1)
                pool.iota(kT_all[:, 2200:2200 + NT].bitcast(I32), pattern=[[T, NT]], base=0, channel_multiplier=0).then_inc(made, 1)
                pool.wait_ge(made, 8)
                pool.affine_select(out=ident[:, :], in_=ident[:, :], compare_op=ALU.not_equal, fill=1.0,
                                   base=0, pattern=[[-1, P]], channel_multiplier=1).then_inc(made, 1)

            @block.vector
            def _(dve):
                n = [0]

                def step(ins):
                    n[0] += 1
                    ins.then_inc(s_dve, 1)
                    dve.wait_ge(s_dve, n[0])

                dve.memset(zeros[:, :], 0.0).then_inc(zeroed, 1)
                dve.wait_ge(made, 9)
                step(dve.tensor_copy(iota[:, :], kT_all[:, 2000:2000 + T].bitcast(I32)))
                step(dve.tensor_copy(thr[:, :], kT_all[:, 2200:2200 + NT].bitcast(I32)))
                step(dve.tensor_copy(iota8[:, :], iota[0:T, 0:EX]))
                dve.wait_ge(load_edges, 16)
                step(dve.tensor_copy(dstf, dst_all.rearrange("p (n s) -> p n s", s=SAMPLE)[:, :, 0]))
                step(dve.tensor_tensor(cmp, mid(dstf, NT), col(thr[0:T, :], 85), ALU.is_lt))
                dve.tensor_reduce(cnt, cmp, AX, ALU.add).then_inc(s_count, 1)
                dve.wait_ge(s_norm, 1)
                step(dve.tensor_scalar(startf, ps[4][0:1, 0:NT], float(SAMPLE), -float(SAMPLE), ALU.mult, ALU.add))
                step(dve.tensor_scalar(startf, startf, 0.0, float(E - WIN), ALU.max, ALU.min))
                dve.tensor_copy(starti, startf).then_inc(s_start, 1)

                dve.wait_ge(load_setup, 16 * setup_loads[0])
                for g, (target, sources) in enumerate(turns):
                    dve.wait_ge(turned, g + 1)
                    if len(sources) == 4:
                        dve.tensor_copy(target, ps[g % 4][:, :]).then_inc(turned_copied, 1)
                    else:
                        dve.tensor_copy(target, ps[g % 4][:, 0:448]).then_inc(turned_copied, 1)
                dve.wait_ge(turned_copied, len(turns))
                heads = wkvT.rearrange("p k (h d) -> p (k h) d", d=HD0)
                step(dve.tensor_reduce(wmean, heads, AX, ALU.add))
                step(dve.tensor_scalar(wmean, wmean, 1.0 / HD0, None, ALU.mult))
                step(dve.tensor_tensor(heads, heads, col(wmean, HD0), ALU.subtract))
                for l in range(2):
                    g_, b_, be_, m_, v_ = (bnc[:, l, v, :] for v in range(5))
                    step(dve.tensor_scalar(v_, v_, BN_EPS, None, ALU.add))
                    inverse_root(dve, step, bnt[:, l, 0, :], v_, bnt[:, l, 1, :])
                    step(dve.tensor_tensor(bn[:, l, 0, :], bnt[:, l, 0, :], g_, ALU.mult))
                    step(dve.tensor_tensor(bnt[:, l, 1, :], b_, m_, ALU.subtract))
                    step(dve.tensor_tensor(bnt[:, l, 1, :], bnt[:, l, 1, :], bn[:, l, 0, :], ALU.mult))
                    step(dve.tensor_tensor(bn[:, l, 1, :], bnt[:, l, 1, :], be_, ALU.add))
                step(dve.tensor_tensor(bias0[:, :], bias0[:, :], bl[:, :], ALU.add))
                step(dve.tensor_tensor(WL[:, 0:KD, :], WL[:, 0:KD, :], wright, ALU.add))
                step(dve.tensor_tensor(asq, acol[:, 0, :], acol[:, 0, :], ALU.mult))
                step(dve.tensor_reduce(asum, asq, AX, ALU.add))
                dve.tensor_copy(bfull, col(bcol, T)).then_inc(s_count, 1)
                dve.wait_ge(s_a, 1)
                step(dve.tensor_copy(wg3[:, :, 1:3], ps[5][:, 0:4].rearrange("p (k s) -> p k s", k=KD)))
                step(dve.tensor_copy(c3[:, 1:3], ps[5][0:T, 8:10]))
                step(dve.tensor_copy(c3[:, 0:1], magb))
                step(dve.tensor_copy(asum, ps[5][:, 16:17]))
                inverse_root(dve, step, hbound[:, :], asum, asq[:, 0:1])
                step(dve.tensor_tensor(hbound[:, :], hbound[:, :], asum, ALU.mult))
                step(dve.tensor_scalar(hbound[:, :], hbound[:, :], 1.51, 1.0, ALU.mult, ALU.add))
                step(dve.tensor_scalar(nbound[:, :], hbound[:, :], -1.0, None, ALU.mult))
                dve.wait_ge(windows, 32 * NT)
                step(dve.tensor_copy(relw[:, :], dstw))
                rel3 = relw[:, :].rearrange("p (t c) -> p t c", t=NT)
                step(dve.tensor_tensor(rel3, rel3, col(thr[:, :], CH), ALU.subtract))
                step(dve.tensor_scalar(ge, relw[:, :], 0.0, None, ALU.is_ge))
                step(dve.tensor_scalar(lt, relw[:, :], float(T), None, ALU.is_lt))
                step(dve.tensor_tensor(ge, ge, lt, ALU.mult))
                dve.tensor_reduce(fl[:, 0:1], ge, AX, ALU.add).then_inc(s_count, 1)
                dve.wait_ge(s_match, 1)
                step(dve.tensor_scalar(fl[:, 1:2], ps[6][:, 0:1], float(E), None, ALU.not_equal))
                step(dve.tensor_scalar(fl[:, 2:3], fl[:, 1:2], -1.0, 1.0, ALU.mult, ALU.add))
                step(dve.tensor_scalar(relw[:, :], relw[:, :], fl[:, 2:3], fl[:, 1:2], ALU.mult, ALU.subtract))
                step(dve.tensor_copy(flag[:, :], fl[0:1, 1:2]))

            @block.tensor
            def _(pe):
                pe.wait_ge(made, 9)
                pe.wait_ge(s_count, 1)
                pe.matmul(ps[4][0:1, 0:NT], ones[0:T, 0:1], cnt, start=True, stop=True).then_inc(s_norm, 1)
                pe.wait_ge(load_setup, 16 * setup_loads[0])
                for g, (target, sources) in enumerate(turns):
                    if g >= 4:
                        pe.wait_ge(turned_copied, g - 3)
                    at = 0
                    for src, r in sources:
                        last = pe.transpose(ps[g % 4][:, at:at + r], src, ident[0:r, 0:r])
                        at += r
                    last.then_inc(turned, 1)
                pe.wait_ge(s_count, 2)
                for k in range(KD):
                    for o in range(2):
                        pe.matmul(ps[5][:, 2 * k:2 * k + 2], gnnW[:, o, k * P:k * P + P], acol[:, :, o],
                                  start=(o == 0), stop=(o == 1))
                for o in range(2):
                    pe.matmul(ps[5][0:T, 8:10], bfull[:, o, :], acol[:, :, o], start=(o == 0), stop=(o == 1))
                pe.matmul(ps[5][:, 16:17], ones[:, :], asum, start=True, stop=True).then_inc(s_a, 1)
                pe.wait_ge(s_count, 3)
                pe.matmul(ps[6][:, 0:1], ones[:, :], fl[:, 0:1], start=True, stop=True).then_inc(s_match, 1)

        sq = big[0:T, :, :, :].rearrange("p u c d -> p u (c d)")[:, :, 0:KV0]
        kc = ring[0:T, 0, :, :].rearrange("p c d -> p (c d)")[:, 0:1024].rearrange("p (u d) -> p u d", u=2)
        vc = ring[0:T, 0, :, :].rearrange("p c d -> p (c d)")[:, 1024:2048].rearrange("p (u d) -> p u d", u=2)
        x16 = ring[0:T, 1, :, :].rearrange("p c d -> p (c d)")[:, 0:512].bitcast(F16)\
            .rearrange("p (u d) -> p u d", u=2)
        rk = ring[0:T, 1, :, :].rearrange("p c d -> p (c d)")[:, 600:640].rearrange("p (u d) -> p u d", u=2)
        rk8, rk8y, rk8t = (ring[0:T, 1, :, :].rearrange("p c d -> p (c d)")[:, n:n + 16]
                           .rearrange("p (u d) -> p u d", u=2) for n in (700, 716, 732))
        xTp = [xT[:, :, 0:T], xT[:, :, T:TP]]

        a_load = [sem("a_x_loaded_0"), sem("a_x_loaded_1")]
        a_norm = sem("a_stats_mean")
        a_root = sem("a_root_steps")
        a_nb = sem("a_shift")
        a_xn = sem("a_xn")
        a_hi = sem("a_hi")
        a_lo = sem("a_lo")
        a_tab = sem("a_table_stored")
        a_tr = sem("a_turned")
        a_xT = sem("a_xT")
        a_xTs = sem("a_xT_stored")
        a_kv = sem("a_kv")
        a_k = sem("a_k_copied")
        a_sq = sem("a_squares")
        a_ms = sem("a_mean_squares")
        a_r = sem("a_kv_var_product")
        a_v = sem("a_v_scaled")
        a_dots = sem("a_dots")

        with nc.Block() as block:
            @block.sync
            def _(sp):
                with sp.Fori(0, PAIRS) as i:
                    for u in range(2):
                        t = i * 2 + u
                        sp.wait_ge(made, 1)
                        sp.wait_ge(a_xn, t - u)
                        sp.dma_start(xin[:, u, :], a["x"][bass.ds(t * T, T), :]).then_inc(a_load[u], 16)
                    for u in range(2):
                        t = i * 2 + u
                        sp.wait_ge(made, 1)
                        sp.wait_ge(a_lo, t + 1)
                        sp.wait_ge(a_hi, t + 1)
                        sp.dma_start(xtab[bass.ds(t * T, T), :], x16[:, u, :]).then_inc(a_tab, 16)
                        sp.wait_ge(made, 1)
                        sp.wait_ge(a_xT, t + 1)
                        sp.dma_start(xnT_d[:, :, bass.ds(t * T, T)], xTp[u]).then_inc(a_xTs, 16)
                sp.wait_ge(a_tab, 16 * NT)
                sp.wait_ge(a_xTs, 16 * NT)

            @block.scalar
            def _(act):
                with act.Fori(0, PAIRS) as i:
                    for u in range(2):
                        t = i * 2 + u
                        act.wait_ge(a_nb, i + 1)
                        act.wait_ge(a_lo, t - u)
                        act.wait_ge(a_tr, t - u)
                        act.activation(xn[:, u, :], xin[:, u, :], ACT.Identity, bias=nb[:, u:u + 1],
                                       scale=rs[:, u:u + 1]).then_inc(a_xn, 1)
                        act.wait_ge(a_tab, 16 * (t - u))
                        act.wait_ge(a_xn, t + 1)
                        act.copy(x16[:, u, 0:D], xn[:, u, :]).then_inc(a_hi, 1)
                    for u in range(2):
                        t = i * 2 + u
                        act.wait_ge(a_kv, t + 1)
                        act.wait_ge(a_ms, t - u)
                        act.activation(sq[:, u, 0:512], ps[2 * u][0:T, :], ACT.Square).then_inc(a_sq, 1)
                        act.activation(sq[:, u, 512:1024], ps[2 * u + 1][0:T, :], ACT.Square).then_inc(a_sq, 1)
                        act.wait_ge(a_dots, t - u)
                        act.copy(kc[:, u, :], ps[2 * u][0:T, :]).then_inc(a_k, 1)

            @block.gpsimd
            def _(pool):
                with pool.Fori(0, PAIRS) as i:
                    for u in range(2):
                        t = i * 2 + u
                        pool.wait_ge(a_hi, t + 1)
                        pool.tensor_tensor(x16[:, u, D:2 * D], xn[:, u, :], x16[:, u, 0:D], ALU.subtract)\
                            .then_inc(a_lo, 1)

            @block.vector
            def _(dve):
                with dve.Fori(0, PAIRS) as i:
                    done = [0]

                    def step(ins):
                        done[0] += 1
                        ins.then_inc(a_root, 1)
                        dve.wait_ge(a_root, (2 * ROOT_STEPS + 1) * i + done[0])

                    for u in range(2):
                        dve.wait_ge(a_load[u], 16 * (i + 1))
                        dve.bn_stats(st[:, u, :], xin[:, u, :]).then_inc(a_norm, 1)
                    wait_apart(dve, a_norm, 4 * i + 2)
                    for u in range(2):
                        dve.bn_aggr(mv[:, u, :], st[:, u, :]).then_inc(a_norm, 1)
                    dve.wait_ge(a_norm, 4 * i + 4)
                    dve.wait_ge(a_xn, 2 * i)
                    step(dve.tensor_scalar(sm[:, 14, :], mv[:, :, 1], LN_EPS, None, ALU.add))
                    inverse_root(dve, step, rs[:, :], sm[:, 14, :], sm[:, 15, :])
                    dve.scalar_tensor_tensor(nb[:, :], mv[:, :, 0], -1.0, rs[:, :], ALU.mult, ALU.mult)\
                        .then_inc(a_nb, 1)
                    for u in range(2):
                        t = i * 2 + u
                        dve.wait_ge(a_tr, t + 1)
                        dve.wait_ge(a_xTs, 16 * (t - u))
                        dve.wait_ge(a_kv, t - u)
                        dve.tensor_copy(xTp[u], ps[4 + u][:, 0:2 * T].rearrange("p (k n) -> p k n", k=KD))\
                            .then_inc(a_xT, 1)
                    for u in range(2):
                        dve.wait_ge(a_sq, 4 * i + 2 * u + 2)
                        dve.tensor_reduce(rk[:, u, 0:16], sq[:, u, :].rearrange("p (h d) -> p h d", d=HD0),
                                          AX, ALU.add).then_inc(a_ms, 1)
                    dve.wait_ge(a_ms, 2 * i + 2)
                    dve.tensor_scalar(rk[:, :, 0:16], rk[:, :, 0:16], 1.0 / HD0, LN_EPS, ALU.mult, ALU.add)\
                        .then_inc(a_r, 1)
                    dve.wait_ge(a_r, 2 * i + 1)
                    dve.tensor_tensor(rk8, rk[:, :, 0:8], rk[:, :, 8:16], ALU.mult).then_inc(a_r, 1)
                    dve.wait_ge(a_r, 2 * i + 2)
                    inverse_root(dve, step, rk8y, rk8, rk8t)
                    dve.wait_ge(a_dots, 2 * i)
                    for u in range(2):
                        dve.tensor_tensor(vc[:, u, :].rearrange("p (h d) -> p h d", d=HD0),
                                          ps[2 * u + 1][0:T, :].rearrange("p (h d) -> p h d", d=HD0),
                                          col(rk8y[:, u, :], HD0), ALU.mult).then_inc(a_v, 1)

            @block.tensor
            def _(pe):
                pe.matmul(ps[6][:, :], zeros[:, 0:P], zeros[:, :], start=True, stop=False,
                          skip_group_check=True)
                with pe.Fori(0, PAIRS) as i:
                    for u in range(2):
                        t = i * 2 + u
                        pe.wait_ge(a_xn, t + 1)
                        pe.wait_ge(a_xT, t - u)
                        for k in range(KD):
                            last = pe.transpose(ps[4 + u][:, k * T:k * T + T], xn[:, u, k * P:k * P + P],
                                                ident[0:T, 0:T])
                        last.then_inc(a_tr, 1)
                    for u in range(2):
                        t = i * 2 + u
                        pe.wait_ge(a_xT, t + 1)
                        pe.wait_ge(a_k, t - u)
                        pe.wait_ge(a_v, t - u)
                        for half in range(2):
                            for k in range(KD):
                                last = pe.matmul(ps[2 * u + half][0:T, :], xTp[u][:, k, :],
                                                 wkvT[:, k, 512 * half:512 * half + 512],
                                                 start=(k == 0), stop=(k == KD - 1))
                        last.then_inc(a_kv, 1)
                    for u in range(2):
                        t = i * 2 + u
                        pe.wait_ge(a_k, t + 1)
                        pe.wait_ge(a_v, t + 1)
                        for q in range(4):
                            last = pe.matmul(ps[6][:, q * P:q * P + P], vc[:, u, q * P:q * P + P],
                                             kc[:, u, q * P:q * P + P], start=False, stop=False,
                                             skip_group_check=True)
                        last.then_inc(a_dots, 1)

        dsb = ring[:, 0, :, :].rearrange("p c d -> p (c d)")[:, 0:512].rearrange("p (q d) -> p q d", q=4)
        gsb = ring[:, 0, :, :].rearrange("p c d -> p (c d)")[:, 512:1536].rearrange("p (q d) -> p q d", q=4)
        f_copied = sem("f_copied")
        f_product = sem("f_product")
        with nc.Block() as block:
            @block.vector
            def _(dve):
                dve.memset(dsb, 0.0).then_inc(f_copied, 1)
                dve.wait_ge(f_copied, 1)
                for h in range(2):
                    r = slice(HD0 * h, HD0 * h + HD0)
                    dve.tensor_scalar(dsb[r, :, r], ps[6][r, :].rearrange("p (q d) -> p q d", q=4)[:, :, r],
                                      1.0 / N, None, ALU.mult).then_inc(f_copied, 1)
                dve.wait_ge(f_product, 1)
                for g in range(2):
                    dve.tensor_copy(gsb[:, 2 * g:2 * g + 2, :].rearrange("p q d -> p (q d)"), ps[g][:, :])\
                        .then_inc(f_copied, 1)
                dve.wait_ge(f_product, 2)
                dve.tensor_tensor(WL[:, 0:KD, :], WL[:, 0:KD, :], ps[2][:, :].rearrange("p (k d) -> p k d", k=KD),
                                  ALU.add).then_inc(f_copied, 1)

            @block.tensor
            def _(pe):
                pe.wait_ge(f_copied, 3)
                for q in range(4):
                    last = pe.matmul(ps[q // 2][:, (q % 2) * D:(q % 2) * D + D], dsb[:, q, :], woutT[:, q, :],
                                     start=True, stop=True)
                last.then_inc(f_product, 1)
                pe.wait_ge(f_copied, 5)
                for k in range(KD):
                    for q in range(4):
                        last = pe.matmul(ps[2][:, k * D:k * D + D], wqkv0[:, q, k * P:k * P + P], gsb[:, q, :],
                                         start=(q == 0), stop=(q == 3))
                last.then_inc(f_product, 1)

            @block.sync
            def _(sp):
                sp.wait_ge(f_product, 2)
                for w, name in ((W1, "L0_ffn_W1"), (W2, "L0_ffn_W2")):
                    sp.dma_start(w[:, :, :, :], a[name].rearrange("e (k p) d -> p e k d", p=P))\
                        .then_inc(load_experts0, 16)

        b_x = sem("b_x_loaded")
        b_xT = sem("b_xT_loaded")
        b_base = sem("b_sweep_mean_loaded")
        b_idx = sem("b_idx")
        b_rows = [sem("b_rows_gathered_0"), sem("b_rows_gathered_1")]
        b_hot = sem("b_one_hot")
        b_xb = sem("b_x_bias")
        b_seg = sem("b_segment_sums")
        b_cnt = sem("b_count_reciprocal_steps")
        b_router = sem("b_router_steps")
        b_mag = sem("b_magnitude_steps")
        b_s1 = sem("b_low_mean")
        b_hn = sem("b_neighbour_mean")
        b_hnTp = sem("b_mean_turned")
        b_hnT = sem("b_mean_turned_copied")
        b_lin = sem("b_linear")
        b_x1 = sem("b_x1")
        b_root = sem("b_root_steps")
        b_norm = sem("b_stats_mean_rstd")
        b_nb = sem("b_shift")
        b_u = sem("b_normalized")
        b_uTp = sem("b_turned")
        b_uT = sem("b_uT")
        b_lg = sem("b_logits")
        b_zs = sem("b_logits_less_max")
        b_e = sem("b_router_exp")
        b_w = sem("b_router_weights")
        b_wTp = sem("b_weights_turned")
        b_wT = sem("b_weights_turned_copied")
        b_bo = sem("b_expert_biases")
        b_A = sem("b_hidden1_product")
        b_h1 = sem("b_hidden1")
        b_B = sem("b_hidden2_product")
        b_h2 = sem("b_hidden2")
        b_Y = sem("b_expert_out")
        b_acc = sem("b_expert_added")
        b_x2s = sem("b_x2_stored")
        b_x2T = sem("b_x2T")
        b_x2Ts = sem("b_x2T_stored")
        b_hr = sem("b_h_raw")
        b_kv = sem("b_k_v")
        b_hb = sem("b_h_bias")
        b_ss = sem("b_h_squares")
        b_ext = sem("b_magnitude_and_scores")
        b_me = sem("b_magnitude_exp")
        b_h = sem("b_h")
        b_hs = sem("b_h_stored")
        b_kc = sem("b_k_v_copied")
        x2T = sb("x2T", [P, KD, TP])
        ext = sb("ext", [T, 2, 3])

        def bank2(n):
            return ps[n][0:T, :].rearrange("p (u d) -> p u d", u=2)

        def turned_pair(n):
            return ps[n][:, 0:KD * TP].rearrange("p (k n) -> p k n", k=KD)

        with nc.Block() as block:
            @block.sync
            def _(sp):
                with sp.Fori(0, PAIRS) as i:
                    sp.wait_ge(made, 1)
                    sp.wait_ge(b_xb, i)
                    sp.dma_start(xin[:, :, :], pair_rows(a["x"], i)).then_inc(b_x, 16)
                    sp.wait_ge(made, 1)
                    sp.wait_ge(b_lin, i)
                    sp.dma_start(xT[:, :, :], xnT_d[:, :, bass.ds(i * TP, TP)]).then_inc(b_xT, 16)
                    sp.wait_ge(made, 1)
                    sp.wait_ge(b_s1, 2 * i)
                    sp.dma_start(base[:, :, :], pair_rows(nslow_d, i)).then_inc(b_base, 16)
                    sp.wait_ge(made, 1)
                    sp.wait_ge(b_acc, 2 * EX * (i + 1))
                    sp.dma_start(pair_rows(x2_d, i), acc[:, :, :]).then_inc(b_x2s, 16)
                    sp.wait_ge(made, 1)
                    sp.wait_ge(b_x2T, i + 1)
                    sp.dma_start(xn2T_d[:, :, bass.ds(i * TP, TP)], x2T[:, :, :]).then_inc(b_x2Ts, 16)
                    sp.wait_ge(made, 1)
                    sp.wait_ge(b_h, 3 * (i + 1))
                    sp.dma_start(pair_rows(htab, i), hrow[:, :, :]).then_inc(b_hs, 16)
                    sp.dma_start(pair_rows(hbase_d, i), hrow[:, :, 0:D]).then_inc(b_hs, 16)
                sp.wait_ge(b_x2s, 16 * PAIRS)
                sp.wait_ge(b_x2Ts, 16 * PAIRS)
                sp.wait_ge(b_hs, 32 * PAIRS)

            @block.gpsimd
            def _(pool):
                with pool.Fori(0, PAIRS) as i:
                    for u in range(2):
                        t = i * 2 + u
                        pool.wait_ge(b_seg, 2 * i)
                        pool.wait_ge(b_rows[u], 16 * CH * i)
                        pool.tensor_copy(idx[:, u, :], srcw[:, bass.ds(t * CH, CH)]).then_inc(b_idx, 1)
                        wait_apart(pool, b_idx, t + 1)
                        for c in range(CH):
                            pool.indirect_dma_start(
                                ring16[:, u, c, 0:2 * D], None, xtab,
                                bass.IndirectOffsetOnAxis(ap=idx[:, u, c:c + 1], axis=0)).then_inc(b_rows[u], 16)

            @block.tensor
            def _(pe):
                pe.wait_ge(load_experts0, 48)

                def hidden(w, rhs, e, bank, done):
                    for m in range(KD):
                        for k in range(KD):
                            last = pe.matmul(ps[bank][:, m * D:m * D + TP], w[:, e, k, m * P:m * P + P],
                                             rhs[:, k, :], start=(k == 0), stop=(k == KD - 1))
                    last.then_inc(done, 1)

                with pe.Fori(0, PAIRS) as i:
                    for u in range(2):
                        t = i * 2 + u
                        pe.wait_ge(b_rows[u], 16 * CH * (i + 1))
                        pe.wait_ge(b_hot, t + 1)
                        pe.wait_ge(b_hn, 2 * i)
                        for c in range(CH):
                            pe.matmul(ps[u][0:T, :], hot[:, u, c, :], ring16[:, u, c, 0:2 * D],
                                      start=(c == 0), stop=(c == CH - 1))
                        for c in range(CH):
                            last = pe.matmul(ps[7][0:T, u:u + 1], hot[:, u, c, :], ones16[:, :],
                                             start=(c == 0), stop=(c == CH - 1))
                        last.then_inc(b_seg, 1)
                    for u in range(2):
                        pe.wait_ge(b_hn, 2 * i + u + 1)
                        for k in range(KD):
                            last = pe.transpose(ps[6][:, k * TP + u * T:k * TP + u * T + T],
                                                hn[:, u, k * P:k * P + P], ident[0:T, 0:T])
                    last.then_inc(b_hnTp, 1)
                    pe.wait_ge(b_xT, 16 * (i + 1))
                    pe.wait_ge(b_hnT, i + 1)
                    pe.wait_ge(b_acc, 2 * EX * i)
                    for u in range(2):
                        for k in range(2 * KD):
                            src = xT if k < KD else hnT
                            last = pe.matmul(ps[4][0:T, u * D:u * D + D], src[:, k % KD, u * T:u * T + T],
                                             WL[:, k, :], start=(k == 0), stop=(k == 2 * KD - 1))
                    last.then_inc(b_lin, 1)
                    pe.wait_ge(b_u, 4 * i + 2)
                    for u in range(2):
                        for k in range(KD):
                            last = pe.transpose(ps[6][:, k * TP + u * T:k * TP + u * T + T],
                                                xn[:, u, k * P:k * P + P], ident[0:T, 0:T])
                    last.then_inc(b_uTp, 1)
                    pe.wait_ge(b_uT, i + 1)
                    for u in range(2):
                        for k in range(KD):
                            last = pe.matmul(ps[7][0:T, 8 + EX * u:8 + EX * u + EX], uT[:, k, u * T:u * T + T],
                                             Wr[:, k, :], start=(k == 0), stop=(k == KD - 1))
                    last.then_inc(b_lg, 1)
                    pe.wait_ge(b_h1, 2 * EX * i)
                    hidden(W1, uT, 0, 2, b_A)
                    pe.wait_ge(b_w, i + 1)
                    for u in range(2):
                        last = pe.transpose(ps[7][0:EX, 32 + u * T:32 + u * T + T], lg[:, 5, u, :], ident[0:T, 0:T])
                    last.then_inc(b_wTp, 1)
                    pe.wait_ge(b_wT, i + 1)
                    for u in range(2):
                        last = pe.matmul(ps[5][0:T, u * D:u * D + D], wT[:, u * T:u * T + T], bo[:, :],
                                         start=True, stop=True)
                    last.then_inc(b_bo, 1)

                    def out_of(e):
                        n = EX * i + e
                        pe.wait_ge(b_h2, 2 * n + 2)
                        if e < 2:
                            pe.wait_ge(b_x1, 2 * i + 2)
                        else:
                            pe.wait_ge(b_acc, 2 * (n - 1))
                        for u in range(2):
                            for k in range(KD):
                                last = pe.matmul(ps[4 + e % 2][0:T, u * D:u * D + D], h2[:, k, u * T:u * T + T],
                                                 Wo[:, e, k, :], start=(k == 0), stop=(k == KD - 1))
                        last.then_inc(b_Y, 1)

                    for e in range(EX):
                        n = EX * i + e
                        if e + 1 < EX:
                            pe.wait_ge(b_h1, 2 * n + 2)
                            hidden(W1, uT, e + 1, 2, b_A)
                        else:
                            pe.wait_ge(b_h1, 2 * n + 2)
                        pe.wait_ge(b_h2, 2 * n)
                        hidden(W2, h1, e, 3, b_B)
                        if e:
                            out_of(e - 1)
                    out_of(EX - 1)

                    pe.wait_ge(b_u, 4 * i + 4)
                    for u in range(2):
                        for k in range(KD):
                            last = pe.transpose(ps[6][:, k * TP + u * T:k * TP + u * T + T],
                                                xn[:, u, k * P:k * P + P], ident[0:T, 0:T])
                    last.then_inc(b_uTp, 1)
                    pe.wait_ge(b_x2T, i + 1)
                    for u in range(2):
                        for k in range(KD):
                            pe.matmul(ps[2][0:T, u * D:u * D + D], x2T[:, k, u * T:u * T + T], wg[:, k, :],
                                      start=(k == 0), stop=(k == KD - 1))
                    for u in range(2):
                        for k in range(KD):
                            last = pe.matmul(ps[7][0:T, 288 + 3 * u:291 + 3 * u], x2T[:, k, u * T:u * T + T],
                                             wg3[:, k, :], start=(k == 0), stop=(k == KD - 1))
                    last.then_inc(b_hr, 1)
                    pe.wait_ge(b_kc, 2 * i)
                    for k in range(KD):
                        pe.matmul(ps[3][:, 0:TP], wqkv1[:, k, HID1:2 * HID1], x2T[:, k, :],
                                  start=(k == 0), stop=(k == KD - 1))
                    for u in range(2):
                        for k in range(KD):
                            last = pe.matmul(ps[3][0:T, D + u * HID1:D + u * HID1 + HID1],
                                             x2T[:, k, u * T:u * T + T], wqkv1[:, k, 2 * HID1:3 * HID1],
                                             start=(k == 0), stop=(k == KD - 1))
                    last.then_inc(b_kv, 1)
                    pe.wait_ge(b_hb, i + 1)
                    pe.wait_ge(b_kc, 2 * i + 2)

            @block.scalar
            def _(act):
                with act.Fori(0, PAIRS) as i:
                    act.wait_ge(b_hnTp, i + 1)
                    act.copy(hnT[:, :, :], turned_pair(6)).then_inc(b_hnT, 1)
                    act.wait_ge(b_nb, 2 * i + 1)
                    act.wait_ge(b_uTp, 2 * i)
                    for u in range(2):
                        act.activation(xn[:, u, :], acc[:, u, :], ACT.Identity, bias=nb[:, u:u + 1],
                                       scale=rs[:, u:u + 1]).then_inc(b_u, 1)
                    act.wait_ge(b_uTp, 2 * i + 1)
                    act.copy(uT[:, :, :], turned_pair(6)).then_inc(b_uT, 1)
                    act.wait_ge(b_zs, i + 1)
                    act.activation(lg[:, 2, :, :], lg[:, 1, :, :], ACT.Exp).then_inc(b_e, 1)
                    act.wait_ge(b_wTp, i + 1)
                    act.copy(wT[:, :], ps[7][0:EX, 32:32 + TP]).then_inc(b_wT, 1)

                    def relu(e, bank, layer, target, product, free, free_at, done):
                        act.wait_ge(product, EX * i + e + 1)
                        act.wait_ge(free, free_at)
                        for m in range(KD):
                            act.activation(target[:, m, :], ps[bank][:, m * D:m * D + TP], ACT.Relu,
                                           bias=bn[:, layer, 1, 2 * e + m:2 * e + m + 1],
                                           scale=bn[:, layer, 0, 2 * e + m:2 * e + m + 1]).then_inc(done, 1)

                    relu(0, 2, 0, h1, b_A, b_B, EX * i, b_h1)
                    for e in range(EX):
                        n = EX * i + e
                        relu(e, 3, 1, h2, b_B, b_Y, n, b_h2)
                        if e + 1 < EX:
                            relu(e + 1, 2, 0, h1, b_A, b_B, n + 1, b_h1)
                    act.wait_ge(b_nb, 2 * i + 2)
                    for u in range(2):
                        act.activation(xn[:, u, :], acc[:, u, :], ACT.Identity, bias=nb[:, u:u + 1],
                                       scale=rs[:, u:u + 1]).then_inc(b_u, 1)
                    act.wait_ge(b_uTp, 2 * i + 2)
                    act.wait_ge(b_x2Ts, 16 * i)
                    act.copy(x2T[:, :, :], turned_pair(6)).then_inc(b_x2T, 1)
                    act.wait_ge(b_ext, i + 1)
                    act.activation(sm[:, 8, :], ext[:, :, 0], ACT.Exp, scale=-1.0).then_inc(b_me, 1)
                    act.wait_ge(b_kv, i + 1)
                    act.copy(kT_all[:, bass.ds(i * TP, TP)], ps[3][:, 0:TP]).then_inc(b_kc, 1)
                    act.copy(v_all[:, bass.ds(i * 2, 2), :],
                             ps[3][0:T, D:2 * D].rearrange("p (u d) -> p u d", u=2)).then_inc(b_kc, 1)

            @block.vector
            def _(dve):
                roots = [0]

                def root_step(i):
                    def step(ins):
                        roots[0] += 1
                        ins.then_inc(b_root, 1)
                        dve.wait_ge(b_root, 3 * ROOT_STEPS * i + roots[0])
                    return step

                def norm(i, s, ready):
                    n = 2 * i + s
                    for w in ready:
                        dve.wait_ge(*w)
                    for u in range(2):
                        dve.bn_stats(st[:, u, :], acc[:, u, :]).then_inc(b_norm, 1)
                    wait_apart(dve, b_norm, 5 * n + 2)
                    for u in range(2):
                        dve.bn_aggr(mv[:, u, :], st[:, u, :]).then_inc(b_norm, 1)
                    dve.wait_ge(b_norm, 5 * n + 4)
                    dve.wait_ge(b_u, 2 * n)
                    dve.tensor_scalar(sm[:, 14, :], mv[:, :, 1], LN_EPS, None, ALU.add).then_inc(b_norm, 1)
                    dve.wait_ge(b_norm, 5 * n + 5)
                    inverse_root(dve, root_step(i), rs[:, :], sm[:, 14, :], sm[:, 15, :])
                    dve.scalar_tensor_tensor(nb[:, :], mv[:, :, 0], -1.0, rs[:, :], ALU.mult, ALU.mult)\
                        .then_inc(b_nb, 1)

                with dve.Fori(0, PAIRS) as i:
                    for u in range(2):
                        t = i * 2 + u
                        dve.wait_ge(b_seg, 2 * i)
                        dve.tensor_tensor(hot[:, u, :, :], col(relw[:, bass.ds(t * CH, CH)], T),
                                          mid(iota[:, :], CH), ALU.is_equal).then_inc(b_hot, 1)
                    dve.wait_ge(b_x, 16 * (i + 1))
                    dve.tensor_tensor(tmp[:, :, :], xin[:, :, :], mid(bias0[:, :], 2), ALU.add).then_inc(b_xb, 1)
                    dve.wait_ge(b_seg, 2 * i + 2)
                    dve.tensor_scalar(sm[:, 0, :], ps[7][0:T, 0:2], 1.0, None, ALU.max).then_inc(b_cnt, 1)
                    dve.wait_ge(b_cnt, 2 * i + 1)
                    dve.reciprocal(sm[:, 1, :], sm[:, 0, :]).then_inc(b_cnt, 1)
                    dve.wait_ge(b_cnt, 2 * i + 2)
                    dve.wait_ge(b_base, 16 * (i + 1))
                    dve.wait_ge(b_hnTp, i)
                    for u in range(2):
                        dve.scalar_tensor_tensor(base[:, u, :], ps[u][0:T, D:2 * D], sm[:, 1, u:u + 1], base[:, u, :],
                                                 ALU.mult, ALU.add).then_inc(b_s1, 1)
                    for u in range(2):
                        dve.wait_ge(b_s1, 2 * i + u + 1)
                        dve.scalar_tensor_tensor(hn[:, u, :], ps[u][0:T, 0:D], sm[:, 1, u:u + 1], base[:, u, :],
                                                 ALU.mult, ALU.add).then_inc(b_hn, 1)
                    dve.wait_ge(b_lin, i + 1)
                    dve.wait_ge(b_xb, i + 1)
                    dve.wait_ge(b_x2s, 16 * i)
                    dve.tensor_tensor(acc[:, :, :], tmp[:, :, :], bank2(4), ALU.add).then_inc(b_x1, 1)
                    norm(i, 0, [(b_x1, 2 * i + 1)])
                    dve.wait_ge(b_lg, i + 1)
                    dve.tensor_tensor(lg[:, 0, :, :], ps[7][0:T, 8:8 + 2 * EX].rearrange("p (u e) -> p u e", u=2),
                                      mid(br[:, :], 2), ALU.add).then_inc(b_router, 1)
                    dve.wait_ge(b_router, 4 * i + 1)
                    dve.tensor_reduce(sm[:, 2, :], lg[:, 0, :, :], AX, ALU.max).then_inc(b_router, 1)
                    dve.wait_ge(b_router, 4 * i + 2)
                    dve.tensor_tensor(lg[:, 1, :, :], lg[:, 0, :, :], col(sm[:, 2, :], EX), ALU.subtract)\
                        .then_inc(b_zs, 1)
                    dve.wait_ge(b_e, i + 1)
                    dve.tensor_reduce(sm[:, 3, :], lg[:, 2, :, :], AX, ALU.add).then_inc(b_router, 1)
                    dve.wait_ge(b_router, 4 * i + 3)
                    dve.reciprocal(sm[:, 4, :], sm[:, 3, :]).then_inc(b_router, 1)
                    dve.wait_ge(b_router, 4 * i + 4)
                    dve.tensor_tensor(lg[:, 5, :, :], lg[:, 2, :, :], col(sm[:, 4, :], EX), ALU.mult).then_inc(b_w, 1)
                    dve.wait_ge(b_bo, i + 1)
                    dve.wait_ge(b_u, 4 * i + 2)
                    dve.tensor_tensor(acc[:, :, :], acc[:, :, :], bank2(5), ALU.add).then_inc(b_x1, 1)
                    dve.wait_ge(b_x1, 2 * i + 2)
                    for e in range(EX):
                        dve.wait_ge(b_Y, EX * i + e + 1)
                        for u in range(2):
                            if e:
                                dve.wait_ge(b_acc, 2 * (EX * i + e) - 1 + u)
                            dve.scalar_tensor_tensor(acc[:, u, :], bank2(4 + e % 2)[:, u, :], lg[:, 5, u, e:e + 1],
                                                     acc[:, u, :], ALU.mult, ALU.add).then_inc(b_acc, 1)
                    norm(i, 1, [(b_acc, 2 * EX * (i + 1))])
                    dve.wait_ge(b_hr, i + 1)
                    dve.tensor_tensor(ext[:, :, :], ps[7][0:T, 288:294].rearrange("p (u c) -> p u c", u=2),
                                      mid(c3[:, :], 2), ALU.add).then_inc(b_ext, 1)
                    dve.tensor_tensor(tmp[:, :, :], bank2(2), mid(gb[:, :], 2), ALU.add).then_inc(b_hb, 1)
                    dve.wait_ge(b_hb, i + 1)
                    for u in range(2):
                        dve.tensor_tensor_reduce(hn[:, u, :], tmp[:, u, :], tmp[:, u, :], 1.0, 0.0, ALU.mult,
                                                 ALU.add, sm[:, 5, u:u + 1]).then_inc(b_ss, 1)
                    dve.wait_ge(b_ss, 2 * i + 2)
                    inverse_root(dve, root_step(i), sm[:, 6, :], sm[:, 5, :], sm[:, 15, :])
                    dve.tensor_scalar(sm[:, 7, :], sm[:, 6, :], 1e12, None, ALU.min).then_inc(b_mag, 1)
                    dve.wait_ge(b_me, i + 1)
                    dve.tensor_scalar(sm[:, 9, :], sm[:, 8, :], 1.0, None, ALU.add).then_inc(b_mag, 1)
                    dve.wait_ge(b_mag, 4 * i + 2)
                    dve.reciprocal(sm[:, 10, :], sm[:, 9, :]).then_inc(b_mag, 1)
                    dve.wait_ge(b_mag, 4 * i + 3)
                    dve.scalar_tensor_tensor(sm[:, 11, :], sm[:, 10, :], 1.5, sm[:, 7, :], ALU.mult, ALU.mult)\
                        .then_inc(b_mag, 1)
                    dve.wait_ge(b_mag, 4 * i + 4)
                    dve.wait_ge(b_hs, 32 * i)
                    dve.tensor_tensor(ht_all[:, bass.ds(i * 2, 2)], ext[:, :, 2], sm[:, 11, :], ALU.mult)\
                        .then_inc(b_h, 1)
                    dve.tensor_tensor(hrow[:, :, D + 1], ext[:, :, 1], sm[:, 11, :], ALU.mult).then_inc(b_h, 1)
                    dve.tensor_tensor(hrow[:, :, 0:D], tmp[:, :, :], col(sm[:, 11, :], D), ALU.mult).then_inc(b_h, 1)

        ekT = ring[0:T, 0, :, :].rearrange("p c d -> p (c d)")[:, 0:2 * HID1].rearrange("p (u d) -> p u d", u=2)
        ek = ring[:, 1, :, :].rearrange("p c d -> p (c d)")[:, 0:TP]
        ctxs = ring[:, 1, :, :].rearrange("p c d -> p (c d)")[:, 512:640]
        ctxT = ring[:, 1, :, :].rearrange("p c d -> p (c d)")[:, 640:768]
        g1 = ring[:, 1, :, :].rearrange("p c d -> p (c d)")[:, 768:1024]
        m_max = sem("m_k_max")
        m_e = sem("m_k_exp")
        m_t = sem("m_k_turned")
        m_c = sem("m_k_turned_copied")
        m_ctx = sem("m_context")
        m_copied = sem("m_copied")
        m_product = sem("m_product")
        with nc.Block() as block:
            @block.sync
            def _(sp):
                for w, name in ((W1, "L1_ffn_w1"), (W2, "L1_ffn_w2")):
                    sp.dma_start(w[:, :, :, :], a[name].rearrange("e (k p) d -> p e k d", p=P))\
                        .then_inc(load_experts1, 16)

            @block.vector
            def _(dve):
                dve.memset(ctxs, 0.0).then_inc(m_copied, 1)
                dve.tensor_reduce(fl[:, 0:1], kT_all[:, :], AX, ALU.max).then_inc(m_max, 1)
                dve.wait_ge(m_max, 1)
                dve.tensor_scalar(fl[:, 1:2], fl[:, 0:1], -1.0, None, ALU.mult).then_inc(m_max, 1)
                with dve.Fori(0, PAIRS) as i:
                    dve.wait_ge(m_t, i + 1)
                    dve.wait_ge(m_ctx, i)
                    dve.tensor_copy(ekT, ps[0][0:T, 0:2 * HID1].rearrange("p (u d) -> p u d", u=2)).then_inc(m_c, 1)
                dve.wait_ge(m_ctx, PAIRS)
                dve.reciprocal(fl[:, 2:3], ps[2][:, 0:1]).then_inc(m_copied, 1)
                dve.wait_ge(m_copied, 2)
                for h in range(HEADS1):
                    r = slice(HD1 * h, HD1 * h + HD1)
                    dve.tensor_scalar(ctxs[r, r], ps[1][r, r], fl[r, 2:3], HD1 ** -0.5, ALU.mult, ALU.mult)\
                        .then_inc(m_copied, 1)
                dve.wait_ge(m_product, 1)
                dve.tensor_copy(ctxT, ps[3][:, 0:P]).then_inc(m_copied, 1)
                dve.wait_ge(m_product, 2)
                dve.tensor_copy(g1, ps[4][:, 0:D]).then_inc(m_copied, 1)
                dve.wait_ge(m_product, 3)
                dve.tensor_copy(M1[:, :, :], ps[5][:, :].rearrange("p (k d) -> p k d", k=KD)).then_inc(m_copied, 1)

            @block.scalar
            def _(act):
                act.wait_ge(m_max, 2)
                with act.Fori(0, PAIRS) as i:
                    act.wait_ge(m_t, i)
                    act.activation(ek, kT_all[:, bass.ds(i * TP, TP)], ACT.Exp, bias=fl[:, 1:2]).then_inc(m_e, 1)

            @block.tensor
            def _(pe):
                pe.matmul(ps[1][:, 0:HID1], zeros[:, 0:P], zeros[:, 0:HID1], start=True, stop=False,
                          skip_group_check=True)
                pe.matmul(ps[2][:, 0:1], zeros[:, 0:P], zeros[:, 0:1], start=True, stop=False,
                          skip_group_check=True)
                with pe.Fori(0, PAIRS) as i:
                    pe.wait_ge(m_e, i + 1)
                    pe.wait_ge(m_c, i)
                    for u in range(2):
                        last = pe.transpose(ps[0][0:T, u * HID1:(u + 1) * HID1], ek[:, u * T:u * T + T], ident[:, :])
                    last.then_inc(m_t, 1)
                    pe.wait_ge(m_c, i + 1)
                    for u in range(2):
                        pe.matmul(ps[1][:, 0:HID1], ekT[:, u, :], v_all[:, bass.ds(i * 2 + u, 1), :],
                                  start=False, stop=False, skip_group_check=True)
                        last = pe.matmul(ps[2][:, 0:1], ekT[:, u, :], ones[0:T, 0:1], start=False, stop=False,
                                         skip_group_check=True)
                    last.then_inc(m_ctx, 1)
                pe.wait_ge(m_copied, 2 + HEADS1)
                pe.transpose(ps[3][:, 0:P], ctxs, ident[:, :]).then_inc(m_product, 1)
                pe.wait_ge(m_copied, 3 + HEADS1)
                pe.matmul(ps[4][:, 0:D], ctxT, wout1[:, :], start=True, stop=True).then_inc(m_product, 1)
                pe.wait_ge(m_copied, 4 + HEADS1)
                for k in range(KD):
                    last = pe.matmul(ps[5][:, k * D:k * D + D], wq1T[:, k, :], g1, start=True, stop=True)
                last.then_inc(m_product, 1)

        c_x = sem("c_x2_loaded")
        c_xT = sem("c_xT_loaded")
        c_base = sem("c_h_loaded")
        c_idx = sem("c_idx")
        c_rows = [sem("c_rows_gathered_0"), sem("c_rows_gathered_1")]
        c_hot = sem("c_one_hot")
        c_xb = sem("c_x_bias")
        c_hk = sem("c_score_positive")
        c_V = sem("c_scores_of_targets")
        c_vm = sem("c_max_over_chunks")
        c_vT = sem("c_max_turned")
        c_m = sem("c_max_of_target")
        c_chain = sem("c_shift_steps")
        c_dg = sem("c_shift_diagonal")
        c_row = sem("c_shift_rows")
        c_E = sem("c_edge_exp")
        c_P = sem("c_edge_weights")
        c_agg = sem("c_weighted_sums")
        c_se = sem("c_sum_guarded_reciprocal")
        c_hc = sem("c_h_combined")
        c_ss = sem("c_h_squares")
        c_ball = sem("c_ball_steps")
        c_th = sem("c_tanh")
        c_ff = sem("c_h_scale")
        c_lin = sem("c_mixer")
        c_x3 = sem("c_x3")
        c_root = sem("c_root_steps")
        c_norm = sem("c_stats_mean_rstd")
        c_nb = sem("c_shift")
        c_u = sem("c_normalized")
        c_uTp = sem("c_turned")
        c_uT = sem("c_uT")
        c_lg = sem("c_logits")
        c_zs = sem("c_logits_less_max")
        c_e = sem("c_router_exp")
        c_top = sem("c_router_steps")
        c_w = sem("c_router_weights")
        c_w2 = sem("c_router_masks")
        c_wTp = sem("c_weights_turned")
        c_wT = sem("c_weights_turned_copied")
        c_b2 = sem("c_expert_biases")
        c_A = sem("c_hidden_product")
        c_g = sem("c_hidden")
        c_Y = sem("c_expert_out")
        c_acc = sem("c_expert_added")
        c_out = sem("c_out_stored")
        vm = sb("vm", [P, 2, T])
        dg = sb("dg", [T, 2, T])
        hk = sb("hk", [P, 2, CH])

        with nc.Block() as block:
            @block.sync
            def _(sp):
                with sp.Fori(0, PAIRS) as i:
                    sp.wait_ge(made, 1)
                    sp.wait_ge(c_xb, i)
                    sp.dma_start(xin[:, :, :], pair_rows(x2_d, i)).then_inc(c_x, 16)
                    sp.wait_ge(made, 1)
                    sp.wait_ge(c_lin, i)
                    sp.dma_start(xT[:, :, :], xn2T_d[:, :, bass.ds(i * TP, TP)]).then_inc(c_xT, 16)
                    sp.wait_ge(made, 1)
                    sp.wait_ge(c_hc, 2 * i)
                    sp.dma_start(base[:, :, :], pair_rows(hbase_d, i)).then_inc(c_base, 16)
                    sp.wait_ge(made, 1)
                    sp.wait_ge(c_acc, 2 * EX * (i + 1))
                    sp.dma_start(pair_rows(out, i), acc[:, :, :]).then_inc(c_out, 16)
                sp.wait_ge(c_out, 16 * PAIRS)

            @block.gpsimd
            def _(pool):
                with pool.Fori(0, PAIRS) as i:
                    for u in range(2):
                        t = i * 2 + u
                        pool.wait_ge(c_agg, 2 * i)
                        pool.wait_ge(c_rows[u], 16 * CH * i)
                        pool.tensor_copy(idx[:, u, :], srcw[:, bass.ds(t * CH, CH)]).then_inc(c_idx, 1)
                        wait_apart(pool, c_idx, t + 1)
                        for c in range(CH):
                            pool.indirect_dma_start(
                                ring[:, u, c, :], None, htab,
                                bass.IndirectOffsetOnAxis(ap=idx[:, u, c:c + 1], axis=0)).then_inc(c_rows[u], 16)

            @block.tensor
            def _(pe):
                pe.wait_ge(load_experts1, 32)
                with pe.Fori(0, PAIRS) as i:
                    for u in range(2):
                        pe.wait_ge(c_vm, 2 * i + u + 1)
                        pe.transpose(ps[7 - u][0:T, 0:P], vm[:, u, :], ident[:, :]).then_inc(c_vT, 1)
                    pe.wait_ge(c_xT, 16 * (i + 1))
                    pe.wait_ge(c_acc, 2 * EX * i)
                    for u in range(2):
                        for k in range(KD):
                            last = pe.matmul(ps[4][0:T, u * D:u * D + D], xT[:, k, u * T:u * T + T], M1[:, k, :],
                                             start=(k == 0), stop=(k == KD - 1))
                    last.then_inc(c_lin, 1)
                    for u in range(2):
                        pe.wait_ge(c_dg, 2 * i + u + 1)
                        pe.matmul(ps[3 - u][:, 0:T], ones[0:T, :], dg[:, u, :], start=True, stop=True)\
                            .then_inc(c_row, 1)
                    for u in range(2):
                        pe.wait_ge(c_P, 2 * i + u + 1)
                        for c in range(CH):
                            last = pe.matmul(ps[u][0:T, 0:D + 1], big[:, u, c, :], ring[:, u, c, 0:D + 1],
                                             start=(c == 0), stop=(c == CH - 1))
                        last.then_inc(c_agg, 1)
                    pe.wait_ge(c_u, 2 * i + 2)
                    for u in range(2):
                        for k in range(KD):
                            last = pe.transpose(ps[6][:, k * TP + u * T:k * TP + u * T + T],
                                                xn[:, u, k * P:k * P + P], ident[0:T, 0:T])
                    last.then_inc(c_uTp, 1)
                    pe.wait_ge(c_uT, i + 1)
                    for u in range(2):
                        for k in range(KD):
                            last = pe.matmul(ps[7][0:T, 256 + EX * u:256 + EX * u + EX], uT[:, k, u * T:u * T + T],
                                             rwT[:, k, :], start=(k == 0), stop=(k == KD - 1))
                    last.then_inc(c_lg, 1)

                    def hidden(e):
                        bank = 2 if e % 2 == 0 else 6
                        for m in range(KD):
                            for k in range(KD):
                                last = pe.matmul(ps[bank][:, m * D:m * D + TP], W1[:, e, k, m * P:m * P + P],
                                                 uT[:, k, :], start=(k == 0), stop=(k == KD - 1))
                        last.then_inc(c_A, 1)

                    hidden(0)
                    hidden(1)
                    pe.wait_ge(c_w, i + 1)
                    for u in range(2):
                        last = pe.transpose(ps[3][0:EX, 256 + u * T:256 + u * T + T], lg[:, 5, u, :], ident[0:T, 0:T])
                    last.then_inc(c_wTp, 1)
                    pe.wait_ge(c_wT, i + 1)
                    for u in range(2):
                        last = pe.matmul(ps[5][0:T, u * D:u * D + D], wT[:, u * T:u * T + T], b2[:, :],
                                         start=True, stop=True)
                    last.then_inc(c_b2, 1)
                    for e in range(EX):
                        n = EX * i + e
                        src = h1 if e % 2 == 0 else h2
                        pe.wait_ge(c_g, 2 * n + 2)
                        if e < 2:
                            pe.wait_ge(c_x3, 5 * i + 5)
                        else:
                            pe.wait_ge(c_acc, 2 * (n - 1))
                        for u in range(2):
                            for k in range(KD):
                                last = pe.matmul(ps[4 + e % 2][0:T, u * D:u * D + D], src[:, k, u * T:u * T + T],
                                                 W2[:, e, k, :], start=(k == 0), stop=(k == KD - 1))
                        last.then_inc(c_Y, 1)
                        if e + 2 < EX:
                            hidden(e + 2)

            @block.scalar
            def _(act):
                with act.Fori(0, PAIRS) as i:
                    for u in range(2):
                        act.wait_ge(c_row, 2 * i + u + 1)
                        act.wait_ge(c_vm, 2 * i + u + 1)
                        for c in range(CH):
                            act.activation(big[:, u, c, :], ps[3 - u][:, 0:T], ACT.Exp,
                                           bias=ring[:, u, c, D + 1:D + 2]).then_inc(c_E, 1)
                    act.wait_ge(c_ball, 8 * i + 2)
                    act.activation(sm[:, 12, :], sm[:, 11, :], ACT.Tanh).then_inc(c_th, 1)
                    act.wait_ge(c_nb, i + 1)
                    for u in range(2):
                        act.activation(xn[:, u, :], acc[:, u, :], ACT.Identity, bias=nb[:, u:u + 1],
                                       scale=rs[:, u:u + 1]).then_inc(c_u, 1)
                    act.wait_ge(c_uTp, i + 1)
                    act.copy(uT[:, :, :], turned_pair(6)).then_inc(c_uT, 1)
                    act.wait_ge(c_zs, i + 1)
                    act.activation(lg[:, 2, :, :], lg[:, 1, :, :], ACT.Exp).then_inc(c_e, 1)
                    act.wait_ge(c_wTp, i + 1)
                    act.copy(wT[:, :], ps[3][0:EX, 256:256 + TP]).then_inc(c_wT, 1)
                    for e in range(EX):
                        n = EX * i + e
                        act.wait_ge(c_A, n + 1)
                        if e >= 2:
                            act.wait_ge(c_Y, n - 1)
                        bank = 2 if e % 2 == 0 else 6
                        target = h1 if e % 2 == 0 else h2
                        for m in range(KD):
                            act.activation(target[:, m, :], ps[bank][:, m * D:m * D + TP], ACT.Gelu,
                                           bias=b1c[:, 2 * e + m:2 * e + m + 1]).then_inc(c_g, 1)

            @block.vector
            def _(dve):
                with dve.Fori(0, PAIRS) as i:
                    chain = {c_chain: 0, c_ball: 0, c_top: 0, c_root: 0}
                    per = {c_chain: 4, c_ball: 8, c_top: 18, c_root: 2 * ROOT_STEPS}

                    def step(s, ins):
                        chain[s] += 1
                        ins.then_inc(s, 1)
                        dve.wait_ge(s, i * per[s] + chain[s])

                    for u in range(2):
                        t = i * 2 + u
                        dve.wait_ge(c_agg, 2 * i)
                        dve.tensor_tensor(hot[:, u, :, :], col(relw[:, bass.ds(t * CH, CH)], T),
                                          mid(iota[:, :], CH), ALU.is_equal).then_inc(c_hot, 1)
                    for u in range(2):
                        t = i * 2 + u
                        dve.wait_ge(c_rows[u], 16 * CH * (i + 1))
                        dve.tensor_scalar(hk[:, u, :], ring[:, u, :, D + 1], hbound[:, 0:1], None, ALU.add)\
                            .then_inc(c_hk, 1)
                        dve.wait_ge(c_hk, t + 1)
                        dve.wait_ge(c_hot, t + 1)
                        dve.tensor_tensor(big[:, u, :, :], hot[:, u, :, :], col(hk[:, u, :], T), ALU.mult)\
                            .then_inc(c_V, 1)
                        dve.wait_ge(c_V, t + 1)
                        dve.wait_ge(c_vT, t)
                        dve.tensor_reduce(vm[:, u, :], big[:, u, :, :].rearrange("p c d -> p d c"), AX, ALU.max)\
                            .then_inc(c_vm, 1)
                    dve.wait_ge(c_x, 16 * (i + 1))
                    dve.tensor_tensor(tmp[:, :, :], xin[:, :, :], mid(bias1[:, :], 2), ALU.add).then_inc(c_xb, 1)
                    for u in range(2):
                        dve.wait_ge(c_vT, 2 * i + u + 1)
                        dve.tensor_reduce(sm[:, 0, u:u + 1], ps[7 - u][0:T, 0:P], AX, ALU.max)\
                            .then_inc(c_m, 1)
                    dve.wait_ge(c_m, 2 * i + 2)
                    ht = ht_all[:, bass.ds(i * 2, 2)]
                    step(c_chain, dve.tensor_scalar(sm[:, 1, :], sm[:, 0, :], nbound[0:T, 0:1], None, ALU.add))
                    step(c_chain, dve.tensor_tensor(sm[:, 2, :], sm[:, 1, :], ht, ALU.add))
                    step(c_chain, dve.tensor_scalar(sm[:, 3, :], sm[:, 2, :], -1e9, None, ALU.max))
                    step(c_chain, dve.tensor_tensor(sm[:, 4, :], ht, sm[:, 3, :], ALU.subtract))
                    for u in range(2):
                        dve.tensor_scalar(dg[:, u, :], ident[0:T, 0:T], sm[:, 4, u:u + 1], None, ALU.mult)\
                            .then_inc(c_dg, 1)
                    for u in range(2):
                        dve.wait_ge(c_E, CH * (2 * i + u + 1))
                        dve.scalar_tensor_tensor(big[:, u, :, :], big[:, u, :, :], FAR, hot[:, u, :, :],
                                                 ALU.min, ALU.mult).then_inc(c_P, 1)
                    dve.wait_ge(c_base, 16 * (i + 1))
                    for u in range(2):
                        t = i * 2 + u
                        dve.wait_ge(c_agg, t + 1)
                        dve.tensor_scalar(sm[:, 5, u:u + 1], ps[u][0:T, D:D + 1], 1e-10, None, ALU.add).then_inc(c_se, 1)
                        dve.wait_ge(c_se, 2 * t + 1)
                        dve.reciprocal(sm[:, 6, u:u + 1], sm[:, 5, u:u + 1]).then_inc(c_se, 1)
                        dve.wait_ge(c_se, 2 * t + 2)
                        dve.scalar_tensor_tensor(hn[:, u, :], ps[u][0:T, 0:D], sm[:, 6, u:u + 1], base[:, u, :],
                                                 ALU.mult, ALU.add).then_inc(c_hc, 1)
                    for u in range(2):
                        dve.wait_ge(c_hc, 2 * i + u + 1)
                        dve.tensor_tensor_reduce(xin[:, u, :], hn[:, u, :], hn[:, u, :], 1.0, 0.0, ALU.mult,
                                                 ALU.add, sm[:, 7, u:u + 1]).then_inc(c_ss, 1)
                    dve.wait_ge(c_ss, 2 * i + 2)
                    inverse_root(dve, lambda ins: step(c_root, ins), sm[:, 10, :], sm[:, 7, :], sm[:, 15, :])
                    step(c_ball, dve.tensor_tensor(sm[:, 10, :], sm[:, 10, :], sm[:, 7, :], ALU.mult))
                    step(c_ball, dve.tensor_scalar(sm[:, 11, :], sm[:, 10, :], 1e-15, None, ALU.max))
                    step(c_ball, dve.reciprocal(sm[:, 13, :], sm[:, 11, :]))
                    dve.wait_ge(c_th, i + 1)
                    step(c_ball, dve.tensor_tensor(sm[:, 14, :], sm[:, 12, :], sm[:, 13, :], ALU.mult))
                    step(c_ball, dve.tensor_tensor(sm[:, 15, :], sm[:, 14, :], sm[:, 10, :], ALU.mult))
                    step(c_ball, dve.tensor_scalar(sm[:, 16, :], sm[:, 15, :], 1e-8, None, ALU.add))
                    step(c_ball, dve.reciprocal(sm[:, 17, :], sm[:, 16, :]))
                    step(c_ball, dve.tensor_scalar(sm[:, 17, :], sm[:, 17, :], MAX_NORM, 1.0, ALU.mult, ALU.subtract))
                    dve.scalar_tensor_tensor(sm[:, 18, :], sm[:, 15, :], MAX_NORM, sm[:, 17, :], ALU.is_gt, ALU.mult)\
                        .then_inc(c_ff, 1)
                    dve.wait_ge(c_ff, 2 * i + 1)
                    dve.scalar_tensor_tensor(sm[:, 19, :], sm[:, 18, :], 1.0, sm[:, 14, :], ALU.add, ALU.mult)\
                        .then_inc(c_ff, 1)
                    dve.wait_ge(c_lin, i + 1)
                    dve.wait_ge(c_xb, i + 1)
                    dve.wait_ge(c_out, 16 * i)
                    dve.tensor_tensor(acc[:, :, :], tmp[:, :, :], bank2(4), ALU.add).then_inc(c_x3, 1)
                    dve.wait_ge(c_x3, 5 * i + 1)
                    dve.wait_ge(c_ff, 2 * i + 2)
                    for u in range(2):
                        dve.scalar_tensor_tensor(acc[:, u, :], hn[:, u, :], sm[:, 19, u:u + 1], acc[:, u, :],
                                                 ALU.mult, ALU.add).then_inc(c_x3, 1)
                    for u in range(2):
                        dve.wait_ge(c_x3, 5 * i + 2 + u)
                        dve.bn_stats(st[:, u, :], acc[:, u, :]).then_inc(c_norm, 1)
                    wait_apart(dve, c_norm, 5 * i + 2)
                    for u in range(2):
                        dve.bn_aggr(mv[:, u, :], st[:, u, :]).then_inc(c_norm, 1)
                    dve.wait_ge(c_norm, 5 * i + 4)
                    dve.tensor_scalar(sm[:, 14, :], mv[:, :, 1], LN_EPS, None, ALU.add).then_inc(c_norm, 1)
                    dve.wait_ge(c_norm, 5 * i + 5)
                    inverse_root(dve, lambda ins: step(c_root, ins), rs[:, :], sm[:, 14, :], sm[:, 15, :])
                    dve.scalar_tensor_tensor(nb[:, :], mv[:, :, 0], -1.0, rs[:, :], ALU.mult, ALU.mult)\
                        .then_inc(c_nb, 1)
                    dve.wait_ge(c_lg, i + 1)
                    z = ps[7][0:T, 256:256 + 2 * EX].rearrange("p (u e) -> p u e", u=2)
                    io = mid(iota8[:, :], 2)
                    step(c_top, dve.tensor_reduce(sm[:, 20, :], z, AX, ALU.max))
                    dve.tensor_tensor(lg[:, 1, :, :], z, col(sm[:, 20, :], EX), ALU.subtract).then_inc(c_zs, 1)
                    dve.wait_ge(c_e, i + 1)
                    step(c_top, dve.tensor_reduce(sm[:, 21, :], lg[:, 2, :, :], AX, ALU.add))
                    step(c_top, dve.reciprocal(sm[:, 22, :], sm[:, 21, :]))
                    step(c_top, dve.tensor_tensor(lg[:, 3, :, :], lg[:, 2, :, :], col(sm[:, 22, :], EX), ALU.mult))
                    for best in range(2):
                        p = lg[:, 3, :, :] if best == 0 else lg[:, 6, :, :]
                        step(c_top, dve.tensor_reduce(sm[:, 8 + best, :], p, AX, ALU.max))
                        step(c_top, dve.tensor_tensor(lg[:, 0, :, :], p, col(sm[:, 8 + best, :], EX), ALU.not_equal))
                        step(c_top, dve.scalar_tensor_tensor(lg[:, 0, :, :], lg[:, 0, :, :], 99.0, io, ALU.mult, ALU.add))
                        step(c_top, dve.tensor_reduce(sm[:, 23, :], lg[:, 0, :, :], AX, ALU.min))
                        if best == 0:
                            step(c_top, dve.tensor_tensor(lg[:, 4, :, :], io, col(sm[:, 23, :], EX), ALU.is_equal))
                            step(c_top, dve.scalar_tensor_tensor(lg[:, 6, :, :], lg[:, 4, :, :], -2.0, lg[:, 3, :, :],
                                                                 ALU.mult, ALU.add))
                        else:
                            dve.tensor_tensor(lg[:, 7, :, :], io, col(sm[:, 23, :], EX), ALU.is_equal).then_inc(c_w2, 1)
                    step(c_top, dve.tensor_tensor(sm[:, 20, :], sm[:, 8, :], sm[:, 9, :], ALU.add))
                    dve.wait_ge(c_w2, 2 * i + 1)
                    dve.tensor_tensor(lg[:, 7, :, :], lg[:, 7, :, :], lg[:, 4, :, :], ALU.add).then_inc(c_w2, 1)
                    dve.wait_ge(c_w2, 2 * i + 2)
                    step(c_top, dve.tensor_scalar(sm[:, 20, :], sm[:, 20, :], 1e-12, None, ALU.max))
                    step(c_top, dve.reciprocal(sm[:, 21, :], sm[:, 20, :]))
                    step(c_top, dve.tensor_tensor(lg[:, 7, :, :], lg[:, 7, :, :], lg[:, 3, :, :], ALU.mult))
                    dve.tensor_tensor(lg[:, 5, :, :], lg[:, 7, :, :], col(sm[:, 21, :], EX), ALU.mult).then_inc(c_w, 1)
                    dve.wait_ge(c_b2, i + 1)
                    dve.wait_ge(c_u, 2 * i + 2)
                    dve.tensor_tensor(acc[:, :, :], acc[:, :, :], xn[:, :, :], ALU.add).then_inc(c_x3, 1)
                    dve.wait_ge(c_x3, 5 * i + 4)
                    dve.tensor_tensor(acc[:, :, :], acc[:, :, :], bank2(5), ALU.add).then_inc(c_x3, 1)
                    dve.wait_ge(c_x3, 5 * i + 5)
                    for e in range(EX):
                        dve.wait_ge(c_Y, EX * i + e + 1)
                        for u in range(2):
                            if e:
                                dve.wait_ge(c_acc, 2 * (EX * i + e) - 1 + u)
                            dve.scalar_tensor_tensor(acc[:, u, :], bank2(4 + e % 2)[:, u, :], lg[:, 5, u, e:e + 1],
                                                     acc[:, u, :], ALU.mult, ALU.add).then_inc(c_acc, 1)
                    assert chain == per, chain.values()


_INS = ['x', 'src', 'dst', 'L0_gnn_W_left', 'L0_gnn_b_left', 'L0_gnn_W_right', 'L0_mix_w_qkv', 'L0_mix_w_out',
        'L0_mix_b_out', 'L0_ffn_Wr', 'L0_ffn_br', 'L0_ffn_W1', 'L0_ffn_b1', 'L0_ffn_g1', 'L0_ffn_be1', 'L0_ffn_m1',
        'L0_ffn_v1', 'L0_ffn_W2', 'L0_ffn_b2', 'L0_ffn_g2', 'L0_ffn_be2', 'L0_ffn_m2', 'L0_ffn_v2', 'L0_ffn_Wo',
        'L0_ffn_bo', 'L1_gnn_W', 'L1_gnn_b', 'L1_gnn_mag_w', 'L1_gnn_mag_b', 'L1_gnn_attn_w', 'L1_mix_W_qkv',
        'L1_mix_W_out', 'L1_mix_b_out', 'L1_ffn_router_w', 'L1_ffn_w1', 'L1_ffn_b1', 'L1_ffn_w2', 'L1_ffn_b2']


def kernel(**inputs):
    import numpy as _np
    import concourse.bacc as _bacc
    from concourse import mybir as _mybir
    from concourse.bass_utils import run_bass_kernel_spmd as _run

    nc = _bacc.Bacc("TRN2", target_bir_lowering=False, num_devices=1)
    arrays, aps = {}, {}
    for name in _INS:
        arr = _np.ascontiguousarray(inputs[name])
        arrays[f"in_{name}"] = arr
        aps[name] = nc.dram_tensor(f"in_{name}", arr.shape, _mybir.dt.from_np(arr.dtype), kind="ExternalInput").ap()
    out = nc.dram_tensor("out_0", (N, D), F32, kind="ExternalOutput").ap()
    gps_kernel(nc, aps, out)
    r = _run(nc, [arrays], core_ids=[0])
    return r.results[0]["out_0"]
```

```python
from contextlib import ExitStack

import concourse.bass as bass
from concourse import mybir

F32 = mybir.dt.float32
F16 = mybir.dt.float16
I32 = mybir.dt.int32
ALU = mybir.AluOpType
ACT = mybir.ActivationFunctionType
AX = mybir.AxisListType.X

P = 128
N = 6250
E = 106250
D = 256
KD = D // P
T = 125
NT = N // T
PAIRS = NT // 2
TP = 2 * T
CH = 18
WIN = CH * P
SWEEP_CH = 17
SWEEP = SWEEP_CH * T
SWEEPS = E // SWEEP
SAMPLE = 10
EX = 8
HEADS0 = 8
HD0 = 64
KV0 = 2 * HEADS0 * HD0
HEADS1 = 4
HD1 = 32
HID1 = HEADS1 * HD1
ROW1 = D + 2
LN_EPS = 1e-5
BN_EPS = 1e-3
MAX_NORM = 0.95
FAR = 9.0


def col(ap, n):
    return ap.unsqueeze(2).to_broadcast([ap.shape[0], ap.shape[1], n])


def mid(ap, n):
    return ap.unsqueeze(1).to_broadcast([ap.shape[0], n, ap.shape[1]])


ROOT_STEPS = 11


def inverse_root(dve, step, y, x, t):
    step(dve.tensor_scalar(t.bitcast(I32), x.bitcast(I32), 1, None, ALU.logical_shift_right))
    step(dve.tensor_scalar(y.bitcast(I32), t.bitcast(I32), -1.0, float(0x5F3759DF), ALU.mult, ALU.add))
    for _ in range(3):
        step(dve.tensor_tensor(t, y, y, ALU.mult))
        step(dve.scalar_tensor_tensor(t, t, -0.5, x, ALU.mult, ALU.mult))
        step(dve.scalar_tensor_tensor(y, t, 1.5, y, ALU.add, ALU.mult))


def gps_kernel(nc, a, out):
    ctx = ExitStack()
    with ctx:
        def sb(name, shape, dt=F32):
            return ctx.enter_context(nc.sbuf_tensor(name, shape, dt))

        def sem(name):
            return ctx.enter_context(nc.semaphore(name))

        def again(semaphore):
            reused.append(semaphore)
            return semaphore
        reused = []

        ctx.enter_context(nc.allow_non_contiguous_dma(reason="columns of small vectors"))

        xtab = nc.dram_tensor("xtab", (N, 2 * D), F16).ap()
        xnT_d = nc.dram_tensor("xnT_d", (P, KD, N), F32).ap()
        xn2T_d = nc.dram_tensor("xn2T_d", (P, KD, N), F32).ap()
        x2_d = nc.dram_tensor("x2_d", (N, D), F32).ap()
        htab = nc.dram_tensor("htab", (N, ROW1), F32).ap()
        hbase_d = nc.dram_tensor("hbase_d", (N, D), F32).ap()
        nslow_d = nc.dram_tensor("nslow_d", (N, D), F32).ap()

        def pair_rows(t, i):
            return t[bass.ds(i * TP, TP), :].rearrange("(u p) d -> p u d", u=2)

        W1 = sb("W1", [P, EX, KD, D])
        W2 = sb("W2", [P, EX, KD, D])
        Wo = sb("Wo", [P, EX, KD, D])
        kT_all = sb("kT_all", [P, N])
        v_all = sb("v_all", [T, NT, HID1])
        ring = sb("ring", [P, 2, CH, ROW1])
        ring16 = ring[:, :, :, :].rearrange("p u c d -> p (u c d)").bitcast(F16)\
            .rearrange("p (u c d) -> p u c d", u=2, c=CH)
        hot = sb("hot", [P, 2, CH, T], F16)
        big = kT_all[:, 0:2 * CH * T].rearrange("p (u c d) -> p u c d", u=2, c=CH)
        srcw = sb("srcw", [P, NT * CH], I32)
        relw = sb("relw", [P, NT * CH])
        idx = sb("idx", [P, 2, CH], I32)
        ident = sb("ident", [P, P])
        ones = sb("ones", [P, P])
        ones16 = sb("ones16", [P, 1], F16)
        zeros = sb("zeros", [P, 512])
        iota = sb("iota", [P, T])
        thr = sb("thr", [P, NT])
        cols = sb("cols", [P, 448])
        bn = sb("bn", [P, 2, 2, 2 * EX])
        wg = sb("wg", [P, KD, D])
        wg3 = sb("wg3", [P, KD, 3])
        c3 = sb("c3", [T, 3])
        hbound = sb("hbound", [P, 1])
        nbound = sb("nbound", [P, 1])
        Wr = sb("Wr", [P, KD, EX])
        br = sb("br", [T, EX])
        bo = sb("bo", [EX, D])
        b2 = sb("b2", [EX, D])
        bias0 = sb("bias0", [T, D])
        gb = sb("gb", [T, D])
        late = sb("late", [P, 2 * D])
        bias1 = late[0:T, D:2 * D]
        bl = sb("bl", [T, D])
        WL = sb("WL", [P, 2 * KD, D])
        M1 = sb("M1", [P, KD, D])
        wqkv1 = sb("wqkv1", [P, KD, 3 * HID1])
        wout1 = late[:, 0:D]
        flag = sb("flag", [1, 1], I32)
        ht_all = sb("ht_all", [T, NT])
        iota8 = sb("iota8", [T, EX])
        fl = sb("fl", [P, 4])
        lay = sb("lay", [P, 512])
        nothing = sb("nothing", [1, 96])
        xin = sb("xin", [T, 2, D])
        xT = sb("xT", [P, KD, TP])
        base = sb("base", [T, 2, D])
        st = sb("st", [T, 2, 6])
        mv = sb("mv", [T, 2, 2])
        rs = sb("rs", [T, 2])
        nb = sb("nb", [T, 2])
        xn = sb("xn", [T, 2, D])
        acc = sb("acc", [T, 2, D])
        uT = sb("uT", [P, KD, TP])
        h1 = sb("h1", [P, KD, TP])
        h2 = sb("h2", [P, KD, TP])
        tmp = sb("tmp", [T, 2, D])
        hn = sb("hn", [T, 2, D])
        hnT = sb("hnT", [P, KD, TP])
        sm = sb("sm", [T, 24, 2])
        lg = sb("lg", [T, 8, 2, EX])
        wT = sb("wT", [EX, TP])
        hrow = sb("hrow", [T, 2, ROW1])
        ps = [ctx.enter_context(nc.psum_tensor(f"ps{i}", [P, 512], F32)) for i in range(8)]

        f1 = W1[:, :, :, :].rearrange("p e k d -> p (e k d)")
        f2 = W2[:, :, :, :].rearrange("p e k d -> p (e k d)")
        wqkv0 = f1[:, 0:12 * D].rearrange("p (r d) -> p r d", r=12)
        wout0 = f2[:, 0:2 * 512].rearrange("p (r d) -> p r d", r=2)
        woutT = f2[:, 1024:1024 + 4 * D].rearrange("p (r d) -> p r d", r=4)
        wkvT = f2[:, 2048:2048 + 2 * KV0].rearrange("p (k d) -> p k d", k=KD)
        gnnW = f1[:, 3072:3072 + 2 * D].rearrange("p (r d) -> p r d", r=2)

        setup_loads = []
        uses = []
        load_setup = sem("load_setup")
        load_edges = sem("load_edges")
        load_experts0 = sem("load_experts0")
        load_experts1 = sem("load_experts1")

        rows = kT_all[0:80, 0:2 * P].rearrange("p (l d) -> p l d", l=2)
        rows_b1 = kT_all[0:16, 256:256 + P]
        rwrow = kT_all[0:EX, 384:384 + D]
        acol = kT_all[:, 640:644].rearrange("p (s t) -> p s t", s=2)
        bcol = kT_all[:, 644:646]
        asq = kT_all[:, 646:648]
        asum = kT_all[:, 648:649]
        bfull = kT_all[:, 656:656 + 2 * T].rearrange("p (t n) -> p t n", t=2)
        magb = kT_all[0:T, 910:911]
        wright = kT_all[:, 1024:1024 + 2 * D].rearrange("p (k d) -> p k d", k=KD)
        wmean = kT_all[:, 1600:1632]
        bnt = kT_all[:, 1664:1664 + 64].rearrange("p (l v n) -> p l v n", l=2, v=2)
        dst_all = v_all[:, :, :].rearrange("p t d -> p (t d)")[:, 0:850].bitcast(I32)
        dstf = v_all[:, :, :].rearrange("p t d -> p (t d)")[:, 900:985]
        cnt = v_all[:, :, :].rearrange("p t d -> p (t d)")[:, 1000:1050]
        startf = v_all[:, :, :].rearrange("p t d -> p (t d)")[0:1, 1100:1150]
        starti = v_all[:, :, :].rearrange("p t d -> p (t d)")[0:1, 1200:1250].bitcast(I32)
        dstw = ring[:, 0, :, :].rearrange("p c d -> p (c d)")[:, 0:NT * CH].bitcast(I32)
        ge = ring[:, 0, :, :].rearrange("p c d -> p (c d)")[:, 1000:1000 + NT * CH]
        lt = ring[:, 0, :, :].rearrange("p c d -> p (c d)")[:, 2000:2000 + NT * CH]
        cmp = ring[0:T, :, :, :].rearrange("p u c d -> p (u c d)")[:, 0:NT * 85]\
            .rearrange("p (t s) -> p t s", t=NT)

        turns = []
        for k in range(KD):
            for g in range(2):
                turns.append((wkvT[:, k, 512 * g:512 * g + 512],
                              [(wqkv0[:, 4 + 4 * g + r, k * P:k * P + P], P) for r in range(4)]))
        for g in range(2):
            turns.append((woutT[:, 2 * g:2 * g + 2, :].rearrange("p r d -> p (r d)"),
                          [(wout0[:, o, (2 * g + q) * P:(2 * g + q) * P + P], P) for q in range(2) for o in range(2)]))
        turns.append((wg[:, :, :].rearrange("p k d -> p (k d)"),
                      [(gnnW[:, o, k * P:k * P + P], P) for k in range(KD) for o in range(2)]))
        turns.append((cols[:, :],
                      [(wqkv1[:, 0, 0:P], P), (wqkv1[:, 1, 0:P], P)]
                      + [(rwrow[:, k * P:k * P + P], EX) for k in range(KD)]
                      + [(rows[:, l, :], 80) for l in range(2)] + [(rows_b1, 16)]))
        wq1T = cols[:, 0:2 * P].rearrange("p (k i) -> p k i", k=KD)
        rwT = cols[:, 256:272].rearrange("p (k e) -> p k e", k=KD)
        bnc = cols[:, 272:432].rearrange("p (l v n) -> p l v n", l=2, v=5)
        b1c = cols[:, 432:448]

        def carry(engine):
            at = len(uses)
            uses.append(at)
            target = nothing[0:1, 2 + at:3 + at]
            if engine.engine == nc.gpsimd.engine:
                return engine.tensor_tensor(target, nothing[0:1, 0:1], nothing[0:1, 1:2], ALU.add)
            return engine.memset(target, 0.0)

        def wait_apart(engine, semaphore, value):
            engine.wait_ge(semaphore, value)
            return carry(engine)

        made = sem("made")
        zeroed = sem("zeroed")
        turned = sem("turned")
        turned_copied = sem("turned_copied")
        s_dve = sem("setup_dve")
        s_count = sem("setup_counted")
        s_start = sem("setup_starts")
        s_a = sem("setup_through_w")
        s_norm = sem("setup_before_summed")
        s_match = sem("setup_matches")
        windows = sem("windows_loaded")
        nslow_zero = sem("nslow_zero")

        with nc.Block() as block:
            @block.sync
            def _(sp):
                sp.dma_start(dst_all, a["dst"].rearrange("(p n) -> p n", p=T)).then_inc(load_edges, 16)

                def put(dst, src):
                    sp.dma_start(dst, src).then_inc(load_setup, 16)
                    put.n += 1
                put.n = 0
                put(wqkv0, a["L0_mix_w_qkv"].rearrange("(r p) d -> p r d", p=P))
                put(wout0, a["L0_mix_w_out"].rearrange("(r p) d -> p r d", p=P))
                put(gnnW, a["L1_gnn_W"].rearrange("(r p) d -> p r d", p=P))
                put(wqkv1[:, :, :], a["L1_mix_W_qkv"].rearrange("(k p) d -> p k d", p=P))
                put(rwrow, a["L1_ffn_router_w"])
                for l, names in enumerate((("g1", "b1", "be1", "m1", "v1"), ("g2", "b2", "be2", "m2", "v2"))):
                    for v, name in enumerate(names):
                        put(rows[16 * v:16 * v + 16, l, :], a["L0_ffn_" + name].rearrange("e (k p) -> (e k) p", p=P))
                put(rows_b1, a["L1_ffn_b1"].rearrange("e (k p) -> (e k) p", p=P))
                put(acol, a["L1_gnn_attn_w"].rearrange("o (s t p) -> p (o s) t", s=2, p=P))
                put(bcol, a["L1_gnn_b"].rearrange("(t p) -> p t", p=P))
                put(magb, a["L1_gnn_mag_b"].rearrange("(o n) -> o n", o=1).to_broadcast([T, 1]))
                put(wg3[:, :, 0:1], a["L1_gnn_mag_w"].rearrange("o (k p) -> p k o", p=P))
                put(WL[:, :, :], a["L0_gnn_W_left"].rearrange("(k p) d -> p k d", p=P))
                put(wright, a["L0_gnn_W_right"].rearrange("(k p) d -> p k d", p=P))
                put(Wr[:, :, :], a["L0_ffn_Wr"].rearrange("(k p) e -> p k e", p=P))
                put(bo[:, :], a["L0_ffn_bo"])
                put(b2[:, :], a["L1_ffn_b2"])

                def row(t, name, n):
                    put(t[:, :], a[name].rearrange("(o n) -> o n", o=1).to_broadcast([T, n]))
                row(br, "L0_ffn_br", EX)
                row(bl, "L0_gnn_b_left", D)
                row(bias0, "L0_mix_b_out", D)
                row(gb, "L1_gnn_b", D)
                setup_loads.append(put.n)
                sp.dma_start(Wo[:, :, :, :], a["L0_ffn_Wo"].rearrange("e (k p) d -> p e k d", p=P)).then_inc(load_experts0, 16)
                sp.wait_ge(zeroed, 1)
                for k in range(PAIRS):
                    sp.dma_start(nslow_d[k * TP:k * TP + TP, :].rearrange("(u p) d -> p u d", u=2), zeros[0:T, :].rearrange("p (u d) -> p u d", u=2))\
                        .then_inc(nslow_zero, 16)
                sp.wait_ge(s_start, 1)
                with sp.Fori(0, NT) as t:
                    start = sp.value_load(starti[0:1, bass.ds(t, 1)], min_val=0, max_val=E - WIN)
                    sp.dma_start(srcw[:, bass.ds(t * CH, CH)],
                                 a["src"][bass.ds(start, WIN)].rearrange("(p c) -> p c", p=P)).then_inc(windows, 16)
                    sp.dma_start(dstw[:, bass.ds(t * CH, CH)],
                                 a["dst"][bass.ds(start, WIN)].rearrange("(p c) -> p c", p=P)).then_inc(windows, 16)
                sp.wait_ge(nslow_zero, 16 * PAIRS)

            @block.gpsimd
            def _(pool):
                pool.memset(ident[:, :], 0.0).then_inc(made, 1)
                pool.memset(ones[:, :], 1.0).then_inc(made, 1)
                pool.memset(nothing[:, 0:2], 0.0).then_inc(made, 1)
                pool.memset(ones16[:, :], 1.0).then_inc(made, 1)
                pool.memset(hrow[:, :, D:D + 1], 1.0).then_inc(made, 1)
                pool.iota(idx[:, 0, 0:1], pattern=[[0, 1]], base=0, channel_multiplier=0).then_inc(made, 1)
                pool.iota(kT_all[:, 2000:2000 + T].bitcast(I32), pattern=[[1, T]], base=0, channel_multiplier=0).then_inc(made, 1)
                pool.iota(kT_all[:, 2200:2200 + NT].bitcast(I32), pattern=[[T, NT]], base=0, channel_multiplier=0).then_inc(made, 1)
                pool.wait_ge(made, 8)
                pool.affine_select(out=ident[:, :], in_=ident[:, :], compare_op=ALU.not_equal, fill=1.0,
                                   base=0, pattern=[[-1, P]], channel_multiplier=1).then_inc(made, 1)

            @block.vector
            def _(dve):
                n = [0]

                def step(ins):
                    n[0] += 1
                    ins.then_inc(s_dve, 1)
                    dve.wait_ge(s_dve, n[0])

                dve.memset(zeros[:, :], 0.0).then_inc(zeroed, 1)
                dve.wait_ge(made, 9)
                step(dve.tensor_copy(iota[:, :], kT_all[:, 2000:2000 + T].bitcast(I32)))
                step(dve.tensor_copy(thr[:, :], kT_all[:, 2200:2200 + NT].bitcast(I32)))
                step(dve.tensor_copy(iota8[:, :], iota[0:T, 0:EX]))
                dve.wait_ge(load_edges, 16)
                step(dve.tensor_copy(dstf, dst_all.rearrange("p (n s) -> p n s", s=SAMPLE)[:, :, 0]))
                step(dve.tensor_tensor(cmp, mid(dstf, NT), col(thr[0:T, :], 85), ALU.is_lt))
                dve.tensor_reduce(cnt, cmp, AX, ALU.add).then_inc(s_count, 1)
                dve.wait_ge(s_norm, 1)
                step(dve.tensor_scalar(startf, ps[4][0:1, 0:NT], float(SAMPLE), -float(SAMPLE), ALU.mult, ALU.add))
                step(dve.tensor_scalar(startf, startf, 0.0, float(E - WIN), ALU.max, ALU.min))
                dve.tensor_copy(starti, startf).then_inc(s_start, 1)

                dve.wait_ge(load_setup, 16 * setup_loads[0])
                for g, (target, sources) in enumerate(turns):
                    dve.wait_ge(turned, g + 1)
                    if len(sources) == 4:
                        dve.tensor_copy(target, ps[g % 4][:, :]).then_inc(turned_copied, 1)
                    else:
                        dve.tensor_copy(target, ps[g % 4][:, 0:448]).then_inc(turned_copied, 1)
                dve.wait_ge(turned_copied, len(turns))
                heads = wkvT.rearrange("p k (h d) -> p (k h) d", d=HD0)
                step(dve.tensor_reduce(wmean, heads, AX, ALU.add))
                step(dve.tensor_scalar(wmean, wmean, 1.0 / HD0, None, ALU.mult))
                step(dve.tensor_tensor(heads, heads, col(wmean, HD0), ALU.subtract))
                for l in range(2):
                    g_, b_, be_, m_, v_ = (bnc[:, l, v, :] for v in range(5))
                    step(dve.tensor_scalar(v_, v_, BN_EPS, None, ALU.add))
                    inverse_root(dve, step, bnt[:, l, 0, :], v_, bnt[:, l, 1, :])
                    step(dve.tensor_tensor(bn[:, l, 0, :], bnt[:, l, 0, :], g_, ALU.mult))
                    step(dve.tensor_tensor(bnt[:, l, 1, :], b_, m_, ALU.subtract))
                    step(dve.tensor_tensor(bnt[:, l, 1, :], bnt[:, l, 1, :], bn[:, l, 0, :], ALU.mult))
                    step(dve.tensor_tensor(bn[:, l, 1, :], bnt[:, l, 1, :], be_, ALU.add))
                step(dve.tensor_tensor(bias0[:, :], bias0[:, :], bl[:, :], ALU.add))
                step(dve.tensor_tensor(WL[:, 0:KD, :], WL[:, 0:KD, :], wright, ALU.add))
                step(dve.tensor_tensor(asq, acol[:, 0, :], acol[:, 0, :], ALU.mult))
                step(dve.tensor_reduce(asum, asq, AX, ALU.add))
                dve.tensor_copy(bfull, col(bcol, T)).then_inc(s_count, 1)
                dve.wait_ge(s_a, 1)
                step(dve.tensor_copy(wg3[:, :, 1:3], ps[5][:, 0:4].rearrange("p (k s) -> p k s", k=KD)))
                step(dve.tensor_copy(c3[:, 1:3], ps[5][0:T, 8:10]))
                step(dve.tensor_copy(c3[:, 0:1], magb))
                step(dve.tensor_copy(asum, ps[5][:, 16:17]))
                inverse_root(dve, step, hbound[:, :], asum, asq[:, 0:1])
                step(dve.tensor_tensor(hbound[:, :], hbound[:, :], asum, ALU.mult))
                step(dve.tensor_scalar(hbound[:, :], hbound[:, :], 1.51, 1.0, ALU.mult, ALU.add))
                step(dve.tensor_scalar(nbound[:, :], hbound[:, :], -1.0, None, ALU.mult))
                dve.wait_ge(windows, 32 * NT)
                step(dve.tensor_copy(relw[:, :], dstw))
                rel3 = relw[:, :].rearrange("p (t c) -> p t c", t=NT)
                step(dve.tensor_tensor(rel3, rel3, col(thr[:, :], CH), ALU.subtract))
                step(dve.tensor_scalar(ge, relw[:, :], 0.0, None, ALU.is_ge))
                step(dve.tensor_scalar(lt, relw[:, :], float(T), None, ALU.is_lt))
                step(dve.tensor_tensor(ge, ge, lt, ALU.mult))
                dve.tensor_reduce(fl[:, 0:1], ge, AX, ALU.add).then_inc(s_count, 1)
                dve.wait_ge(s_match, 1)
                step(dve.tensor_scalar(fl[:, 1:2], ps[6][:, 0:1], float(E), None, ALU.not_equal))
                step(dve.tensor_scalar(fl[:, 2:3], fl[:, 1:2], -1.0, 1.0, ALU.mult, ALU.add))
                step(dve.tensor_scalar(relw[:, :], relw[:, :], fl[:, 2:3], fl[:, 1:2], ALU.mult, ALU.subtract))
                step(dve.tensor_copy(flag[:, :], fl[0:1, 1:2]))

            @block.tensor
            def _(pe):
                pe.wait_ge(made, 9)
                pe.wait_ge(s_count, 1)
                pe.matmul(ps[4][0:1, 0:NT], ones[0:T, 0:1], cnt, start=True, stop=True).then_inc(s_norm, 1)
                pe.wait_ge(load_setup, 16 * setup_loads[0])
                for g, (target, sources) in enumerate(turns):
                    if g >= 4:
                        pe.wait_ge(turned_copied, g - 3)
                    at = 0
                    for src, r in sources:
                        last = pe.transpose(ps[g % 4][:, at:at + r], src, ident[0:r, 0:r])
                        at += r
                    last.then_inc(turned, 1)
                pe.wait_ge(s_count, 2)
                for k in range(KD):
                    for o in range(2):
                        pe.matmul(ps[5][:, 2 * k:2 * k + 2], gnnW[:, o, k * P:k * P + P], acol[:, :, o],
                                  start=(o == 0), stop=(o == 1))
                for o in range(2):
                    pe.matmul(ps[5][0:T, 8:10], bfull[:, o, :], acol[:, :, o], start=(o == 0), stop=(o == 1))
                pe.matmul(ps[5][:, 16:17], ones[:, :], asum, start=True, stop=True).then_inc(s_a, 1)
                pe.wait_ge(s_count, 3)
                pe.matmul(ps[6][:, 0:1], ones[:, :], fl[:, 0:1], start=True, stop=True).then_inc(s_match, 1)

        sq = big[0:T, :, :, :].rearrange("p u c d -> p u (c d)")[:, :, 0:KV0]
        kc = ring[0:T, 0, :, :].rearrange("p c d -> p (c d)")[:, 0:1024].rearrange("p (u d) -> p u d", u=2)
        vc = ring[0:T, 0, :, :].rearrange("p c d -> p (c d)")[:, 1024:2048].rearrange("p (u d) -> p u d", u=2)
        x16 = ring[0:T, 1, :, :].rearrange("p c d -> p (c d)")[:, 0:512].bitcast(F16)\
            .rearrange("p (u d) -> p u d", u=2)
        rk = ring[0:T, 1, :, :].rearrange("p c d -> p (c d)")[:, 600:640].rearrange("p (u d) -> p u d", u=2)
        rk8, rk8y, rk8t = (ring[0:T, 1, :, :].rearrange("p c d -> p (c d)")[:, n:n + 16]
                           .rearrange("p (u d) -> p u d", u=2) for n in (700, 716, 732))
        xTp = [xT[:, :, 0:T], xT[:, :, T:TP]]

        a_load = [sem("a_x_loaded_0"), sem("a_x_loaded_1")]
        a_norm = sem("a_stats_mean")
        a_root = sem("a_root_steps")
        a_nb = sem("a_shift")
        a_xn = sem("a_xn")
        a_hi = sem("a_hi")
        a_lo = sem("a_lo")
        a_tab = sem("a_table_stored")
        a_tr = sem("a_turned")
        a_xT = sem("a_xT")
        a_xTs = sem("a_xT_stored")
        a_kv = sem("a_kv")
        a_k = sem("a_k_copied")
        a_sq = sem("a_squares")
        a_ms = sem("a_mean_squares")
        a_r = sem("a_kv_var_product")
        a_v = sem("a_v_scaled")
        a_dots = sem("a_dots")

        with nc.Block() as block:
            @block.sync
            def _(sp):
                with sp.Fori(0, PAIRS) as i:
                    for u in range(2):
                        t = i * 2 + u
                        sp.wait_ge(made, 1)
                        sp.wait_ge(a_xn, t - u)
                        sp.dma_start(xin[:, u, :], a["x"][bass.ds(t * T, T), :]).then_inc(a_load[u], 16)
                    for u in range(2):
                        t = i * 2 + u
                        sp.wait_ge(made, 1)
                        sp.wait_ge(a_lo, t + 1)
                        sp.wait_ge(a_hi, t + 1)
                        sp.dma_start(xtab[bass.ds(t * T, T), :], x16[:, u, :]).then_inc(a_tab, 16)
                        sp.wait_ge(made, 1)
                        sp.wait_ge(a_xT, t + 1)
                        sp.dma_start(xnT_d[:, :, bass.ds(t * T, T)], xTp[u]).then_inc(a_xTs, 16)
                sp.wait_ge(a_tab, 16 * NT)
                sp.wait_ge(a_xTs, 16 * NT)

            @block.scalar
            def _(act):
                with act.Fori(0, PAIRS) as i:
                    for u in range(2):
                        t = i * 2 + u
                        act.wait_ge(a_nb, i + 1)
                        act.wait_ge(a_lo, t - u)
                        act.wait_ge(a_tr, t - u)
                        act.activation(xn[:, u, :], xin[:, u, :], ACT.Identity, bias=nb[:, u:u + 1],
                                       scale=rs[:, u:u + 1]).then_inc(a_xn, 1)
                        act.wait_ge(a_tab, 16 * (t - u))
                        act.wait_ge(a_xn, t + 1)
                        act.copy(x16[:, u, 0:D], xn[:, u, :]).then_inc(a_hi, 1)
                    for u in range(2):
                        t = i * 2 + u
                        act.wait_ge(a_kv, t + 1)
                        act.wait_ge(a_ms, t - u)
                        act.activation(sq[:, u, 0:512], ps[2 * u][0:T, :], ACT.Square).then_inc(a_sq, 1)
                        act.activation(sq[:, u, 512:1024], ps[2 * u + 1][0:T, :], ACT.Square).then_inc(a_sq, 1)
                        act.wait_ge(a_dots, t - u)
                        act.copy(kc[:, u, :], ps[2 * u][0:T, :]).then_inc(a_k, 1)

            @block.gpsimd
            def _(pool):
                with pool.Fori(0, PAIRS) as i:
                    for u in range(2):
                        t = i * 2 + u
                        pool.wait_ge(a_hi, t + 1)
                        pool.tensor_tensor(x16[:, u, D:2 * D], xn[:, u, :], x16[:, u, 0:D], ALU.subtract)\
                            .then_inc(a_lo, 1)

            @block.vector
            def _(dve):
                with dve.Fori(0, PAIRS) as i:
                    done = [0]

                    def step(ins):
                        done[0] += 1
                        ins.then_inc(a_root, 1)
                        dve.wait_ge(a_root, (2 * ROOT_STEPS + 1) * i + done[0])

                    for u in range(2):
                        dve.wait_ge(a_load[u], 16 * (i + 1))
                        dve.bn_stats(st[:, u, :], xin[:, u, :]).then_inc(a_norm, 1)
                    wait_apart(dve, a_norm, 4 * i + 2)
                    for u in range(2):
                        dve.bn_aggr(mv[:, u, :], st[:, u, :]).then_inc(a_norm, 1)
                    dve.wait_ge(a_norm, 4 * i + 4)
                    dve.wait_ge(a_xn, 2 * i)
                    step(dve.tensor_scalar(sm[:, 14, :], mv[:, :, 1], LN_EPS, None, ALU.add))
                    inverse_root(dve, step, rs[:, :], sm[:, 14, :], sm[:, 15, :])
                    dve.scalar_tensor_tensor(nb[:, :], mv[:, :, 0], -1.0, rs[:, :], ALU.mult, ALU.mult)\
                        .then_inc(a_nb, 1)
                    for u in range(2):
                        t = i * 2 + u
                        dve.wait_ge(a_tr, t + 1)
                        dve.wait_ge(a_xTs, 16 * (t - u))
                        dve.wait_ge(a_kv, t - u)
                        dve.tensor_copy(xTp[u], ps[4 + u][:, 0:2 * T].rearrange("p (k n) -> p k n", k=KD))\
                            .then_inc(a_xT, 1)
                    for u in range(2):
                        dve.wait_ge(a_sq, 4 * i + 2 * u + 2)
                        dve.tensor_reduce(rk[:, u, 0:16], sq[:, u, :].rearrange("p (h d) -> p h d", d=HD0),
                                          AX, ALU.add).then_inc(a_ms, 1)
                    dve.wait_ge(a_ms, 2 * i + 2)
                    dve.tensor_scalar(rk[:, :, 0:16], rk[:, :, 0:16], 1.0 / HD0, LN_EPS, ALU.mult, ALU.add)\
                        .then_inc(a_r, 1)
                    dve.wait_ge(a_r, 2 * i + 1)
                    dve.tensor_tensor(rk8, rk[:, :, 0:8], rk[:, :, 8:16], ALU.mult).then_inc(a_r, 1)
                    dve.wait_ge(a_r, 2 * i + 2)
                    inverse_root(dve, step, rk8y, rk8, rk8t)
                    dve.wait_ge(a_dots, 2 * i)
                    for u in range(2):
                        dve.tensor_tensor(vc[:, u, :].rearrange("p (h d) -> p h d", d=HD0),
                                          ps[2 * u + 1][0:T, :].rearrange("p (h d) -> p h d", d=HD0),
                                          col(rk8y[:, u, :], HD0), ALU.mult).then_inc(a_v, 1)

            @block.tensor
            def _(pe):
                pe.matmul(ps[6][:, :], zeros[:, 0:P], zeros[:, :], start=True, stop=False,
                          skip_group_check=True)
                with pe.Fori(0, PAIRS) as i:
                    for u in range(2):
                        t = i * 2 + u
                        pe.wait_ge(a_xn, t + 1)
                        pe.wait_ge(a_xT, t - u)
                        for k in range(KD):
                            last = pe.transpose(ps[4 + u][:, k * T:k * T + T], xn[:, u, k * P:k * P + P],
                                                ident[0:T, 0:T])
                        last.then_inc(a_tr, 1)
                    for u in range(2):
                        t = i * 2 + u
                        pe.wait_ge(a_xT, t + 1)
                        pe.wait_ge(a_k, t - u)
                        pe.wait_ge(a_v, t - u)
                        for half in range(2):
                            for k in range(KD):
                                last = pe.matmul(ps[2 * u + half][0:T, :], xTp[u][:, k, :],
                                                 wkvT[:, k, 512 * half:512 * half + 512],
                                                 start=(k == 0), stop=(k == KD - 1))
                        last.then_inc(a_kv, 1)
                    for u in range(2):
                        t = i * 2 + u
                        pe.wait_ge(a_k, t + 1)
                        pe.wait_ge(a_v, t + 1)
                        for q in range(4):
                            last = pe.matmul(ps[6][:, q * P:q * P + P], vc[:, u, q * P:q * P + P],
                                             kc[:, u, q * P:q * P + P], start=False, stop=False,
                                             skip_group_check=True)
                        last.then_inc(a_dots, 1)

        dsb = ring[:, 0, :, :].rearrange("p c d -> p (c d)")[:, 0:512].rearrange("p (q d) -> p q d", q=4)
        gsb = ring[:, 0, :, :].rearrange("p c d -> p (c d)")[:, 512:1536].rearrange("p (q d) -> p q d", q=4)
        f_copied = sem("f_copied")
        f_product = sem("f_product")
        with nc.Block() as block:
            @block.vector
            def _(dve):
                dve.memset(dsb, 0.0).then_inc(f_copied, 1)
                dve.wait_ge(f_copied, 1)
                for h in range(2):
                    r = slice(HD0 * h, HD0 * h + HD0)
                    dve.tensor_scalar(dsb[r, :, r], ps[6][r, :].rearrange("p (q d) -> p q d", q=4)[:, :, r],
                                      1.0 / N, None, ALU.mult).then_inc(f_copied, 1)
                dve.wait_ge(f_product, 1)
                for g in range(2):
                    dve.tensor_copy(gsb[:, 2 * g:2 * g + 2, :].rearrange("p q d -> p (q d)"), ps[g][:, :])\
                        .then_inc(f_copied, 1)
                dve.wait_ge(f_product, 2)
                dve.tensor_tensor(WL[:, 0:KD, :], WL[:, 0:KD, :], ps[2][:, :].rearrange("p (k d) -> p k d", k=KD),
                                  ALU.add).then_inc(f_copied, 1)

            @block.tensor
            def _(pe):
                pe.wait_ge(f_copied, 3)
                for q in range(4):
                    last = pe.matmul(ps[q // 2][:, (q % 2) * D:(q % 2) * D + D], dsb[:, q, :], woutT[:, q, :],
                                     start=True, stop=True)
                last.then_inc(f_product, 1)
                pe.wait_ge(f_copied, 5)
                for k in range(KD):
                    for q in range(4):
                        last = pe.matmul(ps[2][:, k * D:k * D + D], wqkv0[:, q, k * P:k * P + P], gsb[:, q, :],
                                         start=(q == 0), stop=(q == 3))
                last.then_inc(f_product, 1)

            @block.sync
            def _(sp):
                sp.wait_ge(f_product, 2)
                for w, name in ((W1, "L0_ffn_W1"), (W2, "L0_ffn_W2")):
                    sp.dma_start(w[:, :, :, :], a[name].rearrange("e (k p) d -> p e k d", p=P))\
                        .then_inc(load_experts0, 16)

        g_seen = sem("g_edges_seen")
        g_load = sem("g_edges_loaded")
        g_rows = sem("g_rows_gathered")
        g_sums = sem("g_sums")
        g_dve = sem("g_vector_steps")
        g_out = sem("g_mean_stored")
        sweep_e = sb("sweep_e", [T, 2, SWEEP_CH], I32)
        sweep_r = sb("sweep_r", [T, SWEEP_CH])
        G_CLEAR, G_STEP, G_END = 2, 4, 4
        G_TILE = G_CLEAR + SWEEPS * G_STEP + G_END

        def sweep_loads(sp, w, load):
            sp.dma_start(sweep_e[:, 0, :], a["src"][bass.ds(w * SWEEP, SWEEP)].rearrange("(p c) -> p c", p=T))\
                .then_inc(load, 16)
            sp.dma_start(sweep_e[:, 1, :], a["dst"][bass.ds(w * SWEEP, SWEEP)].rearrange("(p c) -> p c", p=T))\
                .then_inc(load, 16)

        def flagged(engine):
            return engine.If(engine.value_load(flag[0:1, 0:1], min_val=0, max_val=1) != 0)

        with nc.Block() as block:
            @block.sync
            def _(sp):
                with flagged(sp):
                    with sp.Fori(0, NT) as t:
                        with sp.Fori(0, SWEEPS) as w:
                            sp.wait_ge(made, 1)
                            sp.wait_ge(g_sums, t * SWEEPS + w)
                            sweep_loads(sp, w, g_load)
                        sp.wait_ge(made, 1)
                        sp.wait_ge(g_dve, G_TILE * (t + 1))
                        sp.dma_start(nslow_d[bass.ds(t * T, T), :], hn[:, 0, :]).then_inc(g_out, 16)
                    sp.wait_ge(g_out, 16 * NT)

            @block.gpsimd
            def _(pool):
                with flagged(pool):
                    with pool.Fori(0, NT) as t:
                        with pool.Fori(0, SWEEPS) as w:
                            n = t * SWEEPS + w
                            pool.wait_ge(g_seen, 2 * n)
                            wait_apart(pool, g_load, 32 * (n + 1)).then_inc(g_seen, 1)
                            for c in range(SWEEP_CH):
                                pool.indirect_dma_start(
                                    ring16[0:T, 0, c, 0:2 * D], None, xtab,
                                    bass.IndirectOffsetOnAxis(ap=sweep_e[:, 0, c:c + 1], axis=0)).then_inc(g_rows, 16)
                            wait_apart(pool, g_sums, n + 1).then_inc(g_seen, 1)
                            wait_apart(pool, g_seen, 2 * n + 2)
                            pool.inc_swdge_sem([g_rows], [16 * SWEEP_CH], mode="sub")

            @block.vector
            def _(dve):
                with flagged(dve):
                    with dve.Fori(0, NT) as t:
                        done = [0]

                        def step(ins, before=t * G_TILE):
                            done[0] += 1
                            ins.then_inc(g_dve, 1)
                            dve.wait_ge(g_dve, before + done[0])

                        step(dve.memset(tmp[:, :, :], 0.0))
                        step(dve.memset(sm[:, 0, :], 0.0))
                        assert done[0] == G_CLEAR
                        carry(dve)
                        with dve.Fori(0, SWEEPS) as w:
                            done[0] = 0
                            n = t * SWEEPS + w
                            before = t * G_TILE + G_CLEAR + w * G_STEP
                            dve.wait_ge(g_load, 32 * (n + 1))
                            step(dve.tensor_scalar(sweep_r[:, :], sweep_e[:, 1, :], thr[0:T, bass.ds(t, 1)], None,
                                                   ALU.subtract), before)
                            step(dve.tensor_tensor(hot[0:T, 0, 0:SWEEP_CH, :], col(sweep_r[:, :], T),
                                                   mid(iota[0:T, :], SWEEP_CH), ALU.is_equal), before)
                            dve.wait_ge(g_sums, n + 1)
                            step(dve.tensor_tensor(tmp[:, :, :], tmp[:, :, :],
                                                   ps[0][0:T, :].rearrange("p (u d) -> p u d", u=2), ALU.add), before)
                            step(dve.tensor_tensor(sm[:, 0, 0:1], sm[:, 0, 0:1], ps[7][0:T, 0:1], ALU.add), before)
                            assert done[0] == G_STEP
                        done[0] = 0
                        before = t * G_TILE + G_CLEAR + SWEEPS * G_STEP
                        step(dve.tensor_scalar(sm[:, 1, 0:1], sm[:, 0, 0:1], 1.0, None, ALU.max), before)
                        step(dve.reciprocal(sm[:, 1, 0:1], sm[:, 1, 0:1]), before)
                        step(dve.tensor_tensor(tmp[:, 0, :], tmp[:, 0, :], tmp[:, 1, :], ALU.add), before)
                        dve.wait_ge(g_out, 16 * t)
                        step(dve.tensor_scalar(hn[:, 0, :], tmp[:, 0, :], sm[:, 1, 0:1], None, ALU.mult), before)
                        assert done[0] == G_END

            @block.tensor
            def _(pe):
                with flagged(pe):
                    with pe.Fori(0, NT) as t:
                        with pe.Fori(0, SWEEPS) as w:
                            n = t * SWEEPS + w
                            pe.wait_ge(g_seen, 2 * n + 1)
                            pe.matmul(ps[6][0:1, 0:1], ones16[0:T, :], ones16[0:T, :], start=True, stop=True)
                            pe.wait_ge(g_rows, 16 * SWEEP_CH)
                            pe.wait_ge(g_dve, t * G_TILE + G_CLEAR + w * G_STEP + 2)
                            for c in range(SWEEP_CH):
                                pe.matmul(ps[7][0:T, 0:1], hot[0:T, 0, c, :], ones16[0:T, :],
                                          start=(c == 0), stop=(c == SWEEP_CH - 1))
                            for c in range(SWEEP_CH):
                                last = pe.matmul(ps[0][0:T, :], hot[0:T, 0, c, :], ring16[0:T, 0, c, 0:2 * D],
                                                 start=(c == 0), stop=(c == SWEEP_CH - 1))
                            last.then_inc(g_sums, 1)

        b_x = sem("b_x_loaded")
        b_xT = sem("b_xT_loaded")
        b_base = sem("b_sweep_mean_loaded")
        b_idx = sem("b_idx")
        b_rows = [sem("b_rows_gathered_0"), sem("b_rows_gathered_1")]
        b_hot = sem("b_one_hot")
        b_xb = sem("b_x_bias")
        b_seg = sem("b_segment_sums")
        b_cnt = sem("b_count_reciprocal_steps")
        b_router = sem("b_router_steps")
        b_mag = sem("b_magnitude_steps")
        b_s1 = sem("b_low_mean")
        b_hn = sem("b_neighbour_mean")
        b_hnTp = sem("b_mean_turned")
        b_hnT = sem("b_mean_turned_copied")
        b_lin = sem("b_linear")
        b_x1 = sem("b_x1")
        b_xf = sem("b_x1_expert_biases")
        b_norm = sem("b_x1_norm_steps")
        b_nb = sem("b_x1_shift")
        b_u = sem("b_x1_normalized")
        b_uTp = sem("b_x1_turned")
        b_uT = sem("b_uT")
        b_in = sem("b_experts_input")
        b_lg = sem("b_logits")
        b_zs = sem("b_logits_less_max")
        b_e = sem("b_router_exp")
        b_w = sem("b_router_weights")
        b_wE = sem("b_weights_kept")
        b_wTp = sem("b_weights_turned")
        b_wT = sem("b_weights_turned_copied")
        b_bo = sem("b_expert_biases")
        b_A = sem("b_hidden1_product")
        b_h1 = sem("b_hidden1")
        b_B = sem("b_hidden2_product")
        b_h2 = sem("b_hidden2")
        b_Y = sem("b_expert_out")
        b_acc = sem("b_expert_added")
        b_x2s = sem("b_x2_stored")
        b_normp = sem("b_x2_norm_steps")
        b_nbp = sem("b_x2_shift")
        b_up = sem("b_x2_normalized")
        b_x2Tp = sem("b_x2_turned")
        b_x2T = sem("b_x2T")
        b_x2Ts = sem("b_x2T_stored")
        b_hr = sem("b_h_raw")
        b_kv = sem("b_k_v")
        b_hb = sem("b_h_bias")
        b_ss = sem("b_h_squares")
        b_ext = sem("b_magnitude_and_scores")
        b_me = sem("b_magnitude_exp")
        b_h = sem("b_h")
        b_hs = sem("b_h_stored")
        b_kc = sem("b_k_v_copied")
        x2T = sb("x2T", [P, KD, TP])
        uTf = sb("uTf", [P, KD, TP])
        xf = late[0:T, :].rearrange("p (u d) -> p u d", u=2)
        x2b = M1[0:T, :, :]
        xnp = lay[0:T, :].rearrange("p (u d) -> p u d", u=2)
        tmpp = zeros[0:T, :].rearrange("p (u d) -> p u d", u=2)
        smp = sb("smp", [T, 8, 2])
        stp = sb("stp", [T, 2, 6])
        mvp = sb("mvp", [T, 2, 2])
        wE = sb("wE", [T, 2, EX])
        ext = sb("ext", [T, 2, 3])
        KV_EXT = TP + 2 * HID1
        CNT = 504

        def wait(engine, semaphore, value):
            if not isinstance(value, int) or value > 0:
                engine.wait_ge(semaphore, value)

        def bank2(n):
            return ps[n][0:T, :].rearrange("p (u d) -> p u d", u=2)

        def turned_pair(n):
            return ps[n][:, 0:KD * TP].rearrange("p (k n) -> p k n", k=KD)

        def transpose_pair(pe, bank, src):
            for u in range(2):
                for k in range(KD):
                    last = pe.transpose(ps[bank][:, k * TP + u * T:k * TP + u * T + T],
                                        src[:, u, k * P:k * P + P], ident[0:T, 0:T])
            return last

        LAST = PAIRS - 1

        def pipeline(engine, body):
            body(0, True, False, True)
            with engine.Fori(1, LAST - 1) as j:
                body(j, True, True, True)
            body(LAST - 1, True, True, False)
            body(LAST, False, True, False)

        with nc.Block() as block:
            @block.sync
            def _(sp):
                def load_front(i):
                    wait(sp, made, 1)
                    wait(sp, b_hn, 2 * i)
                    sp.dma_start(base[:, :, :], pair_rows(nslow_d, i)).then_inc(b_base, 16)
                    wait(sp, made, 1)
                    wait(sp, b_xb, i)
                    sp.dma_start(xin[:, :, :], pair_rows(a["x"], i)).then_inc(b_x, 16)
                    wait(sp, made, 1)
                    wait(sp, b_lin, i)
                    sp.dma_start(xT[:, :, :], xnT_d[:, :, bass.ds(i * TP, TP)]).then_inc(b_xT, 16)

                def store_x2(p):
                    wait(sp, made, 1)
                    wait(sp, b_acc, 2 * EX * (p + 1))
                    sp.dma_start(pair_rows(x2_d, p), x2b[:, :, :]).then_inc(b_x2s, 16)
                    wait(sp, made, 1)
                    wait(sp, b_x2T, p + 1)
                    sp.dma_start(xn2T_d[:, :, bass.ds(p * TP, TP)], x2T[:, :, :]).then_inc(b_x2Ts, 16)

                def store_h(p):
                    wait(sp, made, 1)
                    wait(sp, b_h, 3 * (p + 1))
                    sp.dma_start(pair_rows(htab, p), hrow[:, :, :]).then_inc(b_hs, 16)
                    sp.dma_start(pair_rows(hbase_d, p), hrow[:, :, 0:D]).then_inc(b_hs, 16)

                def body(j, front, post, ahead):
                    if post:
                        store_x2(j - 1)
                    if ahead:
                        load_front(j + 2)
                    if post:
                        store_h(j - 1)

                load_front(0)
                load_front(1)
                pipeline(sp, body)
                store_x2(LAST)
                store_h(LAST)
                sp.wait_ge(b_x2s, 16 * PAIRS)
                sp.wait_ge(b_x2Ts, 16 * PAIRS)
                sp.wait_ge(b_hs, 32 * PAIRS)

            @block.gpsimd
            def _(pool):
                def gather(i):
                    for u in range(2):
                        t = i * 2 + u
                        wait(pool, b_seg, t - 1)
                        wait(pool, b_rows[u], 16 * CH * i)
                        pool.tensor_copy(idx[:, u, :], srcw[:, bass.ds(t * CH, CH)]).then_inc(b_idx, 1)
                        wait_apart(pool, b_idx, t + 1)
                        for c in range(CH):
                            pool.indirect_dma_start(
                                ring16[:, u, c, 0:2 * D], None, xtab,
                                bass.IndirectOffsetOnAxis(ap=idx[:, u, c:c + 1], axis=0)).then_inc(b_rows[u], 16)
                gather(0)
                with pool.Fori(1, PAIRS) as i:
                    gather(i)

            @block.tensor
            def _(pe):
                pe.wait_ge(load_experts0, 48)

                def hidden(w, rhs, e, bank, done):
                    for m in range(KD):
                        for k in range(KD):
                            last = pe.matmul(ps[bank][:, m * D:m * D + TP], w[:, e, k, m * P:m * P + P],
                                             rhs[:, k, :], start=(k == 0), stop=(k == KD - 1))
                    last.then_inc(done, 1)

                def segment_sums(i):
                    for u in range(2):
                        t = i * 2 + u
                        wait(pe, b_rows[u], 16 * CH * (i + 1))
                        wait(pe, b_hot, t + 1)
                        wait(pe, b_router, 4 * i)
                        wait(pe, b_xf, i)
                        wait(pe, b_wT, i)
                        for c in range(CH):
                            pe.matmul(ps[u][0:T, :], hot[:, u, c, :], ring16[:, u, c, 0:2 * D],
                                      start=(c == 0), stop=(c == CH - 1))
                        for c in range(CH):
                            last = pe.matmul(ps[7][0:T, CNT + u:CNT + u + 1], hot[:, u, c, :], ones16[:, :],
                                             start=(c == 0), stop=(c == CH - 1))
                        last.then_inc(b_seg, 1)

                def turn_mean(i):
                    wait(pe, b_hn, 2 * i + 2)
                    wait(pe, b_cnt, 2 * i + 1)
                    transpose_pair(pe, 7, hn).then_inc(b_hnTp, 1)

                def linear(i):
                    wait(pe, b_xT, 16 * (i + 1))
                    wait(pe, b_hnT, i + 1)
                    for u in range(2):
                        for k in range(2 * KD):
                            src = xT if k < KD else hnT
                            last = pe.matmul(ps[0][0:T, u * D:u * D + D], src[:, k % KD, u * T:u * T + T],
                                             WL[:, k, :], start=(k == 0), stop=(k == 2 * KD - 1))
                    last.then_inc(b_lin, 1)

                def turn_x1(i):
                    wait(pe, b_u, 2 * i + 2)
                    transpose_pair(pe, 7, xn).then_inc(b_uTp, 1)

                def logits(i):
                    wait(pe, b_uT, i + 1)
                    for u in range(2):
                        for k in range(KD):
                            last = pe.matmul(ps[1][0:T, EX * u:EX * u + EX], uTf[:, k, u * T:u * T + T],
                                             Wr[:, k, :], start=(k == 0), stop=(k == KD - 1))
                    last.then_inc(b_lg, 1)

                def turn_weights(i):
                    wait(pe, b_w, i + 1)
                    for u in range(2):
                        last = pe.transpose(ps[7][0:EX, u * T:u * T + T], lg[:, 5, u, :], ident[0:T, 0:T])
                    last.then_inc(b_wTp, 1)

                def expert_biases(i):
                    wait(pe, b_wT, i + 1)
                    wait(pe, b_x1, i + 1)
                    for u in range(2):
                        last = pe.matmul(ps[0][0:T, u * D:u * D + D], wT[:, u * T:u * T + T], bo[:, :],
                                         start=True, stop=True)
                    last.then_inc(b_bo, 1)

                def turn_x2(p):
                    wait(pe, b_up, 2 * p + 2)
                    wait(pe, b_hb, p)
                    transpose_pair(pe, 6, xnp).then_inc(b_x2Tp, 1)

                def keys_values(p):
                    wait(pe, b_x2T, p + 1)
                    for k in range(KD):
                        pe.matmul(ps[6][:, 0:TP], wqkv1[:, k, HID1:2 * HID1], x2T[:, k, :],
                                  start=(k == 0), stop=(k == KD - 1))
                    for u in range(2):
                        for k in range(KD):
                            pe.matmul(ps[6][0:T, TP + u * HID1:TP + u * HID1 + HID1],
                                      x2T[:, k, u * T:u * T + T], wqkv1[:, k, 2 * HID1:3 * HID1],
                                      start=(k == 0), stop=(k == KD - 1))
                    for u in range(2):
                        for k in range(KD):
                            last = pe.matmul(ps[6][0:T, KV_EXT + 3 * u:KV_EXT + 3 * u + 3],
                                             x2T[:, k, u * T:u * T + T], wg3[:, k, :],
                                             start=(k == 0), stop=(k == KD - 1))
                    last.then_inc(b_kv, 1)

                def raw_h(p):
                    wait(pe, b_ext, p + 1)
                    wait(pe, b_kc, 2 * p + 2)
                    for u in range(2):
                        for k in range(KD):
                            last = pe.matmul(ps[6][0:T, u * D:u * D + D], x2T[:, k, u * T:u * T + T], wg[:, k, :],
                                             start=(k == 0), stop=(k == KD - 1))
                    last.then_inc(b_hr, 1)

                def front_all(i):
                    for stage in (segment_sums, turn_mean, linear, turn_x1, logits, turn_weights, expert_biases):
                        stage(i)

                def body(j, front, post, ahead):
                    fronts = {0: segment_sums, 2: turn_mean, 3: linear, 5: turn_x1, 6: logits, 7: turn_weights,
                              8: expert_biases}
                    posts = {1: turn_x2, 2: keys_values, 4: raw_h}

                    def slot(s):
                        if post and s in posts:
                            posts[s](j - 1)
                        if front and s in fronts:
                            fronts[s](j + 1)

                    wait(pe, b_in, j + 1)
                    wait(pe, b_h1, 2 * EX * j)
                    hidden(W1, uT, 0, 2, b_A)
                    slot(0)
                    for e in range(EX):
                        n = EX * j + e
                        if e + 1 < EX:
                            wait(pe, b_h1, 2 * n + 2)
                            hidden(W1, uT, e + 1, 2, b_A)
                        wait(pe, b_h1, 2 * n + 2)
                        wait(pe, b_h2, 2 * n)
                        hidden(W2, h1, e, 3, b_B)
                        if e:
                            out_of(j, e - 1)
                        slot(e + 1)
                    out_of(j, EX - 1)

                def out_of(j, e):
                    n = EX * j + e
                    wait(pe, b_h2, 2 * n + 2)
                    wait(pe, b_acc, 2 * (n - 1))
                    for u in range(2):
                        for k in range(KD):
                            last = pe.matmul(ps[4 + e % 2][0:T, u * D:u * D + D], h2[:, k, u * T:u * T + T],
                                             Wo[:, e, k, :], start=(k == 0), stop=(k == KD - 1))
                    last.then_inc(b_Y, 1)

                front_all(0)
                pipeline(pe, body)
                for stage in (turn_x2, keys_values, raw_h):
                    stage(LAST)

            @block.scalar
            def _(act):
                def copy_mean(i):
                    wait(act, b_hnTp, i + 1)
                    act.copy(hnT[:, :, :], turned_pair(7)).then_inc(b_hnT, 1)

                def normalize_x1(i):
                    wait(act, b_nb, i + 1)
                    for u in range(2):
                        act.activation(xn[:, u, :], xf[:, u, :], ACT.Identity, bias=nb[:, u:u + 1],
                                       scale=rs[:, u:u + 1]).then_inc(b_u, 1)

                def copy_x1(i):
                    wait(act, b_uTp, i + 1)
                    wait(act, b_in, i)
                    act.copy(uTf[:, :, :], turned_pair(7)).then_inc(b_uT, 1)

                def router_exp(i):
                    wait(act, b_zs, i + 1)
                    act.activation(lg[:, 2, :, :], lg[:, 1, :, :], ACT.Exp).then_inc(b_e, 1)

                def hand_on(i):
                    wait(act, b_uT, i + 1)
                    wait(act, b_lg, i + 1)
                    wait(act, b_A, EX * i)
                    act.copy(uT[:, :, :], uTf[:, :, :]).then_inc(b_in, 1)

                def copy_weights(i):
                    wait(act, b_wTp, i + 1)
                    act.copy(wT[:, :], ps[7][0:EX, 0:TP]).then_inc(b_wT, 1)

                def normalize_x2(p):
                    wait(act, b_nbp, p + 1)
                    for u in range(2):
                        act.activation(xnp[:, u, :], x2b[:, u, :], ACT.Identity, bias=smp[:, 7, u:u + 1],
                                       scale=smp[:, 6, u:u + 1]).then_inc(b_up, 1)

                def copy_x2(p):
                    wait(act, b_x2Tp, p + 1)
                    wait(act, b_x2Ts, 16 * p)
                    act.copy(x2T[:, :, :], turned_pair(6)).then_inc(b_x2T, 1)

                def copy_keys_values(p):
                    wait(act, b_kv, p + 1)
                    act.copy(kT_all[:, bass.ds(p * TP, TP)], ps[6][:, 0:TP]).then_inc(b_kc, 1)
                    act.copy(v_all[:, bass.ds(p * 2, 2), :],
                             ps[6][0:T, TP:TP + 2 * HID1].rearrange("p (u d) -> p u d", u=2)).then_inc(b_kc, 1)

                def magnitude_exp(p):
                    wait(act, b_ext, p + 1)
                    act.activation(smp[:, 0, :], ext[:, :, 0], ACT.Exp, scale=-1.0).then_inc(b_me, 1)

                def relu(j, e, bank, layer, target, product, free, free_at, done):
                    wait(act, product, EX * j + e + 1)
                    wait(act, free, free_at)
                    for m in range(KD):
                        act.activation(target[:, m, :], ps[bank][:, m * D:m * D + TP], ACT.Relu,
                                       bias=bn[:, layer, 1, 2 * e + m:2 * e + m + 1],
                                       scale=bn[:, layer, 0, 2 * e + m:2 * e + m + 1]).then_inc(done, 1)

                def body(j, front, post, ahead):
                    fronts = {2: copy_mean, 4: normalize_x1, 5: copy_x1, 8: copy_weights}
                    posts = {0: normalize_x2, 1: copy_x2, 2: copy_keys_values, 3: magnitude_exp}

                    def slot(s):
                        if post and s in posts:
                            posts[s](j - 1)
                        if front and s in fronts:
                            fronts[s](j + 1)

                    relu(j, 0, 2, 0, h1, b_A, b_B, EX * j, b_h1)
                    slot(0)
                    for e in range(EX):
                        n = EX * j + e
                        if e + 1 < EX:
                            relu(j, e + 1, 2, 0, h1, b_A, b_B, n + 1, b_h1)
                            if e + 1 == EX - 1 and front:
                                router_exp(j + 1)
                                hand_on(j + 1)
                        elif front:
                            copy_weights(j + 1)
                        relu(j, e, 3, 1, h2, b_B, b_Y, n, b_h2)
                        if e + 1 < EX:
                            slot(e + 1)

                copy_mean(0)
                normalize_x1(0)
                copy_x1(0)
                router_exp(0)
                hand_on(0)
                copy_weights(0)
                pipeline(act, body)
                normalize_x2(LAST)
                copy_x2(LAST)
                copy_keys_values(LAST)
                magnitude_exp(LAST)

            @block.vector
            def _(dve):
                NORM_STEPS = 5 + ROOT_STEPS
                POST_STEPS = 5 + 2 * ROOT_STEPS

                def norm(x, s, m, v, w, y, shift, counted, n, free, done):
                    for u in range(2):
                        dve.bn_stats(s[:, u, :], x[:, u, :]).then_inc(counted, 1)
                    wait_apart(dve, counted, n + 2)
                    for u in range(2):
                        dve.bn_aggr(m[:, u, :], s[:, u, :]).then_inc(counted, 1)
                    dve.wait_ge(counted, n + 4)
                    if free is not None:
                        wait(dve, *free)
                    dve.tensor_scalar(v, m[:, :, 1], LN_EPS, None, ALU.add).then_inc(counted, 1)
                    dve.wait_ge(counted, n + 5)
                    steps = [0]

                    def step(ins):
                        steps[0] += 1
                        ins.then_inc(counted, 1)
                        dve.wait_ge(counted, n + 5 + steps[0])
                    inverse_root(dve, step, y, v, w)
                    dve.scalar_tensor_tensor(shift, m[:, :, 0], -1.0, y, ALU.mult, ALU.mult).then_inc(done, 1)

                def one_hot(i):
                    for u in range(2):
                        t = i * 2 + u
                        wait(dve, b_seg, t - 1)
                        dve.tensor_tensor(hot[:, u, :, :], col(relw[:, bass.ds(t * CH, CH)], T),
                                          mid(iota[:, :], CH), ALU.is_equal).then_inc(b_hot, 1)

                def mean(i):
                    wait(dve, b_x, 16 * (i + 1))
                    wait(dve, b_x1, i)
                    dve.tensor_tensor(tmp[:, :, :], xin[:, :, :], mid(bias0[:, :], 2), ALU.add).then_inc(b_xb, 1)
                    wait(dve, b_seg, 2 * i + 2)
                    dve.tensor_scalar(sm[:, 0, :], ps[7][0:T, CNT:CNT + 2], 1.0, None, ALU.max).then_inc(b_cnt, 1)
                    wait(dve, b_cnt, 2 * i + 1)
                    dve.reciprocal(sm[:, 1, :], sm[:, 0, :]).then_inc(b_cnt, 1)
                    wait(dve, b_cnt, 2 * i + 2)
                    wait(dve, b_base, 16 * (i + 1))
                    wait(dve, b_hnTp, i)
                    for u in range(2):
                        dve.scalar_tensor_tensor(base[:, u, :], ps[u][0:T, D:2 * D], sm[:, 1, u:u + 1], base[:, u, :],
                                                 ALU.mult, ALU.add).then_inc(b_s1, 1)
                    for u in range(2):
                        wait(dve, b_s1, 2 * i + u + 1)
                        dve.scalar_tensor_tensor(hn[:, u, :], ps[u][0:T, 0:D], sm[:, 1, u:u + 1], base[:, u, :],
                                                 ALU.mult, ALU.add).then_inc(b_hn, 1)

                def x1(i):
                    wait(dve, b_lin, i + 1)
                    wait(dve, b_xb, i + 1)
                    if not isinstance(i, int) or i > 0:
                        wait(dve, b_acc, 2 * EX * (i - 1) + 2)
                    dve.tensor_tensor(xf[:, :, :], tmp[:, :, :], bank2(0), ALU.add).then_inc(b_x1, 1)
                    wait(dve, b_x1, i + 1)
                    norm(xf, st, mv, sm[:, 14, :], sm[:, 15, :], rs[:, :], nb[:, :], b_norm, NORM_STEPS * i,
                         (b_u, 2 * i), b_nb)

                def router(i):
                    wait(dve, b_lg, i + 1)
                    dve.tensor_tensor(lg[:, 0, :, :], ps[1][0:T, 0:2 * EX].rearrange("p (u e) -> p u e", u=2),
                                      mid(br[:, :], 2), ALU.add).then_inc(b_router, 1)
                    wait(dve, b_router, 4 * i + 1)
                    dve.tensor_reduce(sm[:, 2, :], lg[:, 0, :, :], AX, ALU.max).then_inc(b_router, 1)
                    wait(dve, b_router, 4 * i + 2)
                    dve.tensor_tensor(lg[:, 1, :, :], lg[:, 0, :, :], col(sm[:, 2, :], EX), ALU.subtract)\
                        .then_inc(b_zs, 1)
                    wait(dve, b_e, i + 1)
                    dve.tensor_reduce(sm[:, 3, :], lg[:, 2, :, :], AX, ALU.add).then_inc(b_router, 1)
                    wait(dve, b_router, 4 * i + 3)
                    dve.reciprocal(sm[:, 4, :], sm[:, 3, :]).then_inc(b_router, 1)
                    wait(dve, b_router, 4 * i + 4)
                    wait(dve, b_wE, i)
                    wait(dve, b_wTp, i)
                    dve.tensor_tensor(lg[:, 5, :, :], lg[:, 2, :, :], col(sm[:, 4, :], EX), ALU.mult).then_inc(b_w, 1)

                def add_biases(i):
                    wait(dve, b_bo, i + 1)
                    wait(dve, b_u, 2 * i + 2)
                    dve.tensor_tensor(xf[:, :, :], xf[:, :, :], bank2(0), ALU.add).then_inc(b_xf, 1)

                def keep_weights(j):
                    wait(dve, b_w, j + 1)
                    wait(dve, b_acc, 2 * EX * j)
                    dve.tensor_copy(wE[:, :, :], lg[:, 5, :, :]).then_inc(b_wE, 1)

                def add_expert(j, e, ):
                    n = EX * j + e
                    wait(dve, b_Y, n + 1)
                    if e == 0:
                        wait(dve, b_wE, j + 1)
                        wait(dve, b_xf, j + 1)
                    if e == EX - 1:
                        wait(dve, b_x2s, 16 * j)
                        wait(dve, b_up, 2 * j)
                    source = xf if e == 0 else acc
                    target = x2b if e == EX - 1 else acc
                    for u in range(2):
                        wait(dve, b_acc, 2 * n - 1 + u)
                        dve.scalar_tensor_tensor(target[:, u, :], bank2(4 + e % 2)[:, u, :], wE[:, u, e:e + 1],
                                                 source[:, u, :], ALU.mult, ALU.add).then_inc(b_acc, 1)

                def norm_x2(p):
                    wait(dve, b_acc, 2 * EX * (p + 1))
                    norm(x2b, stp, mvp, smp[:, 4, :], smp[:, 5, :], smp[:, 6, :], smp[:, 7, :], b_normp,
                         POST_STEPS * p, (b_up, 2 * p), b_nbp)

                def extras(p):
                    wait(dve, b_kv, p + 1)
                    wait(dve, b_kc, 2 * p + 2)
                    dve.tensor_tensor(ext[:, :, :], ps[6][0:T, KV_EXT:KV_EXT + 6].rearrange("p (u c) -> p u c", u=2),
                                      mid(c3[:, :], 2), ALU.add).then_inc(b_ext, 1)

                def squares(p):
                    wait(dve, b_hr, p + 1)
                    wait(dve, b_h, 3 * p)
                    dve.tensor_tensor(tmpp[:, :, :], bank2(6), mid(gb[:, :], 2), ALU.add).then_inc(b_hb, 1)
                    wait(dve, b_hb, p + 1)
                    wait(dve, b_x2Tp, p + 1)
                    for u in range(2):
                        dve.tensor_tensor_reduce(xnp[:, u, :], tmpp[:, u, :], tmpp[:, u, :], 1.0, 0.0, ALU.mult,
                                                 ALU.add, smp[:, 1, u:u + 1]).then_inc(b_ss, 1)

                def scaled_h(p):
                    wait(dve, b_ss, 2 * p + 2)
                    steps = [0]

                    def step(ins):
                        steps[0] += 1
                        ins.then_inc(b_normp, 1)
                        dve.wait_ge(b_normp, POST_STEPS * p + NORM_STEPS + steps[0])
                    inverse_root(dve, step, smp[:, 2, :], smp[:, 1, :], smp[:, 3, :])
                    dve.tensor_scalar(smp[:, 2, :], smp[:, 2, :], 1e12, None, ALU.min).then_inc(b_mag, 1)
                    wait(dve, b_me, p + 1)
                    dve.tensor_scalar(smp[:, 3, :], smp[:, 0, :], 1.0, None, ALU.add).then_inc(b_mag, 1)
                    wait(dve, b_mag, 4 * p + 2)
                    dve.reciprocal(smp[:, 3, :], smp[:, 3, :]).then_inc(b_mag, 1)
                    wait(dve, b_mag, 4 * p + 3)
                    dve.scalar_tensor_tensor(smp[:, 3, :], smp[:, 3, :], 1.5, smp[:, 2, :], ALU.mult, ALU.mult)\
                        .then_inc(b_mag, 1)
                    wait(dve, b_mag, 4 * p + 4)
                    wait(dve, b_hs, 32 * p)
                    dve.tensor_tensor(ht_all[:, bass.ds(p * 2, 2)], ext[:, :, 2], smp[:, 3, :], ALU.mult)\
                        .then_inc(b_h, 1)
                    dve.tensor_tensor(hrow[:, :, D + 1], ext[:, :, 1], smp[:, 3, :], ALU.mult).then_inc(b_h, 1)
                    dve.tensor_tensor(hrow[:, :, 0:D], tmpp[:, :, :], col(smp[:, 3, :], D), ALU.mult).then_inc(b_h, 1)

                def body(j, front, post, ahead):
                    keep_weights(j)
                    if post:
                        norm_x2(j - 1)
                    if front:
                        mean(j + 1)
                    add_expert(j, 0)
                    if post:
                        extras(j - 1)
                    add_expert(j, 1)
                    if front:
                        x1(j + 1)
                    add_expert(j, 2)
                    if post:
                        squares(j - 1)
                    add_expert(j, 3)
                    if post:
                        scaled_h(j - 1)
                    add_expert(j, 4)
                    if front:
                        router(j + 1)
                    add_expert(j, 5)
                    add_expert(j, 6)
                    if front:
                        add_biases(j + 1)
                    if ahead:
                        one_hot(j + 2)
                    add_expert(j, 7)

                one_hot(0)
                mean(0)
                x1(0)
                router(0)
                add_biases(0)
                one_hot(1)
                pipeline(dve, body)
                norm_x2(LAST)
                extras(LAST)
                squares(LAST)
                scaled_h(LAST)

        ekT = ring[0:T, 0, :, :].rearrange("p c d -> p (c d)")[:, 0:2 * HID1].rearrange("p (u d) -> p u d", u=2)
        ek = ring[:, 1, :, :].rearrange("p c d -> p (c d)")[:, 0:TP]
        ctxs = ring[:, 1, :, :].rearrange("p c d -> p (c d)")[:, 512:640]
        ctxT = ring[:, 1, :, :].rearrange("p c d -> p (c d)")[:, 640:768]
        g1 = ring[:, 1, :, :].rearrange("p c d -> p (c d)")[:, 768:1024]
        c_x = again(b_x)
        c_xT = again(b_xT)
        c_base = again(b_base)
        c_idx = again(b_idx)
        c_rows = [sem("c_rows_gathered_0"), sem("c_rows_gathered_1")]
        c_hot = again(b_hot)
        c_xb = again(b_xb)
        c_hk = again(b_seg)
        c_V = again(b_cnt)
        c_vm = again(b_router)
        c_vT = again(b_mag)
        c_m = again(b_s1)
        c_chain = again(b_hn)
        c_dg = again(b_hnTp)
        c_row = again(b_hnT)
        c_E = again(b_lin)
        c_P = again(b_x1)
        c_agg = again(b_xf)
        c_se = again(b_norm)
        c_hc = again(b_nb)
        c_ss = again(b_u)
        c_ball = again(b_uTp)
        c_th = again(b_uT)
        c_ff = again(b_in)
        c_lin = again(b_lg)
        c_x3 = again(b_zs)
        c_root = again(b_e)
        c_norm = again(b_w)
        c_nb = again(b_wE)
        c_u = again(b_wTp)
        c_uTp = again(b_wT)
        c_uT = again(b_bo)
        c_lg = again(b_A)
        c_zs = again(b_h1)
        c_e = again(b_B)
        c_top = again(b_h2)
        c_w = again(b_Y)
        c_w2 = again(b_acc)
        c_wTp = again(b_x2s)
        c_wT = again(b_normp)
        c_b2 = again(b_nbp)
        c_A = again(b_up)
        c_g = again(b_x2Tp)
        c_Y = again(b_x2T)
        c_acc = again(b_x2Ts)
        c_out = again(b_hr)
        m_max = sem("m_k_max")
        m_e = sem("m_k_exp")
        m_t = sem("m_k_turned")
        m_c = sem("m_k_turned_copied")
        m_ctx = sem("m_context")
        m_copied = sem("m_copied")
        m_product = sem("m_product")
        with nc.Block() as block:
            @block.sync
            def _(sp):
                sp.dma_start(wout1, a["L1_mix_W_out"]).then_inc(load_experts1, 16)
                sp.dma_start(bias1, a["L1_mix_b_out"].rearrange("(o n) -> o n", o=1).to_broadcast([T, D]))\
                    .then_inc(load_experts1, 16)
                for w, name in ((W1, "L1_ffn_w1"), (W2, "L1_ffn_w2")):
                    sp.dma_start(w[:, :, :, :], a[name].rearrange("e (k p) d -> p e k d", p=P))\
                        .then_inc(load_experts1, 16)

            @block.gpsimd
            def _(pool):
                for semaphore in reused:
                    pool.sem_clear(semaphore)

            @block.vector
            def _(dve):
                dve.memset(zeros[:, 0:P], 0.0).then_inc(m_copied, 1)
                dve.memset(ctxs, 0.0).then_inc(m_copied, 1)
                dve.tensor_reduce(fl[:, 0:1], kT_all[:, :], AX, ALU.max).then_inc(m_max, 1)
                dve.wait_ge(m_max, 1)
                dve.tensor_scalar(fl[:, 1:2], fl[:, 0:1], -1.0, None, ALU.mult).then_inc(m_max, 1)
                with dve.Fori(0, PAIRS) as i:
                    dve.wait_ge(m_t, i + 1)
                    dve.wait_ge(m_ctx, i)
                    dve.tensor_copy(ekT, ps[0][0:T, 0:2 * HID1].rearrange("p (u d) -> p u d", u=2)).then_inc(m_c, 1)
                dve.wait_ge(m_ctx, PAIRS)
                dve.reciprocal(fl[:, 2:3], ps[2][:, 0:1]).then_inc(m_copied, 1)
                dve.wait_ge(m_copied, 3)
                for h in range(HEADS1):
                    r = slice(HD1 * h, HD1 * h + HD1)
                    dve.tensor_scalar(ctxs[r, r], ps[1][r, r], fl[r, 2:3], HD1 ** -0.5, ALU.mult, ALU.mult)\
                        .then_inc(m_copied, 1)
                dve.wait_ge(m_product, 1)
                dve.tensor_copy(ctxT, ps[3][:, 0:P]).then_inc(m_copied, 1)
                dve.wait_ge(m_product, 2)
                dve.tensor_copy(g1, ps[4][:, 0:D]).then_inc(m_copied, 1)
                dve.wait_ge(m_product, 3)
                dve.tensor_copy(M1[:, :, :], ps[5][:, :].rearrange("p (k d) -> p k d", k=KD)).then_inc(m_copied, 1)

            @block.scalar
            def _(act):
                act.wait_ge(m_max, 2)
                with act.Fori(0, PAIRS) as i:
                    act.wait_ge(m_t, i)
                    act.activation(ek, kT_all[:, bass.ds(i * TP, TP)], ACT.Exp, bias=fl[:, 1:2]).then_inc(m_e, 1)

            @block.tensor
            def _(pe):
                pe.wait_ge(m_copied, 1)
                pe.matmul(ps[1][:, 0:HID1], zeros[:, 0:P], zeros[:, 0:HID1], start=True, stop=False,
                          skip_group_check=True)
                pe.matmul(ps[2][:, 0:1], zeros[:, 0:P], zeros[:, 0:1], start=True, stop=False,
                          skip_group_check=True)
                with pe.Fori(0, PAIRS) as i:
                    pe.wait_ge(m_e, i + 1)
                    pe.wait_ge(m_c, i)
                    for u in range(2):
                        last = pe.transpose(ps[0][0:T, u * HID1:(u + 1) * HID1], ek[:, u * T:u * T + T], ident[:, :])
                    last.then_inc(m_t, 1)
                    pe.wait_ge(m_c, i + 1)
                    for u in range(2):
                        pe.matmul(ps[1][:, 0:HID1], ekT[:, u, :], v_all[:, bass.ds(i * 2 + u, 1), :],
                                  start=False, stop=False, skip_group_check=True)
                        last = pe.matmul(ps[2][:, 0:1], ekT[:, u, :], ones[0:T, 0:1], start=False, stop=False,
                                         skip_group_check=True)
                    last.then_inc(m_ctx, 1)
                pe.wait_ge(m_copied, 3 + HEADS1)
                pe.transpose(ps[3][:, 0:P], ctxs, ident[:, :]).then_inc(m_product, 1)
                pe.wait_ge(m_copied, 4 + HEADS1)
                pe.wait_ge(load_experts1, 64)
                pe.matmul(ps[4][:, 0:D], ctxT, wout1[:, :], start=True, stop=True).then_inc(m_product, 1)
                pe.wait_ge(m_copied, 5 + HEADS1)
                for k in range(KD):
                    last = pe.matmul(ps[5][:, k * D:k * D + D], wq1T[:, k, :], g1, start=True, stop=True)
                last.then_inc(m_product, 1)

        i_seen = sem("i_edges_seen")
        i_load = sem("i_edges_loaded")
        i_rows = sem("i_rows_gathered")
        i_pe = sem("i_tensor_steps")
        i_act = sem("i_scalar_steps")
        i_dve = sem("i_vector_steps")
        i_out = sem("i_h_stored")
        i_base = sem("i_h_loaded")
        I_CLEAR, I_STEP, I_END = 4, 17, 3
        I_TILE = I_CLEAR + SWEEPS * I_STEP + I_END
        I_MAXIMA, I_SHIFT, I_DIAG, I_WEIGHTS = 5, 13, 14, 15
        vm = lay[:, 0:2 * T].rearrange("p (u d) -> p u d", u=2)
        dg = lay[0:T, 2 * T:4 * T].rearrange("p (u d) -> p u d", u=2)
        hk = sb("hk", [P, 2, CH])
        hot1 = hot[0:T, 0, 0:SWEEP_CH, :]
        edge1 = big[0:T, 0, 0:SWEEP_CH, :]
        sums1 = tmp[:, :, :].rearrange("p u d -> p (u d)")[:, 0:D + 1]

        with nc.Block() as block:
            @block.sync
            def _(sp):
                with flagged(sp):
                    with sp.Fori(0, NT) as t:
                        sp.wait_ge(made, 1)
                        sp.wait_ge(i_out, 16 * t)
                        sp.dma_start(base[:, 0, :], hbase_d[bass.ds(t * T, T), :]).then_inc(i_base, 16)
                        with sp.Fori(0, SWEEPS) as w:
                            sp.wait_ge(made, 1)
                            sp.wait_ge(i_pe, 3 * (t * SWEEPS + w))
                            sweep_loads(sp, w, i_load)
                        sp.wait_ge(made, 1)
                        sp.wait_ge(i_dve, I_TILE * (t + 1))
                        sp.dma_start(hbase_d[bass.ds(t * T, T), :], hn[:, 0, :]).then_inc(i_out, 16)
                    sp.wait_ge(i_out, 16 * NT)

            @block.gpsimd
            def _(pool):
                with flagged(pool):
                    with pool.Fori(0, NT) as t:
                        with pool.Fori(0, SWEEPS) as w:
                            n = t * SWEEPS + w
                            pool.wait_ge(i_seen, 2 * n)
                            wait_apart(pool, i_load, 32 * (n + 1)).then_inc(i_seen, 1)
                            for c in range(SWEEP_CH):
                                pool.indirect_dma_start(
                                    ring[0:T, 0, c, :], None, htab,
                                    bass.IndirectOffsetOnAxis(ap=sweep_e[:, 0, c:c + 1], axis=0)).then_inc(i_rows, 16)
                            wait_apart(pool, i_pe, 3 * (n + 1)).then_inc(i_seen, 1)
                            wait_apart(pool, i_seen, 2 * n + 2)
                            pool.inc_swdge_sem([i_rows], [16 * SWEEP_CH], mode="sub")

            @block.scalar
            def _(act):
                with flagged(act):
                    with act.Fori(0, NT) as t:
                        with act.Fori(0, SWEEPS) as w:
                            n = t * SWEEPS + w
                            act.wait_ge(i_dve, t * I_TILE + I_CLEAR + w * I_STEP + I_SHIFT)
                            act.activation(sm[:, 7, 0:1], sm[:, 6, 0:1], ACT.Exp).then_inc(i_act, 1)
                            act.wait_ge(i_pe, 3 * n + 2)
                            for c in range(SWEEP_CH):
                                last = act.activation(big[0:T, 0, c, :], ps[3][0:T, 0:T], ACT.Exp,
                                                      bias=ring[0:T, 0, c, D + 1:D + 2])
                            last.then_inc(i_act, 1)

            @block.vector
            def _(dve):
                with flagged(dve):
                    with dve.Fori(0, NT) as t:
                        done = [0]

                        def step(ins, before=t * I_TILE):
                            done[0] += 1
                            ins.then_inc(i_dve, 1)
                            dve.wait_ge(i_dve, before + done[0])

                        step(dve.memset(tmp[:, :, :], 0.0))
                        step(dve.memset(sm[:, 0, :], 0.0))
                        step(dve.memset(sm[:, 5, :], 0.0))
                        step(dve.tensor_copy(sm[:, 8, 0:1], ht_all[:, bass.ds(t, 1)]))
                        assert done[0] == I_CLEAR
                        carry(dve)
                        with dve.Fori(0, SWEEPS) as w:
                            done[0] = 0
                            n = t * SWEEPS + w
                            before = t * I_TILE + I_CLEAR + w * I_STEP
                            dve.wait_ge(i_load, 32 * (n + 1))
                            dve.wait_ge(i_seen, 2 * n + 1)
                            step(dve.tensor_scalar(sweep_r[:, :], sweep_e[:, 1, :], thr[0:T, bass.ds(t, 1)], None,
                                                   ALU.subtract), before)
                            step(dve.tensor_tensor(hot1, col(sweep_r[:, :], T), mid(iota[0:T, :], SWEEP_CH),
                                                   ALU.is_equal), before)
                            dve.wait_ge(i_rows, 16 * SWEEP_CH)
                            step(dve.tensor_scalar(hk[0:T, 0, 0:SWEEP_CH], ring[0:T, 0, 0:SWEEP_CH, D + 1],
                                                   hbound[0:T, 0:1], None, ALU.add), before)
                            step(dve.tensor_tensor(edge1, hot1, col(hk[0:T, 0, 0:SWEEP_CH], T), ALU.mult), before)
                            step(dve.tensor_reduce(vm[0:T, 0, :], edge1.rearrange("p c d -> p d c"), AX, ALU.max),
                                 before)
                            assert done[0] == I_MAXIMA
                            dve.wait_ge(i_pe, 3 * n + 1)
                            step(dve.tensor_reduce(sm[:, 1, 0:1], ps[7][0:T, 0:T], AX, ALU.max), before)
                            step(dve.tensor_tensor(sm[:, 0, 0:1], sm[:, 0, 0:1], sm[:, 1, 0:1], ALU.max), before)
                            step(dve.tensor_scalar(sm[:, 2, 0:1], sm[:, 0, 0:1], nbound[0:T, 0:1], sm[:, 8, 0:1],
                                                   ALU.add, ALU.add), before)
                            step(dve.tensor_scalar(sm[:, 3, 0:1], sm[:, 2, 0:1], -1e9, None, ALU.max), before)
                            step(dve.tensor_tensor(sm[:, 4, 0:1], sm[:, 8, 0:1], sm[:, 3, 0:1], ALU.subtract), before)
                            step(dve.scalar_tensor_tensor(sm[:, 4, 0:1], sm[:, 0, 0:1], 0.0, sm[:, 4, 0:1],
                                                          ALU.is_gt, ALU.mult), before)
                            step(dve.tensor_tensor(sm[:, 6, 0:1], sm[:, 4, 0:1], sm[:, 5, 0:1], ALU.subtract), before)
                            step(dve.tensor_scalar(sm[:, 6, 0:1], sm[:, 6, 0:1], 0.0, None, ALU.min), before)
                            assert done[0] == I_SHIFT
                            step(dve.tensor_scalar(dg[:, 0, :], ident[0:T, 0:T], sm[:, 4, 0:1], None, ALU.mult),
                                 before)
                            assert done[0] == I_DIAG
                            dve.wait_ge(i_act, 2 * n + 2)
                            step(dve.scalar_tensor_tensor(edge1, edge1, FAR, hot1, ALU.min, ALU.mult), before)
                            assert done[0] == I_WEIGHTS
                            dve.wait_ge(i_pe, 3 * n + 3)
                            step(dve.scalar_tensor_tensor(sums1, sums1, sm[:, 7, 0:1], ps[0][0:T, 0:D + 1],
                                                          ALU.mult, ALU.add), before)
                            step(dve.tensor_copy(sm[:, 5, 0:1], sm[:, 4, 0:1]), before)
                            assert done[0] == I_STEP
                        done[0] = 0
                        before = t * I_TILE + I_CLEAR + SWEEPS * I_STEP
                        step(dve.tensor_scalar(sm[:, 9, 0:1], tmp[:, 1, 0:1], 1e-10, None, ALU.add), before)
                        step(dve.reciprocal(sm[:, 9, 0:1], sm[:, 9, 0:1]), before)
                        dve.wait_ge(i_base, 16 * (t + 1))
                        dve.wait_ge(i_out, 16 * t)
                        step(dve.scalar_tensor_tensor(hn[:, 0, :], tmp[:, 0, :], sm[:, 9, 0:1], base[:, 0, :],
                                                      ALU.mult, ALU.add), before)
                        assert done[0] == I_END

            @block.tensor
            def _(pe):
                with flagged(pe):
                    with pe.Fori(0, NT) as t:
                        with pe.Fori(0, SWEEPS) as w:
                            before = t * I_TILE + I_CLEAR + w * I_STEP
                            pe.wait_ge(i_dve, before + I_MAXIMA)
                            pe.transpose(ps[7][0:T, 0:T], vm[0:T, 0, :], ident[0:T, 0:T]).then_inc(i_pe, 1)
                            pe.wait_ge(i_dve, before + I_DIAG)
                            pe.matmul(ps[3][0:T, 0:T], ones[0:T, 0:T], dg[:, 0, :], start=True, stop=True)\
                                .then_inc(i_pe, 1)
                            pe.wait_ge(i_dve, before + I_WEIGHTS)
                            for c in range(SWEEP_CH):
                                last = pe.matmul(ps[0][0:T, 0:D + 1], big[0:T, 0, c, :], ring[0:T, 0, c, 0:D + 1],
                                                 start=(c == 0), stop=(c == SWEEP_CH - 1))
                            last.then_inc(i_pe, 1)


        with nc.Block() as block:
            @block.sync
            def _(sp):
                with sp.Fori(0, PAIRS) as i:
                    sp.wait_ge(made, 1)
                    sp.wait_ge(c_xb, i)
                    sp.dma_start(xin[:, :, :], pair_rows(x2_d, i)).then_inc(c_x, 16)
                    sp.wait_ge(made, 1)
                    sp.wait_ge(c_lin, i)
                    sp.dma_start(xT[:, :, :], xn2T_d[:, :, bass.ds(i * TP, TP)]).then_inc(c_xT, 16)
                    sp.wait_ge(made, 1)
                    sp.wait_ge(c_hc, 2 * i)
                    sp.dma_start(base[:, :, :], pair_rows(hbase_d, i)).then_inc(c_base, 16)
                    sp.wait_ge(made, 1)
                    sp.wait_ge(c_acc, 2 * EX * (i + 1))
                    sp.dma_start(pair_rows(out, i), acc[:, :, :]).then_inc(c_out, 16)
                sp.wait_ge(c_out, 16 * PAIRS)

            @block.gpsimd
            def _(pool):
                with pool.Fori(0, PAIRS) as i:
                    for u in range(2):
                        t = i * 2 + u
                        pool.wait_ge(c_agg, 2 * i)
                        pool.wait_ge(c_rows[u], 16 * CH * i)
                        pool.tensor_copy(idx[:, u, :], srcw[:, bass.ds(t * CH, CH)]).then_inc(c_idx, 1)
                        wait_apart(pool, c_idx, t + 1)
                        for c in range(CH):
                            pool.indirect_dma_start(
                                ring[:, u, c, :], None, htab,
                                bass.IndirectOffsetOnAxis(ap=idx[:, u, c:c + 1], axis=0)).then_inc(c_rows[u], 16)

            @block.tensor
            def _(pe):
                pe.wait_ge(load_experts1, 64)
                with pe.Fori(0, PAIRS) as i:
                    for u in range(2):
                        pe.wait_ge(c_vm, 2 * i + u + 1)
                        pe.transpose(ps[7 - u][0:T, 0:P], vm[:, u, :], ident[:, :]).then_inc(c_vT, 1)
                    pe.wait_ge(c_xT, 16 * (i + 1))
                    pe.wait_ge(c_acc, 2 * EX * i)
                    for u in range(2):
                        for k in range(KD):
                            last = pe.matmul(ps[4][0:T, u * D:u * D + D], xT[:, k, u * T:u * T + T], M1[:, k, :],
                                             start=(k == 0), stop=(k == KD - 1))
                    last.then_inc(c_lin, 1)
                    for u in range(2):
                        pe.wait_ge(c_dg, 2 * i + u + 1)
                        pe.matmul(ps[3 - u][:, 0:T], ones[0:T, :], dg[:, u, :], start=True, stop=True)\
                            .then_inc(c_row, 1)
                    for u in range(2):
                        pe.wait_ge(c_P, 2 * i + u + 1)
                        for c in range(CH):
                            last = pe.matmul(ps[u][0:T, 0:D + 1], big[:, u, c, :], ring[:, u, c, 0:D + 1],
                                             start=(c == 0), stop=(c == CH - 1))
                        last.then_inc(c_agg, 1)
                    pe.wait_ge(c_u, 2 * i + 2)
                    for u in range(2):
                        for k in range(KD):
                            last = pe.transpose(ps[6][:, k * TP + u * T:k * TP + u * T + T],
                                                xn[:, u, k * P:k * P + P], ident[0:T, 0:T])
                    last.then_inc(c_uTp, 1)
                    pe.wait_ge(c_uT, i + 1)
                    for u in range(2):
                        for k in range(KD):
                            last = pe.matmul(ps[7][0:T, 256 + EX * u:256 + EX * u + EX], uT[:, k, u * T:u * T + T],
                                             rwT[:, k, :], start=(k == 0), stop=(k == KD - 1))
                    last.then_inc(c_lg, 1)

                    def hidden(e):
                        bank = 2 if e % 2 == 0 else 6
                        for m in range(KD):
                            for k in range(KD):
                                last = pe.matmul(ps[bank][:, m * D:m * D + TP], W1[:, e, k, m * P:m * P + P],
                                                 uT[:, k, :], start=(k == 0), stop=(k == KD - 1))
                        last.then_inc(c_A, 1)

                    hidden(0)
                    hidden(1)
                    pe.wait_ge(c_w, i + 1)
                    for u in range(2):
                        last = pe.transpose(ps[3][0:EX, 256 + u * T:256 + u * T + T], lg[:, 5, u, :], ident[0:T, 0:T])
                    last.then_inc(c_wTp, 1)
                    pe.wait_ge(c_wT, i + 1)
                    for u in range(2):
                        last = pe.matmul(ps[5][0:T, u * D:u * D + D], wT[:, u * T:u * T + T], b2[:, :],
                                         start=True, stop=True)
                    last.then_inc(c_b2, 1)
                    for e in range(EX):
                        n = EX * i + e
                        src = h1 if e % 2 == 0 else h2
                        pe.wait_ge(c_g, 2 * n + 2)
                        if e < 2:
                            pe.wait_ge(c_x3, 5 * i + 5)
                        else:
                            pe.wait_ge(c_acc, 2 * (n - 1))
                        for u in range(2):
                            for k in range(KD):
                                last = pe.matmul(ps[4 + e % 2][0:T, u * D:u * D + D], src[:, k, u * T:u * T + T],
                                                 W2[:, e, k, :], start=(k == 0), stop=(k == KD - 1))
                        last.then_inc(c_Y, 1)
                        if e + 2 < EX:
                            hidden(e + 2)

            @block.scalar
            def _(act):
                with act.Fori(0, PAIRS) as i:
                    for u in range(2):
                        act.wait_ge(c_row, 2 * i + u + 1)
                        act.wait_ge(c_vm, 2 * i + u + 1)
                        for c in range(CH):
                            act.activation(big[:, u, c, :], ps[3 - u][:, 0:T], ACT.Exp,
                                           bias=ring[:, u, c, D + 1:D + 2]).then_inc(c_E, 1)
                    act.wait_ge(c_ball, 8 * i + 2)
                    act.activation(sm[:, 12, :], sm[:, 11, :], ACT.Tanh).then_inc(c_th, 1)
                    act.wait_ge(c_nb, i + 1)
                    for u in range(2):
                        act.activation(xn[:, u, :], acc[:, u, :], ACT.Identity, bias=nb[:, u:u + 1],
                                       scale=rs[:, u:u + 1]).then_inc(c_u, 1)
                    act.wait_ge(c_uTp, i + 1)
                    act.copy(uT[:, :, :], turned_pair(6)).then_inc(c_uT, 1)
                    act.wait_ge(c_zs, i + 1)
                    act.activation(lg[:, 2, :, :], lg[:, 1, :, :], ACT.Exp).then_inc(c_e, 1)
                    act.wait_ge(c_wTp, i + 1)
                    act.copy(wT[:, :], ps[3][0:EX, 256:256 + TP]).then_inc(c_wT, 1)
                    for e in range(EX):
                        n = EX * i + e
                        act.wait_ge(c_A, n + 1)
                        if e >= 2:
                            act.wait_ge(c_Y, n - 1)
                        bank = 2 if e % 2 == 0 else 6
                        target = h1 if e % 2 == 0 else h2
                        for m in range(KD):
                            act.activation(target[:, m, :], ps[bank][:, m * D:m * D + TP], ACT.Gelu,
                                           bias=b1c[:, 2 * e + m:2 * e + m + 1]).then_inc(c_g, 1)

            @block.vector
            def _(dve):
                with dve.Fori(0, PAIRS) as i:
                    chain = {c_chain: 0, c_ball: 0, c_top: 0, c_root: 0}
                    per = {c_chain: 5, c_ball: 8, c_top: 18, c_root: 2 * ROOT_STEPS}

                    def step(s, ins):
                        chain[s] += 1
                        ins.then_inc(s, 1)
                        dve.wait_ge(s, i * per[s] + chain[s])

                    for u in range(2):
                        t = i * 2 + u
                        dve.wait_ge(c_agg, 2 * i)
                        dve.tensor_tensor(hot[:, u, :, :], col(relw[:, bass.ds(t * CH, CH)], T),
                                          mid(iota[:, :], CH), ALU.is_equal).then_inc(c_hot, 1)
                    for u in range(2):
                        t = i * 2 + u
                        dve.wait_ge(c_rows[u], 16 * CH * (i + 1))
                        dve.tensor_scalar(hk[:, u, :], ring[:, u, :, D + 1], hbound[:, 0:1], None, ALU.add)\
                            .then_inc(c_hk, 1)
                        dve.wait_ge(c_hk, t + 1)
                        dve.wait_ge(c_hot, t + 1)
                        dve.tensor_tensor(big[:, u, :, :], hot[:, u, :, :], col(hk[:, u, :], T), ALU.mult)\
                            .then_inc(c_V, 1)
                        dve.wait_ge(c_V, t + 1)
                        dve.wait_ge(c_vT, t)
                        dve.tensor_reduce(vm[:, u, :], big[:, u, :, :].rearrange("p c d -> p d c"), AX, ALU.max)\
                            .then_inc(c_vm, 1)
                    dve.wait_ge(c_x, 16 * (i + 1))
                    dve.tensor_tensor(tmp[:, :, :], xin[:, :, :], mid(bias1[:, :], 2), ALU.add).then_inc(c_xb, 1)
                    for u in range(2):
                        dve.wait_ge(c_vT, 2 * i + u + 1)
                        dve.tensor_reduce(sm[:, 0, u:u + 1], ps[7 - u][0:T, 0:P], AX, ALU.max)\
                            .then_inc(c_m, 1)
                    dve.wait_ge(c_m, 2 * i + 2)
                    ht = ht_all[:, bass.ds(i * 2, 2)]
                    step(c_chain, dve.tensor_scalar(sm[:, 1, :], sm[:, 0, :], nbound[0:T, 0:1], None, ALU.add))
                    step(c_chain, dve.tensor_tensor(sm[:, 2, :], sm[:, 1, :], ht, ALU.add))
                    step(c_chain, dve.tensor_scalar(sm[:, 3, :], sm[:, 2, :], -1e9, None, ALU.max))
                    step(c_chain, dve.tensor_tensor(sm[:, 4, :], ht, sm[:, 3, :], ALU.subtract))
                    step(c_chain, dve.scalar_tensor_tensor(sm[:, 4, :], sm[:, 0, :], 0.0, sm[:, 4, :],
                                                           ALU.is_gt, ALU.mult))
                    for u in range(2):
                        dve.tensor_scalar(dg[:, u, :], ident[0:T, 0:T], sm[:, 4, u:u + 1], None, ALU.mult)\
                            .then_inc(c_dg, 1)
                    for u in range(2):
                        dve.wait_ge(c_E, CH * (2 * i + u + 1))
                        dve.scalar_tensor_tensor(big[:, u, :, :], big[:, u, :, :], FAR, hot[:, u, :, :],
                                                 ALU.min, ALU.mult).then_inc(c_P, 1)
                    dve.wait_ge(c_base, 16 * (i + 1))
                    for u in range(2):
                        t = i * 2 + u
                        dve.wait_ge(c_agg, t + 1)
                        dve.tensor_scalar(sm[:, 5, u:u + 1], ps[u][0:T, D:D + 1], 1e-10, None, ALU.add).then_inc(c_se, 1)
                        dve.wait_ge(c_se, 2 * t + 1)
                        dve.reciprocal(sm[:, 6, u:u + 1], sm[:, 5, u:u + 1]).then_inc(c_se, 1)
                        dve.wait_ge(c_se, 2 * t + 2)
                        dve.scalar_tensor_tensor(hn[:, u, :], ps[u][0:T, 0:D], sm[:, 6, u:u + 1], base[:, u, :],
                                                 ALU.mult, ALU.add).then_inc(c_hc, 1)
                    for u in range(2):
                        dve.wait_ge(c_hc, 2 * i + u + 1)
                        dve.tensor_tensor_reduce(xin[:, u, :], hn[:, u, :], hn[:, u, :], 1.0, 0.0, ALU.mult,
                                                 ALU.add, sm[:, 7, u:u + 1]).then_inc(c_ss, 1)
                    dve.wait_ge(c_ss, 2 * i + 2)
                    inverse_root(dve, lambda ins: step(c_root, ins), sm[:, 10, :], sm[:, 7, :], sm[:, 15, :])
                    step(c_ball, dve.tensor_tensor(sm[:, 10, :], sm[:, 10, :], sm[:, 7, :], ALU.mult))
                    step(c_ball, dve.tensor_scalar(sm[:, 11, :], sm[:, 10, :], 1e-15, None, ALU.max))
                    step(c_ball, dve.reciprocal(sm[:, 13, :], sm[:, 11, :]))
                    dve.wait_ge(c_th, i + 1)
                    step(c_ball, dve.tensor_tensor(sm[:, 14, :], sm[:, 12, :], sm[:, 13, :], ALU.mult))
                    step(c_ball, dve.tensor_tensor(sm[:, 15, :], sm[:, 14, :], sm[:, 10, :], ALU.mult))
                    step(c_ball, dve.tensor_scalar(sm[:, 16, :], sm[:, 15, :], 1e-8, None, ALU.add))
                    step(c_ball, dve.reciprocal(sm[:, 17, :], sm[:, 16, :]))
                    step(c_ball, dve.tensor_scalar(sm[:, 17, :], sm[:, 17, :], MAX_NORM, 1.0, ALU.mult, ALU.subtract))
                    dve.scalar_tensor_tensor(sm[:, 18, :], sm[:, 15, :], MAX_NORM, sm[:, 17, :], ALU.is_gt, ALU.mult)\
                        .then_inc(c_ff, 1)
                    dve.wait_ge(c_ff, 2 * i + 1)
                    dve.scalar_tensor_tensor(sm[:, 19, :], sm[:, 18, :], 1.0, sm[:, 14, :], ALU.add, ALU.mult)\
                        .then_inc(c_ff, 1)
                    dve.wait_ge(c_lin, i + 1)
                    dve.wait_ge(c_xb, i + 1)
                    dve.wait_ge(c_out, 16 * i)
                    dve.tensor_tensor(acc[:, :, :], tmp[:, :, :], bank2(4), ALU.add).then_inc(c_x3, 1)
                    dve.wait_ge(c_x3, 5 * i + 1)
                    dve.wait_ge(c_ff, 2 * i + 2)
                    for u in range(2):
                        dve.scalar_tensor_tensor(acc[:, u, :], hn[:, u, :], sm[:, 19, u:u + 1], acc[:, u, :],
                                                 ALU.mult, ALU.add).then_inc(c_x3, 1)
                    for u in range(2):
                        dve.wait_ge(c_x3, 5 * i + 2 + u)
                        dve.bn_stats(st[:, u, :], acc[:, u, :]).then_inc(c_norm, 1)
                    wait_apart(dve, c_norm, 5 * i + 2)
                    for u in range(2):
                        dve.bn_aggr(mv[:, u, :], st[:, u, :]).then_inc(c_norm, 1)
                    dve.wait_ge(c_norm, 5 * i + 4)
                    dve.tensor_scalar(sm[:, 14, :], mv[:, :, 1], LN_EPS, None, ALU.add).then_inc(c_norm, 1)
                    dve.wait_ge(c_norm, 5 * i + 5)
                    inverse_root(dve, lambda ins: step(c_root, ins), rs[:, :], sm[:, 14, :], sm[:, 15, :])
                    dve.scalar_tensor_tensor(nb[:, :], mv[:, :, 0], -1.0, rs[:, :], ALU.mult, ALU.mult)\
                        .then_inc(c_nb, 1)
                    dve.wait_ge(c_lg, i + 1)
                    z = ps[7][0:T, 256:256 + 2 * EX].rearrange("p (u e) -> p u e", u=2)
                    io = mid(iota8[:, :], 2)
                    step(c_top, dve.tensor_reduce(sm[:, 20, :], z, AX, ALU.max))
                    dve.tensor_tensor(lg[:, 1, :, :], z, col(sm[:, 20, :], EX), ALU.subtract).then_inc(c_zs, 1)
                    dve.wait_ge(c_e, i + 1)
                    step(c_top, dve.tensor_reduce(sm[:, 21, :], lg[:, 2, :, :], AX, ALU.add))
                    step(c_top, dve.reciprocal(sm[:, 22, :], sm[:, 21, :]))
                    step(c_top, dve.tensor_tensor(lg[:, 3, :, :], lg[:, 2, :, :], col(sm[:, 22, :], EX), ALU.mult))
                    for best in range(2):
                        p = lg[:, 3, :, :] if best == 0 else lg[:, 6, :, :]
                        step(c_top, dve.tensor_reduce(sm[:, 8 + best, :], p, AX, ALU.max))
                        step(c_top, dve.tensor_tensor(lg[:, 0, :, :], p, col(sm[:, 8 + best, :], EX), ALU.not_equal))
                        step(c_top, dve.scalar_tensor_tensor(lg[:, 0, :, :], lg[:, 0, :, :], 99.0, io, ALU.mult, ALU.add))
                        step(c_top, dve.tensor_reduce(sm[:, 23, :], lg[:, 0, :, :], AX, ALU.min))
                        if best == 0:
                            step(c_top, dve.tensor_tensor(lg[:, 4, :, :], io, col(sm[:, 23, :], EX), ALU.is_equal))
                            step(c_top, dve.scalar_tensor_tensor(lg[:, 6, :, :], lg[:, 4, :, :], -2.0, lg[:, 3, :, :],
                                                                 ALU.mult, ALU.add))
                        else:
                            dve.tensor_tensor(lg[:, 7, :, :], io, col(sm[:, 23, :], EX), ALU.is_equal).then_inc(c_w2, 1)
                    step(c_top, dve.tensor_tensor(sm[:, 20, :], sm[:, 8, :], sm[:, 9, :], ALU.add))
                    dve.wait_ge(c_w2, 2 * i + 1)
                    dve.tensor_tensor(lg[:, 7, :, :], lg[:, 7, :, :], lg[:, 4, :, :], ALU.add).then_inc(c_w2, 1)
                    dve.wait_ge(c_w2, 2 * i + 2)
                    step(c_top, dve.tensor_scalar(sm[:, 20, :], sm[:, 20, :], 1e-12, None, ALU.max))
                    step(c_top, dve.reciprocal(sm[:, 21, :], sm[:, 20, :]))
                    step(c_top, dve.tensor_tensor(lg[:, 7, :, :], lg[:, 7, :, :], lg[:, 3, :, :], ALU.mult))
                    dve.tensor_tensor(lg[:, 5, :, :], lg[:, 7, :, :], col(sm[:, 21, :], EX), ALU.mult).then_inc(c_w, 1)
                    dve.wait_ge(c_b2, i + 1)
                    dve.wait_ge(c_u, 2 * i + 2)
                    dve.tensor_tensor(acc[:, :, :], acc[:, :, :], xn[:, :, :], ALU.add).then_inc(c_x3, 1)
                    dve.wait_ge(c_x3, 5 * i + 4)
                    dve.tensor_tensor(acc[:, :, :], acc[:, :, :], bank2(5), ALU.add).then_inc(c_x3, 1)
                    dve.wait_ge(c_x3, 5 * i + 5)
                    for e in range(EX):
                        dve.wait_ge(c_Y, EX * i + e + 1)
                        for u in range(2):
                            if e:
                                dve.wait_ge(c_acc, 2 * (EX * i + e) - 1 + u)
                            dve.scalar_tensor_tensor(acc[:, u, :], bank2(4 + e % 2)[:, u, :], lg[:, 5, u, e:e + 1],
                                                     acc[:, u, :], ALU.mult, ALU.add).then_inc(c_acc, 1)
                    assert chain == per, chain.values()


_INS = ['x', 'src', 'dst', 'L0_gnn_W_left', 'L0_gnn_b_left', 'L0_gnn_W_right', 'L0_mix_w_qkv', 'L0_mix_w_out',
        'L0_mix_b_out', 'L0_ffn_Wr', 'L0_ffn_br', 'L0_ffn_W1', 'L0_ffn_b1', 'L0_ffn_g1', 'L0_ffn_be1', 'L0_ffn_m1',
        'L0_ffn_v1', 'L0_ffn_W2', 'L0_ffn_b2', 'L0_ffn_g2', 'L0_ffn_be2', 'L0_ffn_m2', 'L0_ffn_v2', 'L0_ffn_Wo',
        'L0_ffn_bo', 'L1_gnn_W', 'L1_gnn_b', 'L1_gnn_mag_w', 'L1_gnn_mag_b', 'L1_gnn_attn_w', 'L1_mix_W_qkv',
        'L1_mix_W_out', 'L1_mix_b_out', 'L1_ffn_router_w', 'L1_ffn_w1', 'L1_ffn_b1', 'L1_ffn_w2', 'L1_ffn_b2']


def kernel(**inputs):
    import numpy as _np
    import concourse.bacc as _bacc
    from concourse import mybir as _mybir
    from concourse.bass_utils import run_bass_kernel_spmd as _run

    nc = _bacc.Bacc("TRN2", target_bir_lowering=False, num_devices=1)
    arrays, aps = {}, {}
    for name in _INS:
        arr = _np.ascontiguousarray(inputs[name])
        arrays[f"in_{name}"] = arr
        aps[name] = nc.dram_tensor(f"in_{name}", arr.shape, _mybir.dt.from_np(arr.dtype), kind="ExternalInput").ap()
    out = nc.dram_tensor("out_0", (N, D), F32, kind="ExternalOutput").ap()
    gps_kernel(nc, aps, out)
    r = _run(nc, [arrays], core_ids=[0])
    return r.results[0]["out_0"]
```

```python
from contextlib import ExitStack

import concourse.bass as bass
from concourse import mybir

F32 = mybir.dt.float32
F16 = mybir.dt.float16
I32 = mybir.dt.int32
ALU = mybir.AluOpType
ACT = mybir.ActivationFunctionType
AX = mybir.AxisListType.X

P = 128
N = 6250
E = 106250
D = 256
KD = D // P
T = 125
NT = N // T
PAIRS = NT // 2
TP = 2 * T
CH = 18
WIN = CH * P
SWEEP_CH = 17
SWEEP = SWEEP_CH * T
SWEEPS = E // SWEEP
SAMPLE = 10
EX = 8
HEADS0 = 8
HD0 = 64
KV0 = 2 * HEADS0 * HD0
HEADS1 = 4
HD1 = 32
HID1 = HEADS1 * HD1
ROW1 = D + 2
LN_EPS = 1e-5
BN_EPS = 1e-3
MAX_NORM = 0.95
FAR = 9.0


def col(ap, n):
    return ap.unsqueeze(2).to_broadcast([ap.shape[0], ap.shape[1], n])


def mid(ap, n):
    return ap.unsqueeze(1).to_broadcast([ap.shape[0], n, ap.shape[1]])


ROOT_STEPS = 11


def inverse_root(dve, step, y, x, t):
    step(dve.tensor_scalar(t.bitcast(I32), x.bitcast(I32), 1, None, ALU.logical_shift_right))
    step(dve.tensor_scalar(y.bitcast(I32), t.bitcast(I32), -1.0, float(0x5F3759DF), ALU.mult, ALU.add))
    for _ in range(3):
        step(dve.tensor_tensor(t, y, y, ALU.mult))
        step(dve.scalar_tensor_tensor(t, t, -0.5, x, ALU.mult, ALU.mult))
        step(dve.scalar_tensor_tensor(y, t, 1.5, y, ALU.add, ALU.mult))


def gps_kernel(nc, a, out):
    ctx = ExitStack()
    with ctx:
        def sb(name, shape, dt=F32):
            return ctx.enter_context(nc.sbuf_tensor(name, shape, dt))

        def sem(name):
            return ctx.enter_context(nc.semaphore(name))

        def again(semaphore):
            reused.append(semaphore)
            return semaphore
        reused = []

        ctx.enter_context(nc.allow_non_contiguous_dma(reason="columns of small vectors"))

        xtab = nc.dram_tensor("xtab", (N, 2 * D), F16).ap()
        xnT_d = nc.dram_tensor("xnT_d", (P, KD, N), F32).ap()
        xn2T_d = nc.dram_tensor("xn2T_d", (P, KD, N), F32).ap()
        x2_d = nc.dram_tensor("x2_d", (N, D), F32).ap()
        htab = nc.dram_tensor("htab", (N, ROW1), F32).ap()
        hbase_d = nc.dram_tensor("hbase_d", (N, D), F32).ap()
        nslow_d = nc.dram_tensor("nslow_d", (N, D), F32).ap()

        def pair_rows(t, i):
            return t[bass.ds(i * TP, TP), :].rearrange("(u p) d -> p u d", u=2)

        W1 = sb("W1", [P, EX, KD, D])
        W2 = sb("W2", [P, EX, KD, D])
        Wo = sb("Wo", [P, EX, KD, D])
        kT_all = sb("kT_all", [P, N])
        v_all = sb("v_all", [T, NT, HID1])
        ring = sb("ring", [P, 2, CH, ROW1])
        ring16 = ring[:, :, :, :].rearrange("p u c d -> p (u c d)").bitcast(F16)\
            .rearrange("p (u c d) -> p u c d", u=2, c=CH)
        hot = sb("hot", [P, 2, CH, T], F16)
        big = kT_all[:, 0:2 * CH * T].rearrange("p (u c d) -> p u c d", u=2, c=CH)
        srcw = sb("srcw", [P, NT * CH], I32)
        relw = sb("relw", [P, NT * CH])
        idx = sb("idx", [P, 2, CH], I32)
        ident = sb("ident", [P, P])
        ones = sb("ones", [P, P])
        ones16 = sb("ones16", [P, 1], F16)
        zeros = sb("zeros", [P, 512])
        iota = sb("iota", [P, T])
        thr = sb("thr", [P, NT])
        cols = sb("cols", [P, 448])
        bn = sb("bn", [P, 2, 2, 2 * EX])
        wg = sb("wg", [P, KD, D])
        wg3 = sb("wg3", [P, KD, 3])
        c3 = sb("c3", [T, 3])
        hbound = sb("hbound", [P, 1])
        nbound = sb("nbound", [P, 1])
        Wr = sb("Wr", [P, KD, EX])
        br = sb("br", [T, EX])
        bo = sb("bo", [EX, D])
        b2 = sb("b2", [EX, D])
        bias0 = sb("bias0", [T, D])
        gb = sb("gb", [T, D])
        late = sb("late", [P, 2 * D])
        bias1 = late[0:T, D:2 * D]
        bl = sb("bl", [T, D])
        WL = sb("WL", [P, 2 * KD, D])
        M1 = sb("M1", [P, KD, D])
        wqkv1 = sb("wqkv1", [P, KD, 3 * HID1])
        wout1 = late[:, 0:D]
        flag = sb("flag", [1, 1], I32)
        ht_all = sb("ht_all", [T, NT])
        iota8 = sb("iota8", [T, EX])
        fl = sb("fl", [P, 4])
        lay = sb("lay", [P, 512])
        nothing = sb("nothing", [1, 96])
        xin = sb("xin", [T, 2, D])
        xT = sb("xT", [P, KD, TP])
        base = sb("base", [T, 2, D])
        st = sb("st", [T, 2, 6])
        mv = sb("mv", [T, 2, 2])
        rs = sb("rs", [T, 2])
        nb = sb("nb", [T, 2])
        xn = sb("xn", [T, 2, D])
        acc = sb("acc", [T, 2, D])
        uT = sb("uT", [P, KD, TP])
        h1 = sb("h1", [P, KD, TP])
        h2 = sb("h2", [P, KD, TP])
        tmp = sb("tmp", [T, 2, D])
        hn = sb("hn", [T, 2, D])
        hnT = sb("hnT", [P, KD, TP])
        sm = sb("sm", [T, 24, 2])
        lg = sb("lg", [T, 8, 2, EX])
        wT = sb("wT", [EX, TP])
        hrow = sb("hrow", [T, 2, ROW1])
        ps = [ctx.enter_context(nc.psum_tensor(f"ps{i}", [P, 512], F32)) for i in range(8)]

        f1 = W1[:, :, :, :].rearrange("p e k d -> p (e k d)")
        f2 = W2[:, :, :, :].rearrange("p e k d -> p (e k d)")
        wqkv0 = f1[:, 0:12 * D].rearrange("p (r d) -> p r d", r=12)
        wout0 = f2[:, 0:2 * 512].rearrange("p (r d) -> p r d", r=2)
        woutT = f2[:, 1024:1024 + 4 * D].rearrange("p (r d) -> p r d", r=4)
        wkvT = f2[:, 2048:2048 + 2 * KV0].rearrange("p (k d) -> p k d", k=KD)
        gnnW = f1[:, 3072:3072 + 2 * D].rearrange("p (r d) -> p r d", r=2)

        setup_loads = []
        uses = []
        load_setup = sem("load_setup")
        load_edges = sem("load_edges")
        load_experts0 = sem("load_experts0")
        load_experts1 = sem("load_experts1")

        rows = kT_all[0:80, 0:2 * P].rearrange("p (l d) -> p l d", l=2)
        rows_b1 = kT_all[0:16, 256:256 + P]
        rwrow = kT_all[0:EX, 384:384 + D]
        acol = kT_all[:, 640:644].rearrange("p (s t) -> p s t", s=2)
        bcol = kT_all[:, 644:646]
        asq = kT_all[:, 646:648]
        asum = kT_all[:, 648:649]
        bfull = kT_all[:, 656:656 + 2 * T].rearrange("p (t n) -> p t n", t=2)
        magb = kT_all[0:T, 910:911]
        wright = kT_all[:, 1024:1024 + 2 * D].rearrange("p (k d) -> p k d", k=KD)
        wmean = kT_all[:, 1600:1632]
        bnt = kT_all[:, 3600:3600 + 64].rearrange("p (l v n) -> p l v n", l=2, v=2)
        dst_all = v_all[:, :, :].rearrange("p t d -> p (t d)")[:, 0:850].bitcast(I32)
        dstf = v_all[:, :, :].rearrange("p t d -> p (t d)")[:, 900:985]
        cnt = v_all[:, :, :].rearrange("p t d -> p (t d)")[:, 1000:1050]
        startf = v_all[:, :, :].rearrange("p t d -> p (t d)")[0:1, 1100:1150]
        starti = v_all[:, :, :].rearrange("p t d -> p (t d)")[0:1, 1200:1250].bitcast(I32)
        dstw = kT_all[:, 4500:4500 + NT * CH].bitcast(I32)
        ge = kT_all[:, 1600:1600 + NT * CH]
        lt = kT_all[:, 2600:2600 + NT * CH]
        cmp = ring[0:T, :, :, :].rearrange("p u c d -> p (u c d)")[:, 0:NT * 85]\
            .rearrange("p (t s) -> p t s", t=NT)

        turns = []
        for k in range(KD):
            for g in range(2):
                turns.append((wkvT[:, k, 512 * g:512 * g + 512],
                              [(wqkv0[:, 4 + 4 * g + r, k * P:k * P + P], P) for r in range(4)]))
        for g in range(2):
            turns.append((woutT[:, 2 * g:2 * g + 2, :].rearrange("p r d -> p (r d)"),
                          [(wout0[:, o, (2 * g + q) * P:(2 * g + q) * P + P], P) for q in range(2) for o in range(2)]))
        turns.append((wg[:, :, :].rearrange("p k d -> p (k d)"),
                      [(gnnW[:, o, k * P:k * P + P], P) for k in range(KD) for o in range(2)]))
        turns.append((cols[:, :],
                      [(wqkv1[:, 0, 0:P], P), (wqkv1[:, 1, 0:P], P)]
                      + [(rwrow[:, k * P:k * P + P], EX) for k in range(KD)]
                      + [(rows[:, l, :], 80) for l in range(2)] + [(rows_b1, 16)]))
        wq1T = cols[:, 0:2 * P].rearrange("p (k i) -> p k i", k=KD)
        rwT = cols[:, 256:272].rearrange("p (k e) -> p k e", k=KD)
        bnc = cols[:, 272:432].rearrange("p (l v n) -> p l v n", l=2, v=5)
        b1c = cols[:, 432:448]

        def carry(engine):
            at = len(uses)
            uses.append(at)
            target = nothing[0:1, 2 + at:3 + at]
            if engine.engine == nc.gpsimd.engine:
                return engine.tensor_tensor(target, nothing[0:1, 0:1], nothing[0:1, 1:2], ALU.add)
            return engine.memset(target, 0.0)

        def wait_apart(engine, semaphore, value):
            engine.wait_ge(semaphore, value)
            return carry(engine)

        def wait(engine, semaphore, value):
            if not isinstance(value, int) or value > 0:
                engine.wait_ge(semaphore, value)

        def bank2(n):
            return ps[n][0:T, :].rearrange("p (u d) -> p u d", u=2)

        def turned_pair(n):
            return ps[n][:, 0:KD * TP].rearrange("p (k n) -> p k n", k=KD)

        def transpose_pair(pe, bank, src):
            for u in range(2):
                for k in range(KD):
                    last = pe.transpose(ps[bank][:, k * TP + u * T:k * TP + u * T + T],
                                        src[:, u, k * P:k * P + P], ident[0:T, 0:T])
            return last

        NORM_STEPS = 5 + ROOT_STEPS

        def norm(dve, x, s, m, v, w, y, shift, counted, n, free, done):
            for u in range(2):
                dve.bn_stats(s[:, u, :], x[:, u, :]).then_inc(counted, 1)
            wait_apart(dve, counted, n + 2)
            for u in range(2):
                dve.bn_aggr(m[:, u, :], s[:, u, :]).then_inc(counted, 1)
            dve.wait_ge(counted, n + 4)
            if free is not None:
                wait(dve, *free)
            dve.tensor_scalar(v, m[:, :, 1], LN_EPS, None, ALU.add).then_inc(counted, 1)
            dve.wait_ge(counted, n + 5)
            steps = [0]

            def step(ins):
                steps[0] += 1
                ins.then_inc(counted, 1)
                dve.wait_ge(counted, n + 5 + steps[0])
            inverse_root(dve, step, y, v, w)
            dve.scalar_tensor_tensor(shift, m[:, :, 0], -1.0, y, ALU.mult, ALU.mult).then_inc(done, 1)

        LAST = PAIRS - 1

        def pipeline(engine, body):
            body(0, True, False, True)
            with engine.Fori(1, LAST - 1) as j:
                body(j, True, True, True)
            body(LAST - 1, True, True, False)
            body(LAST, False, True, False)

        made = sem("made")
        zeroed = sem("zeroed")
        turned = sem("turned")
        turned_copied = sem("turned_copied")
        s_dve = sem("setup_dve")
        s_count = sem("setup_counted")
        s_start = sem("setup_starts")
        s_a = sem("setup_through_w")
        s_norm = sem("setup_before_summed")
        s_match = sem("setup_matches")
        windows = sem("windows_loaded")
        nslow_zero = sem("nslow_zero")

        with nc.Block() as block:
            @block.sync
            def _(sp):
                sp.dma_start(dst_all, a["dst"].rearrange("(p n) -> p n", p=T)).then_inc(load_edges, 16)

                def put(dst, src):
                    sp.dma_start(dst, src).then_inc(load_setup, 16)
                    put.n += 1
                put.n = 0
                put(wqkv0, a["L0_mix_w_qkv"].rearrange("(r p) d -> p r d", p=P))
                put(wout0, a["L0_mix_w_out"].rearrange("(r p) d -> p r d", p=P))
                put(gnnW, a["L1_gnn_W"].rearrange("(r p) d -> p r d", p=P))
                put(wqkv1[:, :, :], a["L1_mix_W_qkv"].rearrange("(k p) d -> p k d", p=P))
                put(rwrow, a["L1_ffn_router_w"])
                for l, names in enumerate((("g1", "b1", "be1", "m1", "v1"), ("g2", "b2", "be2", "m2", "v2"))):
                    for v, name in enumerate(names):
                        put(rows[16 * v:16 * v + 16, l, :], a["L0_ffn_" + name].rearrange("e (k p) -> (e k) p", p=P))
                put(rows_b1, a["L1_ffn_b1"].rearrange("e (k p) -> (e k) p", p=P))
                put(acol, a["L1_gnn_attn_w"].rearrange("o (s t p) -> p (o s) t", s=2, p=P))
                put(bcol, a["L1_gnn_b"].rearrange("(t p) -> p t", p=P))
                put(magb, a["L1_gnn_mag_b"].rearrange("(o n) -> o n", o=1).to_broadcast([T, 1]))
                put(wg3[:, :, 0:1], a["L1_gnn_mag_w"].rearrange("o (k p) -> p k o", p=P))
                put(WL[:, :, :], a["L0_gnn_W_left"].rearrange("(k p) d -> p k d", p=P))
                put(wright, a["L0_gnn_W_right"].rearrange("(k p) d -> p k d", p=P))
                put(Wr[:, :, :], a["L0_ffn_Wr"].rearrange("(k p) e -> p k e", p=P))
                put(bo[:, :], a["L0_ffn_bo"])
                put(b2[:, :], a["L1_ffn_b2"])

                def row(t, name, n):
                    put(t[:, :], a[name].rearrange("(o n) -> o n", o=1).to_broadcast([T, n]))
                row(br, "L0_ffn_br", EX)
                row(bl, "L0_gnn_b_left", D)
                row(bias0, "L0_mix_b_out", D)
                row(gb, "L1_gnn_b", D)
                setup_loads.append(put.n)
                sp.dma_start(Wo[:, :, :, :], a["L0_ffn_Wo"].rearrange("e (k p) d -> p e k d", p=P)).then_inc(load_experts0, 16)
                sp.wait_ge(zeroed, 1)
                for k in range(PAIRS):
                    sp.dma_start(nslow_d[k * TP:k * TP + TP, :].rearrange("(u p) d -> p u d", u=2), zeros[0:T, :].rearrange("p (u d) -> p u d", u=2))\
                        .then_inc(nslow_zero, 16)
                sp.wait_ge(s_start, 1)
                sp.wait_ge(nslow_zero, 16 * PAIRS)

            @block.gpsimd
            def _(pool):
                pool.memset(ident[:, :], 0.0).then_inc(made, 1)
                pool.memset(ones[:, :], 1.0).then_inc(made, 1)
                pool.memset(nothing[:, 0:2], 0.0).then_inc(made, 1)
                pool.memset(ones16[:, :], 1.0).then_inc(made, 1)
                pool.memset(hrow[:, :, D:D + 1], 1.0).then_inc(made, 1)
                pool.iota(idx[:, 0, 0:1], pattern=[[0, 1]], base=0, channel_multiplier=0).then_inc(made, 1)
                pool.iota(kT_all[:, 2000:2000 + T].bitcast(I32), pattern=[[1, T]], base=0, channel_multiplier=0).then_inc(made, 1)
                pool.iota(kT_all[:, 2200:2200 + NT].bitcast(I32), pattern=[[T, NT]], base=0, channel_multiplier=0).then_inc(made, 1)
                pool.wait_ge(made, 8)
                pool.affine_select(out=ident[:, :], in_=ident[:, :], compare_op=ALU.not_equal, fill=1.0,
                                   base=0, pattern=[[-1, P]], channel_multiplier=1).then_inc(made, 1)

            @block.vector
            def _(dve):
                n = [0]

                def step(ins):
                    n[0] += 1
                    ins.then_inc(s_dve, 1)
                    dve.wait_ge(s_dve, n[0])

                dve.memset(zeros[:, :], 0.0).then_inc(zeroed, 1)
                dve.wait_ge(made, 9)
                step(dve.tensor_copy(iota[:, :], kT_all[:, 2000:2000 + T].bitcast(I32)))
                step(dve.tensor_copy(thr[:, :], kT_all[:, 2200:2200 + NT].bitcast(I32)))
                step(dve.tensor_copy(iota8[:, :], iota[0:T, 0:EX]))
                dve.wait_ge(load_edges, 16)
                step(dve.tensor_copy(dstf, dst_all.rearrange("p (n s) -> p n s", s=SAMPLE)[:, :, 0]))
                step(dve.tensor_tensor(cmp, mid(dstf, NT), col(thr[0:T, :], 85), ALU.is_lt))
                dve.tensor_reduce(cnt, cmp, AX, ALU.add).then_inc(s_count, 1)
                dve.wait_ge(s_norm, 1)
                step(dve.tensor_scalar(startf, ps[4][0:1, 0:NT], float(SAMPLE), -float(SAMPLE), ALU.mult, ALU.add))
                step(dve.tensor_scalar(startf, startf, 0.0, float(E - WIN), ALU.max, ALU.min))
                dve.tensor_copy(starti, startf).then_inc(s_start, 1)

                dve.wait_ge(load_setup, 16 * setup_loads[0])
                for g, (target, sources) in enumerate(turns):
                    dve.wait_ge(turned, g + 1)
                    if len(sources) == 4:
                        dve.tensor_copy(target, ps[g % 4][:, :]).then_inc(turned_copied, 1)
                    else:
                        dve.tensor_copy(target, ps[g % 4][:, 0:448]).then_inc(turned_copied, 1)
                dve.wait_ge(turned_copied, len(turns))
                heads = wkvT.rearrange("p k (h d) -> p (k h) d", d=HD0)
                step(dve.tensor_reduce(wmean, heads, AX, ALU.add))
                step(dve.tensor_scalar(wmean, wmean, 1.0 / HD0, None, ALU.mult))
                step(dve.tensor_tensor(heads, heads, col(wmean, HD0), ALU.subtract))
                step(dve.tensor_tensor(bias0[:, :], bias0[:, :], bl[:, :], ALU.add))
                step(dve.tensor_tensor(WL[:, 0:KD, :], WL[:, 0:KD, :], wright, ALU.add))
                step(dve.tensor_tensor(asq, acol[:, 0, :], acol[:, 0, :], ALU.mult))
                step(dve.tensor_reduce(asum, asq, AX, ALU.add))
                dve.tensor_copy(bfull, col(bcol, T)).then_inc(s_count, 1)
                dve.wait_ge(s_a, 1)
                step(dve.tensor_copy(wg3[:, :, 1:3], ps[5][:, 0:4].rearrange("p (k s) -> p k s", k=KD)))
                step(dve.tensor_copy(c3[:, 1:3], ps[5][0:T, 8:10]))
                step(dve.tensor_copy(c3[:, 0:1], magb))
                step(dve.tensor_copy(fl[:, 3:4], ps[5][:, 16:17]))

            @block.tensor
            def _(pe):
                pe.wait_ge(made, 9)
                pe.wait_ge(s_count, 1)
                pe.matmul(ps[4][0:1, 0:NT], ones[0:T, 0:1], cnt, start=True, stop=True).then_inc(s_norm, 1)
                pe.wait_ge(load_setup, 16 * setup_loads[0])
                for g, (target, sources) in enumerate(turns):
                    if g >= 4:
                        pe.wait_ge(turned_copied, g - 3)
                    at = 0
                    for src, r in sources:
                        last = pe.transpose(ps[g % 4][:, at:at + r], src, ident[0:r, 0:r])
                        at += r
                    last.then_inc(turned, 1)
                pe.wait_ge(s_count, 2)
                for k in range(KD):
                    for o in range(2):
                        pe.matmul(ps[5][:, 2 * k:2 * k + 2], gnnW[:, o, k * P:k * P + P], acol[:, :, o],
                                  start=(o == 0), stop=(o == 1))
                for o in range(2):
                    pe.matmul(ps[5][0:T, 8:10], bfull[:, o, :], acol[:, :, o], start=(o == 0), stop=(o == 1))
                pe.matmul(ps[5][:, 16:17], ones[:, :], asum, start=True, stop=True).then_inc(s_a, 1)

        sq = big[0:T, :, :, :].rearrange("p u c d -> p u (c d)")[:, :, 0:KV0]
        kc = ring[0:T, 0, :, :].rearrange("p c d -> p (c d)")[:, 0:1024].rearrange("p (u d) -> p u d", u=2)
        vc = ring[0:T, 0, :, :].rearrange("p c d -> p (c d)")[:, 1024:2048].rearrange("p (u d) -> p u d", u=2)
        x16 = ring[0:T, 1, :, :].rearrange("p c d -> p (c d)")[:, 0:512].bitcast(F16)\
            .rearrange("p (u d) -> p u d", u=2)
        vr = v_all[:, :, :].rearrange("p t d -> p (t d)")[:, 2048:3072].rearrange("p (u d) -> p u d", u=2)
        rk = ring[0:T, 1, :, :].rearrange("p c d -> p (c d)")[:, 600:640].rearrange("p (u d) -> p u d", u=2)
        rk8, rk8y, rk8t = (ring[0:T, 1, :, :].rearrange("p c d -> p (c d)")[:, n:n + 16]
                           .rearrange("p (u d) -> p u d", u=2) for n in (700, 716, 732))
        xTp = [xT[:, :, 0:T], xT[:, :, T:TP]]

        a_load = [sem("a_x_loaded_0"), sem("a_x_loaded_1")]
        a_norm = sem("a_stats_mean")
        a_root = sem("a_root_steps")
        a_nb = sem("a_shift")
        a_xn = sem("a_xn")
        a_hi = sem("a_hi")
        a_lo = sem("a_lo")
        a_tab = [sem("a_table_stored_0"), sem("a_table_stored_1")]
        a_tr = sem("a_turned")
        a_xT = sem("a_xT")
        a_xTs = [sem("a_xT_stored_0"), sem("a_xT_stored_1")]
        a_kv = sem("a_kv")
        a_k = sem("a_k_copied")
        a_sq = sem("a_squares")
        a_ms = sem("a_mean_squares")
        a_r = sem("a_kv_var_product")
        a_v = [sem("a_v_scaled_0"), sem("a_v_scaled_1")]
        a_dots = sem("a_dots")

        with nc.Block() as block:
            @block.sync
            def _(sp):
                def load(i):
                    for u in range(2):
                        wait(sp, made, 1)
                        wait(sp, a_xn, 2 * i - 1 + u)
                        sp.dma_start(xin[:, u, :], a["x"][bass.ds((2 * i + u) * T, T), :]).then_inc(a_load[u], 16)

                def window(t):
                    start = sp.value_load(starti[0:1, bass.ds(t, 1)], min_val=0, max_val=E - WIN)
                    sp.dma_start(srcw[:, bass.ds(t * CH, CH)],
                                 a["src"][bass.ds(start, WIN)].rearrange("(p c) -> p c", p=P)).then_inc(windows, 16)
                    sp.dma_start(dstw[:, bass.ds(t * CH, CH)],
                                 a["dst"][bass.ds(start, WIN)].rearrange("(p c) -> p c", p=P)).then_inc(windows, 16)

                def store(i):
                    for u in range(2):
                        t = i * 2 + u
                        wait(sp, made, 1)
                        wait(sp, a_lo, t + 1)
                        wait(sp, a_hi, t + 1)
                        sp.dma_start(xtab[bass.ds(t * T, T), :], x16[:, u, :]).then_inc(a_tab[u], 16)
                        wait(sp, made, 1)
                        wait(sp, a_xT, t + 1)
                        sp.dma_start(xnT_d[:, :, bass.ds(t * T, T)], xTp[u]).then_inc(a_xTs[u], 16)

                def body(i):
                    load(i + 1)
                    window(2 * i)
                    window(2 * i + 1)
                    store(i)

                load(0)
                body(0)
                with sp.Fori(1, LAST) as i:
                    body(i)
                window(2 * LAST)
                window(2 * LAST + 1)
                store(LAST)
                for u in range(2):
                    sp.wait_ge(a_tab[u], 16 * PAIRS)
                    sp.wait_ge(a_xTs[u], 16 * PAIRS)

            @block.scalar
            def _(act):
                def normalize(i):
                    for u in range(2):
                        t = i * 2 + u
                        wait(act, a_nb, i + 1)
                        wait(act, a_lo, t - 1)
                        wait(act, a_tr, t - 1)
                        act.activation(xn[:, u, :], xin[:, u, :], ACT.Identity, bias=nb[:, u:u + 1],
                                       scale=rs[:, u:u + 1]).then_inc(a_xn, 1)
                        wait(act, a_tab[u], 16 * i)
                        wait(act, a_xn, t + 1)
                        act.copy(x16[:, u, 0:D], xn[:, u, :]).then_inc(a_hi, 1)

                def squares(i, u):
                    t = i * 2 + u
                    wait(act, a_kv, t + 1)
                    wait(act, a_ms, t - 1)
                    act.activation(sq[:, u, 0:512], ps[2 * u][0:T, :], ACT.Square).then_inc(a_sq, 1)
                    act.activation(sq[:, u, 512:1024], ps[2 * u + 1][0:T, :], ACT.Square).then_inc(a_sq, 1)
                    wait(act, a_dots, t - 1)
                    act.copy(kc[:, u, :], ps[2 * u][0:T, :]).then_inc(a_k, 1)
                    wait(act, a_v[u], i)
                    act.copy(vr[:, u, :], ps[2 * u + 1][0:T, :]).then_inc(a_k, 1)

                def body(i):
                    squares(i, 0)
                    normalize(i + 1)
                    squares(i, 1)

                normalize(0)
                body(0)
                with act.Fori(1, LAST) as i:
                    body(i)
                squares(LAST, 0)
                squares(LAST, 1)

            @block.gpsimd
            def _(pool):
                def low_part(i):
                    for u in range(2):
                        t = i * 2 + u
                        wait(pool, a_hi, t + 1)
                        pool.tensor_tensor(x16[:, u, D:2 * D], xn[:, u, :], x16[:, u, 0:D], ALU.subtract)\
                            .then_inc(a_lo, 1)

                def scale_values(i):
                    wait(pool, a_root, ROOT_STEPS * (i + 1))
                    wait(pool, a_dots, 2 * i)
                    wait(pool, a_k, 4 * i + 4)
                    pool.tensor_tensor(vc[:, 1, :].rearrange("p (h d) -> p h d", d=HD0),
                                       vr[:, 1, :].rearrange("p (h d) -> p h d", d=HD0),
                                       col(rk8y[:, 1, :], HD0), ALU.mult).then_inc(a_v[1], 1)

                def body(i):
                    low_part(i + 1)
                    scale_values(i)

                low_part(0)
                body(0)
                with pool.Fori(1, LAST) as i:
                    body(i)
                scale_values(LAST)

            @block.vector
            def _(dve):
                def moments(i):
                    for u in range(2):
                        wait(dve, a_load[u], 16 * (i + 1))
                    norm(dve, xin, st, mv, sm[:, 14, :], sm[:, 15, :], rs[:, :], nb[:, :], a_norm, NORM_STEPS * i,
                         (a_xn, 2 * i), a_nb)

                def copy_turned(i):
                    for u in range(2):
                        t = i * 2 + u
                        wait(dve, a_tr, t + 1)
                        wait(dve, a_xTs[u], 16 * i)
                        wait(dve, a_kv, t - 1)
                        dve.tensor_copy(xTp[u], ps[4 + u][:, 0:2 * T].rearrange("p (k n) -> p k n", k=KD))\
                            .then_inc(a_xT, 1)

                def sum_squares(i, u):
                    wait(dve, a_sq, 4 * i + 2 * u + 2)
                    dve.tensor_reduce(rk[:, u, 0:16], sq[:, u, :].rearrange("p (h d) -> p h d", d=HD0),
                                      AX, ALU.add).then_inc(a_ms, 1)

                def deviations(i):
                    wait(dve, a_ms, 2 * i + 2)
                    dve.tensor_scalar(rk[:, :, 0:16], rk[:, :, 0:16], 1.0 / HD0, LN_EPS, ALU.mult, ALU.add)\
                        .then_inc(a_r, 1)
                    wait(dve, a_r, 2 * i + 1)
                    dve.tensor_tensor(rk8, rk[:, :, 0:8], rk[:, :, 8:16], ALU.mult).then_inc(a_r, 1)
                    wait(dve, a_r, 2 * i + 2)
                    done = [0]

                    def step(ins):
                        done[0] += 1
                        ins.then_inc(a_root, 1)
                        dve.wait_ge(a_root, ROOT_STEPS * i + done[0])
                    wait(dve, a_v[1], i)
                    inverse_root(dve, step, rk8y, rk8, rk8t)
                    wait(dve, a_dots, 2 * i)
                    wait(dve, a_k, 4 * i + 2)
                    dve.tensor_tensor(vc[:, 0, :].rearrange("p (h d) -> p h d", d=HD0),
                                      vr[:, 0, :].rearrange("p (h d) -> p h d", d=HD0),
                                      col(rk8y[:, 0, :], HD0), ALU.mult).then_inc(a_v[0], 1)

                def body(i):
                    moments(i + 1)
                    sum_squares(i, 0)
                    copy_turned(i + 1)
                    sum_squares(i, 1)
                    deviations(i)

                moments(0)
                copy_turned(0)
                body(0)
                with dve.Fori(1, LAST) as i:
                    body(i)
                sum_squares(LAST, 0)
                sum_squares(LAST, 1)
                deviations(LAST)

            @block.tensor
            def _(pe):
                def turn(i):
                    for u in range(2):
                        t = i * 2 + u
                        wait(pe, a_xn, t + 1)
                        wait(pe, a_xT, t - 1)
                        for k in range(KD):
                            last = pe.transpose(ps[4 + u][:, k * T:k * T + T], xn[:, u, k * P:k * P + P],
                                                ident[0:T, 0:T])
                        last.then_inc(a_tr, 1)

                def keys_values(i, u):
                    t = i * 2 + u
                    wait(pe, a_xT, t + 1)
                    wait(pe, a_k, 2 * (t - 1))
                    for half in range(2):
                        for k in range(KD):
                            last = pe.matmul(ps[2 * u + half][0:T, :], xTp[u][:, k, :],
                                             wkvT[:, k, 512 * half:512 * half + 512],
                                             start=(k == 0), stop=(k == KD - 1))
                    last.then_inc(a_kv, 1)

                def dots(i):
                    for u in range(2):
                        t = i * 2 + u
                        wait(pe, a_k, 2 * t + 2)
                        wait(pe, a_v[u], i + 1)
                        for q in range(4):
                            last = pe.matmul(ps[6][:, q * P:q * P + P], vc[:, u, q * P:q * P + P],
                                             kc[:, u, q * P:q * P + P], start=False, stop=False,
                                             skip_group_check=True)
                        last.then_inc(a_dots, 1)

                pe.matmul(ps[6][:, :], zeros[:, 0:P], zeros[:, :], start=True, stop=False,
                          skip_group_check=True)
                turn(0)
                keys_values(0, 0)
                keys_values(0, 1)
                turn(1)
                with pe.Fori(1, LAST) as i:
                    keys_values(i, 0)
                    dots(i - 1)
                    keys_values(i, 1)
                    turn(i + 1)
                keys_values(LAST, 0)
                dots(LAST - 1)
                keys_values(LAST, 1)
                dots(LAST)

        dsb = kT_all[:, 0:512].rearrange("p (q d) -> p q d", q=4)
        gsb = kT_all[:, 512:1536].rearrange("p (q d) -> p q d", q=4)
        b_idx = sem("b_idx")
        b_rows = [sem("b_rows_gathered_0"), sem("b_rows_gathered_1")]
        b_seg = sem("b_segment_sums")

        def gather_x(pool, i):
            for u in range(2):
                t = i * 2 + u
                wait(pool, b_seg, t - 1)
                wait(pool, b_rows[u], 16 * CH * i)
                pool.tensor_copy(idx[:, u, :], srcw[:, bass.ds(t * CH, CH)]).then_inc(b_idx, 1)
                wait_apart(pool, b_idx, t + 1)
                for c in range(CH):
                    pool.indirect_dma_start(
                        ring16[:, u, c, 0:2 * D], None, xtab,
                        bass.IndirectOffsetOnAxis(ap=idx[:, u, c:c + 1], axis=0)).then_inc(b_rows[u], 16)

        f_copied = sem("f_copied")
        f_steps = sem("f_window_steps")
        f_found = sem("f_edges_counted")
        f_product = sem("f_product")
        with nc.Block() as block:
            @block.gpsimd
            def _(pool):
                wait_apart(pool, windows, 32 * NT)
                gather_x(pool, 0)
                for u in range(2):
                    wait_apart(pool, b_rows[u], 16 * CH)

            @block.vector
            def _(dve):
                dve.memset(dsb, 0.0).then_inc(f_copied, 1)
                dve.wait_ge(f_copied, 1)
                for h in range(2):
                    r = slice(HD0 * h, HD0 * h + HD0)
                    dve.tensor_scalar(dsb[r, :, r], ps[6][r, :].rearrange("p (q d) -> p q d", q=4)[:, :, r],
                                      1.0 / N, None, ALU.mult).then_inc(f_copied, 1)
                dve.wait_ge(f_product, 1)
                for g in range(2):
                    dve.tensor_copy(gsb[:, 2 * g:2 * g + 2, :].rearrange("p q d -> p (q d)"), ps[g][:, :])\
                        .then_inc(f_copied, 1)
                dve.wait_ge(f_product, 2)
                dve.tensor_tensor(WL[:, 0:KD, :], WL[:, 0:KD, :], ps[2][:, :].rearrange("p (k d) -> p k d", k=KD),
                                  ALU.add).then_inc(f_copied, 1)
                n = [0]

                def f_step(ins):
                    n[0] += 1
                    ins.then_inc(f_steps, 1)
                    dve.wait_ge(f_steps, n[0])

                dve.wait_ge(windows, 32 * NT)
                f_step(dve.tensor_copy(relw[:, :], dstw))
                for l in range(2):
                    g_, b_, be_, m_, v_ = (bnc[:, l, v, :] for v in range(5))
                    f_step(dve.tensor_scalar(v_, v_, BN_EPS, None, ALU.add))
                    inverse_root(dve, f_step, bnt[:, l, 0, :], v_, bnt[:, l, 1, :])
                    f_step(dve.tensor_tensor(bn[:, l, 0, :], bnt[:, l, 0, :], g_, ALU.mult))
                    f_step(dve.tensor_tensor(bnt[:, l, 1, :], b_, m_, ALU.subtract))
                    f_step(dve.tensor_tensor(bnt[:, l, 1, :], bnt[:, l, 1, :], bn[:, l, 0, :], ALU.mult))
                    f_step(dve.tensor_tensor(bn[:, l, 1, :], bnt[:, l, 1, :], be_, ALU.add))
                inverse_root(dve, f_step, hbound[:, :], fl[:, 3:4], fl[:, 2:3])
                f_step(dve.tensor_tensor(hbound[:, :], hbound[:, :], fl[:, 3:4], ALU.mult))
                f_step(dve.tensor_scalar(hbound[:, :], hbound[:, :], 1.51, 1.0, ALU.mult, ALU.add))
                f_step(dve.tensor_scalar(nbound[:, :], hbound[:, :], -1.0, None, ALU.mult))
                rel3 = relw[:, :].rearrange("p (t c) -> p t c", t=NT)
                f_step(dve.tensor_tensor(rel3, rel3, col(thr[:, :], CH), ALU.subtract))
                f_step(dve.tensor_scalar(ge, relw[:, :], 0.0, None, ALU.is_ge))
                f_step(dve.tensor_scalar(lt, relw[:, :], float(T), None, ALU.is_lt))
                f_step(dve.tensor_tensor(ge, ge, lt, ALU.mult))
                dve.tensor_reduce(fl[:, 0:1], ge, AX, ALU.add).then_inc(f_found, 1)
                dve.wait_ge(s_match, 1)
                f_step(dve.tensor_scalar(fl[:, 1:2], ps[7][:, 0:1], float(E), None, ALU.not_equal))
                f_step(dve.tensor_scalar(fl[:, 2:3], fl[:, 1:2], -1.0, 1.0, ALU.mult, ALU.add))
                f_step(dve.tensor_scalar(relw[:, :], relw[:, :], fl[:, 2:3], fl[:, 1:2], ALU.mult, ALU.subtract))
                f_step(dve.tensor_copy(flag[:, :], fl[0:1, 1:2]))

            @block.tensor
            def _(pe):
                pe.wait_ge(f_copied, 3)
                for q in range(4):
                    last = pe.matmul(ps[q // 2][:, (q % 2) * D:(q % 2) * D + D], dsb[:, q, :], woutT[:, q, :],
                                     start=True, stop=True)
                last.then_inc(f_product, 1)
                pe.wait_ge(f_copied, 5)
                for k in range(KD):
                    for q in range(4):
                        last = pe.matmul(ps[2][:, k * D:k * D + D], wqkv0[:, q, k * P:k * P + P], gsb[:, q, :],
                                         start=(q == 0), stop=(q == 3))
                last.then_inc(f_product, 1)
                pe.wait_ge(f_found, 1)
                pe.matmul(ps[7][:, 0:1], ones[:, :], fl[:, 0:1], start=True, stop=True).then_inc(s_match, 1)

            @block.sync
            def _(sp):
                sp.wait_ge(f_product, 2)
                for w, name in ((W1, "L0_ffn_W1"), (W2, "L0_ffn_W2")):
                    sp.dma_start(w[:, :, :, :], a[name].rearrange("e (k p) d -> p e k d", p=P))\
                        .then_inc(load_experts0, 16)

        g_seen = sem("g_edges_seen")
        g_load = sem("g_edges_loaded")
        g_rows = sem("g_rows_gathered")
        g_sums = sem("g_sums")
        g_dve = sem("g_vector_steps")
        g_out = sem("g_mean_stored")
        sweep_e = sb("sweep_e", [T, 2, SWEEP_CH], I32)
        sweep_r = sb("sweep_r", [T, SWEEP_CH])
        G_CLEAR, G_STEP, G_END = 2, 4, 4
        G_TILE = G_CLEAR + SWEEPS * G_STEP + G_END

        def sweep_loads(sp, w, load):
            sp.dma_start(sweep_e[:, 0, :], a["src"][bass.ds(w * SWEEP, SWEEP)].rearrange("(p c) -> p c", p=T))\
                .then_inc(load, 16)
            sp.dma_start(sweep_e[:, 1, :], a["dst"][bass.ds(w * SWEEP, SWEEP)].rearrange("(p c) -> p c", p=T))\
                .then_inc(load, 16)

        def flagged(engine):
            return engine.If(engine.value_load(flag[0:1, 0:1], min_val=0, max_val=1) != 0)

        with nc.Block() as block:
            @block.sync
            def _(sp):
                with flagged(sp):
                    with sp.Fori(0, NT) as t:
                        with sp.Fori(0, SWEEPS) as w:
                            sp.wait_ge(made, 1)
                            sp.wait_ge(g_sums, t * SWEEPS + w)
                            sweep_loads(sp, w, g_load)
                        sp.wait_ge(made, 1)
                        sp.wait_ge(g_dve, G_TILE * (t + 1))
                        sp.dma_start(nslow_d[bass.ds(t * T, T), :], hn[:, 0, :]).then_inc(g_out, 16)
                    sp.wait_ge(g_out, 16 * NT)

            @block.gpsimd
            def _(pool):
                with flagged(pool):
                    with pool.Fori(0, NT) as t:
                        with pool.Fori(0, SWEEPS) as w:
                            n = t * SWEEPS + w
                            pool.wait_ge(g_seen, 2 * n)
                            wait_apart(pool, g_load, 32 * (n + 1)).then_inc(g_seen, 1)
                            for c in range(SWEEP_CH):
                                pool.indirect_dma_start(
                                    ring16[0:T, 0, c, 0:2 * D], None, xtab,
                                    bass.IndirectOffsetOnAxis(ap=sweep_e[:, 0, c:c + 1], axis=0)).then_inc(g_rows, 16)
                            wait_apart(pool, g_sums, n + 1).then_inc(g_seen, 1)
                            wait_apart(pool, g_seen, 2 * n + 2)
                            pool.inc_swdge_sem([g_rows], [16 * SWEEP_CH], mode="sub")

            @block.vector
            def _(dve):
                with flagged(dve):
                    with dve.Fori(0, NT) as t:
                        done = [0]

                        def step(ins, before=t * G_TILE):
                            done[0] += 1
                            ins.then_inc(g_dve, 1)
                            dve.wait_ge(g_dve, before + done[0])

                        step(dve.memset(tmp[:, :, :], 0.0))
                        step(dve.memset(sm[:, 0, :], 0.0))
                        assert done[0] == G_CLEAR
                        carry(dve)
                        with dve.Fori(0, SWEEPS) as w:
                            done[0] = 0
                            n = t * SWEEPS + w
                            before = t * G_TILE + G_CLEAR + w * G_STEP
                            dve.wait_ge(g_load, 32 * (n + 1))
                            step(dve.tensor_scalar(sweep_r[:, :], sweep_e[:, 1, :], thr[0:T, bass.ds(t, 1)], None,
                                                   ALU.subtract), before)
                            step(dve.tensor_tensor(hot[0:T, 0, 0:SWEEP_CH, :], col(sweep_r[:, :], T),
                                                   mid(iota[0:T, :], SWEEP_CH), ALU.is_equal), before)
                            dve.wait_ge(g_sums, n + 1)
                            step(dve.tensor_tensor(tmp[:, :, :], tmp[:, :, :],
                                                   ps[0][0:T, :].rearrange("p (u d) -> p u d", u=2), ALU.add), before)
                            step(dve.tensor_tensor(sm[:, 0, 0:1], sm[:, 0, 0:1], ps[7][0:T, 0:1], ALU.add), before)
                            assert done[0] == G_STEP
                        done[0] = 0
                        before = t * G_TILE + G_CLEAR + SWEEPS * G_STEP
                        step(dve.tensor_scalar(sm[:, 1, 0:1], sm[:, 0, 0:1], 1.0, None, ALU.max), before)
                        step(dve.reciprocal(sm[:, 1, 0:1], sm[:, 1, 0:1]), before)
                        step(dve.tensor_tensor(tmp[:, 0, :], tmp[:, 0, :], tmp[:, 1, :], ALU.add), before)
                        dve.wait_ge(g_out, 16 * t)
                        step(dve.tensor_scalar(hn[:, 0, :], tmp[:, 0, :], sm[:, 1, 0:1], None, ALU.mult), before)
                        assert done[0] == G_END

            @block.tensor
            def _(pe):
                with flagged(pe):
                    with pe.Fori(0, NT) as t:
                        with pe.Fori(0, SWEEPS) as w:
                            n = t * SWEEPS + w
                            pe.wait_ge(g_seen, 2 * n + 1)
                            pe.matmul(ps[6][0:1, 0:1], ones16[0:T, :], ones16[0:T, :], start=True, stop=True)
                            pe.wait_ge(g_rows, 16 * SWEEP_CH)
                            pe.wait_ge(g_dve, t * G_TILE + G_CLEAR + w * G_STEP + 2)
                            for c in range(SWEEP_CH):
                                pe.matmul(ps[7][0:T, 0:1], hot[0:T, 0, c, :], ones16[0:T, :],
                                          start=(c == 0), stop=(c == SWEEP_CH - 1))
                            for c in range(SWEEP_CH):
                                last = pe.matmul(ps[0][0:T, :], hot[0:T, 0, c, :], ring16[0:T, 0, c, 0:2 * D],
                                                 start=(c == 0), stop=(c == SWEEP_CH - 1))
                            last.then_inc(g_sums, 1)

        b_x = sem("b_x_loaded")
        b_xT = sem("b_xT_loaded")
        b_base = sem("b_sweep_mean_loaded")
        b_hot = sem("b_one_hot")
        b_xb = sem("b_x_bias")
        b_cnt = sem("b_count_reciprocal_steps")
        b_router = sem("b_router_steps")
        b_mag = sem("b_magnitude_steps")
        b_s1 = sem("b_low_mean")
        b_hn = sem("b_neighbour_mean")
        b_hnTp = sem("b_mean_turned")
        b_hnT = sem("b_mean_turned_copied")
        b_lin = sem("b_linear")
        b_x1 = sem("b_x1")
        b_xf = sem("b_x1_expert_biases")
        b_norm = sem("b_x1_norm_steps")
        b_nb = sem("b_x1_shift")
        b_u = sem("b_x1_normalized")
        b_uTp = sem("b_x1_turned")
        b_uT = sem("b_uT")
        b_in = sem("b_experts_input")
        b_lg = sem("b_logits")
        b_zs = sem("b_logits_less_max")
        b_e = sem("b_router_exp")
        b_w = sem("b_router_weights")
        b_wE = sem("b_weights_kept")
        b_wTp = sem("b_weights_turned")
        b_wT = sem("b_weights_turned_copied")
        b_bo = sem("b_expert_biases")
        b_A = sem("b_hidden1_product")
        b_h1 = sem("b_hidden1")
        b_B = sem("b_hidden2_product")
        b_h2 = sem("b_hidden2")
        b_Y = sem("b_expert_out")
        b_acc = sem("b_expert_added")
        b_x2s = sem("b_x2_stored")
        b_normp = sem("b_x2_norm_steps")
        b_nbp = sem("b_x2_shift")
        b_up = sem("b_x2_normalized")
        b_x2Tp = sem("b_x2_turned")
        b_x2T = sem("b_x2T")
        b_x2Ts = sem("b_x2T_stored")
        b_hr = sem("b_h_raw")
        b_kv = sem("b_k_v")
        b_hb = sem("b_h_bias")
        b_ss = sem("b_h_squares")
        b_ext = sem("b_magnitude_and_scores")
        b_me = sem("b_magnitude_exp")
        b_h = sem("b_h")
        b_hs = sem("b_h_stored")
        b_kc = sem("b_k_v_copied")
        x2T = sb("x2T", [P, KD, TP])
        uTf = sb("uTf", [P, KD, TP])
        xf = late[0:T, :].rearrange("p (u d) -> p u d", u=2)
        x2b = M1[0:T, :, :]
        xnp = lay[0:T, :].rearrange("p (u d) -> p u d", u=2)
        tmpp = zeros[0:T, :].rearrange("p (u d) -> p u d", u=2)
        smp = sb("smp", [T, 8, 2])
        stp = sb("stp", [T, 2, 6])
        mvp = sb("mvp", [T, 2, 2])
        wE = sb("wE", [T, 2, EX])
        ext = sb("ext", [T, 2, 3])
        hots = sb("hots", [P, 2, T], F16)
        KV_EXT = TP + 2 * HID1
        CNT = 504

        with nc.Block() as block:
            @block.sync
            def _(sp):
                def load_front(i):
                    wait(sp, made, 1)
                    wait(sp, b_hn, 2 * i)
                    sp.dma_start(base[:, :, :], pair_rows(nslow_d, i)).then_inc(b_base, 16)
                    wait(sp, made, 1)
                    wait(sp, b_xb, i)
                    sp.dma_start(xin[:, :, :], pair_rows(a["x"], i)).then_inc(b_x, 16)
                    wait(sp, made, 1)
                    wait(sp, b_lin, i)
                    sp.dma_start(xT[:, :, :], xnT_d[:, :, bass.ds(i * TP, TP)]).then_inc(b_xT, 16)

                def store_x2(p):
                    wait(sp, made, 1)
                    wait(sp, b_acc, 2 * EX * (p + 1))
                    sp.dma_start(pair_rows(x2_d, p), x2b[:, :, :]).then_inc(b_x2s, 16)
                    wait(sp, made, 1)
                    wait(sp, b_x2T, p + 1)
                    sp.dma_start(xn2T_d[:, :, bass.ds(p * TP, TP)], x2T[:, :, :]).then_inc(b_x2Ts, 16)

                def store_h(p):
                    wait(sp, made, 1)
                    wait(sp, b_h, 3 * (p + 1))
                    sp.dma_start(pair_rows(htab, p), hrow[:, :, :]).then_inc(b_hs, 16)
                    sp.dma_start(pair_rows(hbase_d, p), hrow[:, :, 0:D]).then_inc(b_hs, 16)

                def body(j, front, post, ahead):
                    if post:
                        store_x2(j - 1)
                    if ahead:
                        load_front(j + 2)
                    if post:
                        store_h(j - 1)

                load_front(0)
                load_front(1)
                pipeline(sp, body)
                store_x2(LAST)
                store_h(LAST)
                sp.wait_ge(b_x2s, 16 * PAIRS)
                sp.wait_ge(b_x2Ts, 16 * PAIRS)
                sp.wait_ge(b_hs, 32 * PAIRS)

            @block.gpsimd
            def _(pool):
                with pool.Fori(1, PAIRS) as i:
                    gather_x(pool, i)

            @block.tensor
            def _(pe):
                def hidden(w, rhs, e, bank, done):
                    for m in range(KD):
                        for k in range(KD):
                            last = pe.matmul(ps[bank][:, m * D:m * D + TP], w[:, e, k, m * P:m * P + P],
                                             rhs[:, k, :], start=(k == 0), stop=(k == KD - 1))
                    last.then_inc(done, 1)

                def segment_sums(i, tiles=(0, 1)):
                    for u in tiles:
                        t = i * 2 + u
                        wait(pe, b_rows[u], 16 * CH * (i + 1))
                        wait(pe, b_hot, 2 * t + 2)
                        wait(pe, b_router, 4 * i)
                        wait(pe, b_xf, i)
                        wait(pe, b_wT, i)
                        for c in range(CH):
                            pe.matmul(ps[u][0:T, :], hot[:, u, c, :], ring16[:, u, c, 0:2 * D],
                                      start=(c == 0), stop=(c == CH - 1))
                        pe.matmul(ps[7][0:T, CNT + u:CNT + u + 1], hots[:, u, :], ones16[:, :],
                                  start=True, stop=True).then_inc(b_seg, 1)

                def turn_mean(i):
                    wait(pe, b_hn, 2 * i + 2)
                    wait(pe, b_cnt, 2 * i + 1)
                    transpose_pair(pe, 7, hn).then_inc(b_hnTp, 1)

                def linear(i):
                    wait(pe, b_xT, 16 * (i + 1))
                    wait(pe, b_hnT, i + 1)
                    for u in range(2):
                        for k in range(2 * KD):
                            src = xT if k < KD else hnT
                            last = pe.matmul(ps[0][0:T, u * D:u * D + D], src[:, k % KD, u * T:u * T + T],
                                             WL[:, k, :], start=(k == 0), stop=(k == 2 * KD - 1))
                    last.then_inc(b_lin, 1)

                def turn_x1(i):
                    wait(pe, b_u, 2 * i + 2)
                    transpose_pair(pe, 7, xn).then_inc(b_uTp, 1)

                def logits(i):
                    wait(pe, b_uT, i + 1)
                    for u in range(2):
                        for k in range(KD):
                            last = pe.matmul(ps[1][0:T, EX * u:EX * u + EX], uTf[:, k, u * T:u * T + T],
                                             Wr[:, k, :], start=(k == 0), stop=(k == KD - 1))
                    last.then_inc(b_lg, 1)

                def turn_weights(i):
                    wait(pe, b_w, i + 1)
                    for u in range(2):
                        last = pe.transpose(ps[7][0:EX, u * T:u * T + T], lg[:, 5, u, :], ident[0:T, 0:T])
                    last.then_inc(b_wTp, 1)

                def expert_biases(i):
                    wait(pe, b_wT, i + 1)
                    wait(pe, b_x1, i + 1)
                    for u in range(2):
                        last = pe.matmul(ps[0][0:T, u * D:u * D + D], wT[:, u * T:u * T + T], bo[:, :],
                                         start=True, stop=True)
                    last.then_inc(b_bo, 1)

                def turn_x2(p):
                    wait(pe, b_up, 2 * p + 2)
                    wait(pe, b_hb, p)
                    transpose_pair(pe, 6, xnp).then_inc(b_x2Tp, 1)

                def keys_values(p):
                    wait(pe, b_x2T, p + 1)
                    for k in range(KD):
                        pe.matmul(ps[6][:, 0:TP], wqkv1[:, k, HID1:2 * HID1], x2T[:, k, :],
                                  start=(k == 0), stop=(k == KD - 1))
                    for u in range(2):
                        for k in range(KD):
                            pe.matmul(ps[6][0:T, TP + u * HID1:TP + u * HID1 + HID1],
                                      x2T[:, k, u * T:u * T + T], wqkv1[:, k, 2 * HID1:3 * HID1],
                                      start=(k == 0), stop=(k == KD - 1))
                    for u in range(2):
                        for k in range(KD):
                            last = pe.matmul(ps[6][0:T, KV_EXT + 3 * u:KV_EXT + 3 * u + 3],
                                             x2T[:, k, u * T:u * T + T], wg3[:, k, :],
                                             start=(k == 0), stop=(k == KD - 1))
                    last.then_inc(b_kv, 1)

                def raw_h(p):
                    wait(pe, b_ext, p + 1)
                    wait(pe, b_kc, 2 * p + 2)
                    for u in range(2):
                        for k in range(KD):
                            last = pe.matmul(ps[6][0:T, u * D:u * D + D], x2T[:, k, u * T:u * T + T], wg[:, k, :],
                                             start=(k == 0), stop=(k == KD - 1))
                    last.then_inc(b_hr, 1)

                def front_all(i):
                    for stage in (segment_sums, turn_mean, linear, turn_x1, logits, turn_weights, expert_biases):
                        stage(i)

                def body(j, front, post, ahead):
                    fronts = {0: lambda i: segment_sums(i, (0,)), 1: lambda i: segment_sums(i, (1,)), 2: turn_mean, 3: linear, 5: turn_x1, 6: logits, 7: turn_weights,
                              8: expert_biases}
                    posts = {1: turn_x2, 2: keys_values, 4: raw_h}

                    def slot(s):
                        if post and s in posts:
                            posts[s](j - 1)
                        if front and s in fronts:
                            fronts[s](j + 1)

                    wait(pe, b_in, j + 1)
                    wait(pe, b_h1, 2 * EX * j)
                    hidden(W1, uT, 0, 2, b_A)
                    slot(0)
                    for e in range(EX):
                        n = EX * j + e
                        if e + 1 < EX:
                            wait(pe, b_h1, 2 * n + 2)
                            hidden(W1, uT, e + 1, 2, b_A)
                        wait(pe, b_h1, 2 * n + 2)
                        wait(pe, b_h2, 2 * n)
                        hidden(W2, h1, e, 3, b_B)
                        if e:
                            out_of(j, e - 1)
                        slot(e + 1)
                    out_of(j, EX - 1)

                def out_of(j, e):
                    n = EX * j + e
                    wait(pe, b_h2, 2 * n + 2)
                    wait(pe, b_acc, 2 * (n - 1))
                    for u in range(2):
                        for k in range(KD):
                            last = pe.matmul(ps[4 + e % 2][0:T, u * D:u * D + D], h2[:, k, u * T:u * T + T],
                                             Wo[:, e, k, :], start=(k == 0), stop=(k == KD - 1))
                    last.then_inc(b_Y, 1)

                front_all(0)
                pe.wait_ge(load_experts0, 48)
                pipeline(pe, body)
                for stage in (turn_x2, keys_values, raw_h):
                    stage(LAST)

            @block.scalar
            def _(act):
                def copy_mean(i):
                    wait(act, b_hnTp, i + 1)
                    act.copy(hnT[:, :, :], turned_pair(7)).then_inc(b_hnT, 1)

                def normalize_x1(i):
                    wait(act, b_nb, i + 1)
                    for u in range(2):
                        act.activation(xn[:, u, :], xf[:, u, :], ACT.Identity, bias=nb[:, u:u + 1],
                                       scale=rs[:, u:u + 1]).then_inc(b_u, 1)

                def copy_x1(i):
                    wait(act, b_uTp, i + 1)
                    wait(act, b_in, i)
                    act.copy(uTf[:, :, :], turned_pair(7)).then_inc(b_uT, 1)

                def router_exp(i):
                    wait(act, b_zs, i + 1)
                    act.activation(lg[:, 2, :, :], lg[:, 1, :, :], ACT.Exp).then_inc(b_e, 1)

                def hand_on(i):
                    wait(act, b_uT, i + 1)
                    wait(act, b_lg, i + 1)
                    wait(act, b_A, EX * i)
                    act.copy(uT[:, :, :], uTf[:, :, :]).then_inc(b_in, 1)

                def copy_weights(i):
                    wait(act, b_wTp, i + 1)
                    act.copy(wT[:, :], ps[7][0:EX, 0:TP]).then_inc(b_wT, 1)

                def normalize_x2(p):
                    wait(act, b_nbp, p + 1)
                    for u in range(2):
                        act.activation(xnp[:, u, :], x2b[:, u, :], ACT.Identity, bias=smp[:, 7, u:u + 1],
                                       scale=smp[:, 6, u:u + 1]).then_inc(b_up, 1)

                def copy_x2(p):
                    wait(act, b_x2Tp, p + 1)
                    wait(act, b_x2Ts, 16 * p)
                    act.copy(x2T[:, :, :], turned_pair(6)).then_inc(b_x2T, 1)

                def copy_keys_values(p):
                    wait(act, b_kv, p + 1)
                    act.copy(kT_all[:, bass.ds(p * TP, TP)], ps[6][:, 0:TP]).then_inc(b_kc, 1)
                    act.copy(v_all[:, bass.ds(p * 2, 2), :],
                             ps[6][0:T, TP:TP + 2 * HID1].rearrange("p (u d) -> p u d", u=2)).then_inc(b_kc, 1)

                def magnitude_exp(p):
                    wait(act, b_ext, p + 1)
                    act.activation(smp[:, 0, :], ext[:, :, 0], ACT.Exp, scale=-1.0).then_inc(b_me, 1)

                def relu(j, e, bank, layer, target, product, free, free_at, done):
                    wait(act, product, EX * j + e + 1)
                    wait(act, free, free_at)
                    for m in range(KD):
                        act.activation(target[:, m, :], ps[bank][:, m * D:m * D + TP], ACT.Relu,
                                       bias=bn[:, layer, 1, 2 * e + m:2 * e + m + 1],
                                       scale=bn[:, layer, 0, 2 * e + m:2 * e + m + 1]).then_inc(done, 1)

                def body(j, front, post, ahead):
                    fronts = {2: copy_mean, 4: normalize_x1, 5: copy_x1, 8: copy_weights}
                    posts = {0: normalize_x2, 1: copy_x2, 2: copy_keys_values, 3: magnitude_exp}

                    def slot(s):
                        if post and s in posts:
                            posts[s](j - 1)
                        if front and s in fronts:
                            fronts[s](j + 1)

                    relu(j, 0, 2, 0, h1, b_A, b_B, EX * j, b_h1)
                    slot(0)
                    for e in range(EX):
                        n = EX * j + e
                        if e + 1 < EX:
                            relu(j, e + 1, 2, 0, h1, b_A, b_B, n + 1, b_h1)
                            if e + 1 == EX - 1 and front:
                                router_exp(j + 1)
                        elif front:
                            copy_weights(j + 1)
                        relu(j, e, 3, 1, h2, b_B, b_Y, n, b_h2)
                        if e + 1 == EX - 1 and front:
                            hand_on(j + 1)
                        if e + 1 < EX:
                            slot(e + 1)

                copy_mean(0)
                normalize_x1(0)
                copy_x1(0)
                router_exp(0)
                hand_on(0)
                copy_weights(0)
                pipeline(act, body)
                normalize_x2(LAST)
                copy_x2(LAST)
                copy_keys_values(LAST)
                magnitude_exp(LAST)

            @block.vector
            def _(dve):
                POST_STEPS = NORM_STEPS + ROOT_STEPS

                def one_hot(i, u):
                    t = i * 2 + u
                    wait(dve, b_seg, t - 1)
                    dve.tensor_tensor(hot[:, u, :, :], col(relw[:, bass.ds(t * CH, CH)], T),
                                      mid(iota[:, :], CH), ALU.is_equal).then_inc(b_hot, 1)
                    wait(dve, b_hot, 2 * t + 1)
                    with nc.allow_low_precision("small whole numbers"):
                        dve.tensor_reduce(hots[:, u, :], hot[:, u, :, :].rearrange("p c d -> p d c"), AX, ALU.add)\
                            .then_inc(b_hot, 1)

                def mean(i):
                    wait(dve, b_x, 16 * (i + 1))
                    wait(dve, b_x1, i)
                    dve.tensor_tensor(tmp[:, :, :], xin[:, :, :], mid(bias0[:, :], 2), ALU.add).then_inc(b_xb, 1)
                    wait(dve, b_seg, 2 * i + 2)
                    dve.tensor_scalar(sm[:, 0, :], ps[7][0:T, CNT:CNT + 2], 1.0, None, ALU.max).then_inc(b_cnt, 1)
                    wait(dve, b_cnt, 2 * i + 1)
                    dve.reciprocal(sm[:, 1, :], sm[:, 0, :]).then_inc(b_cnt, 1)
                    wait(dve, b_cnt, 2 * i + 2)
                    wait(dve, b_base, 16 * (i + 1))
                    wait(dve, b_hnTp, i)
                    for u in range(2):
                        dve.scalar_tensor_tensor(base[:, u, :], ps[u][0:T, D:2 * D], sm[:, 1, u:u + 1], base[:, u, :],
                                                 ALU.mult, ALU.add).then_inc(b_s1, 1)
                    for u in range(2):
                        wait(dve, b_s1, 2 * i + u + 1)
                        dve.scalar_tensor_tensor(hn[:, u, :], ps[u][0:T, 0:D], sm[:, 1, u:u + 1], base[:, u, :],
                                                 ALU.mult, ALU.add).then_inc(b_hn, 1)

                def x1(i):
                    wait(dve, b_lin, i + 1)
                    wait(dve, b_xb, i + 1)
                    if not isinstance(i, int) or i > 0:
                        wait(dve, b_acc, 2 * EX * (i - 1) + 2)
                    dve.tensor_tensor(xf[:, :, :], tmp[:, :, :], bank2(0), ALU.add).then_inc(b_x1, 1)
                    wait(dve, b_x1, i + 1)
                    norm(dve, xf, st, mv, sm[:, 14, :], sm[:, 15, :], rs[:, :], nb[:, :], b_norm, NORM_STEPS * i,
                         (b_u, 2 * i), b_nb)

                def router(i):
                    wait(dve, b_lg, i + 1)
                    dve.tensor_tensor(lg[:, 0, :, :], ps[1][0:T, 0:2 * EX].rearrange("p (u e) -> p u e", u=2),
                                      mid(br[:, :], 2), ALU.add).then_inc(b_router, 1)
                    wait(dve, b_router, 4 * i + 1)
                    dve.tensor_reduce(sm[:, 2, :], lg[:, 0, :, :], AX, ALU.max).then_inc(b_router, 1)
                    wait(dve, b_router, 4 * i + 2)
                    dve.tensor_tensor(lg[:, 1, :, :], lg[:, 0, :, :], col(sm[:, 2, :], EX), ALU.subtract)\
                        .then_inc(b_zs, 1)
                    wait(dve, b_e, i + 1)
                    dve.tensor_reduce(sm[:, 3, :], lg[:, 2, :, :], AX, ALU.add).then_inc(b_router, 1)
                    wait(dve, b_router, 4 * i + 3)
                    dve.reciprocal(sm[:, 4, :], sm[:, 3, :]).then_inc(b_router, 1)
                    wait(dve, b_router, 4 * i + 4)
                    wait(dve, b_wE, i)
                    wait(dve, b_wTp, i)
                    dve.tensor_tensor(lg[:, 5, :, :], lg[:, 2, :, :], col(sm[:, 4, :], EX), ALU.mult).then_inc(b_w, 1)

                def add_biases(i):
                    wait(dve, b_bo, i + 1)
                    wait(dve, b_u, 2 * i + 2)
                    dve.tensor_tensor(xf[:, :, :], xf[:, :, :], bank2(0), ALU.add).then_inc(b_xf, 1)

                def keep_weights(j):
                    wait(dve, b_w, j + 1)
                    wait(dve, b_acc, 2 * EX * j)
                    dve.tensor_copy(wE[:, :, :], lg[:, 5, :, :]).then_inc(b_wE, 1)

                def add_expert(j, e):
                    n = EX * j + e
                    wait(dve, b_Y, n + 1)
                    if e == 0:
                        wait(dve, b_wE, j + 1)
                        wait(dve, b_xf, j + 1)
                    if e == EX - 1:
                        wait(dve, b_x2s, 16 * j)
                        wait(dve, b_up, 2 * j)
                    source = xf if e == 0 else acc
                    target = x2b if e == EX - 1 else acc
                    for u in range(2):
                        wait(dve, b_acc, 2 * n - 1 + u)
                        dve.scalar_tensor_tensor(target[:, u, :], bank2(4 + e % 2)[:, u, :], wE[:, u, e:e + 1],
                                                 source[:, u, :], ALU.mult, ALU.add).then_inc(b_acc, 1)

                def norm_x2(p):
                    wait(dve, b_acc, 2 * EX * (p + 1))
                    norm(dve, x2b, stp, mvp, smp[:, 4, :], smp[:, 5, :], smp[:, 6, :], smp[:, 7, :], b_normp,
                         POST_STEPS * p, (b_up, 2 * p), b_nbp)

                def extras(p):
                    wait(dve, b_kv, p + 1)
                    wait(dve, b_kc, 2 * p + 2)
                    dve.tensor_tensor(ext[:, :, :], ps[6][0:T, KV_EXT:KV_EXT + 6].rearrange("p (u c) -> p u c", u=2),
                                      mid(c3[:, :], 2), ALU.add).then_inc(b_ext, 1)

                def squares(p):
                    wait(dve, b_hr, p + 1)
                    wait(dve, b_h, 3 * p)
                    dve.tensor_tensor(tmpp[:, :, :], bank2(6), mid(gb[:, :], 2), ALU.add).then_inc(b_hb, 1)
                    wait(dve, b_hb, p + 1)
                    wait(dve, b_x2Tp, p + 1)
                    for u in range(2):
                        dve.tensor_tensor_reduce(xnp[:, u, :], tmpp[:, u, :], tmpp[:, u, :], 1.0, 0.0, ALU.mult,
                                                 ALU.add, smp[:, 1, u:u + 1]).then_inc(b_ss, 1)

                def scaled_h(p):
                    wait(dve, b_ss, 2 * p + 2)
                    steps = [0]

                    def step(ins):
                        steps[0] += 1
                        ins.then_inc(b_normp, 1)
                        dve.wait_ge(b_normp, POST_STEPS * p + NORM_STEPS + steps[0])
                    inverse_root(dve, step, smp[:, 2, :], smp[:, 1, :], smp[:, 3, :])
                    dve.tensor_scalar(smp[:, 2, :], smp[:, 2, :], 1e12, None, ALU.min).then_inc(b_mag, 1)
                    wait(dve, b_me, p + 1)
                    dve.tensor_scalar(smp[:, 3, :], smp[:, 0, :], 1.0, None, ALU.add).then_inc(b_mag, 1)
                    wait(dve, b_mag, 4 * p + 2)
                    dve.reciprocal(smp[:, 3, :], smp[:, 3, :]).then_inc(b_mag, 1)
                    wait(dve, b_mag, 4 * p + 3)
                    dve.scalar_tensor_tensor(smp[:, 3, :], smp[:, 3, :], 1.5, smp[:, 2, :], ALU.mult, ALU.mult)\
                        .then_inc(b_mag, 1)
                    wait(dve, b_mag, 4 * p + 4)
                    wait(dve, b_hs, 32 * p)
                    dve.tensor_tensor(ht_all[:, bass.ds(p * 2, 2)], ext[:, :, 2], smp[:, 3, :], ALU.mult)\
                        .then_inc(b_h, 1)
                    dve.tensor_tensor(hrow[:, :, D + 1], ext[:, :, 1], smp[:, 3, :], ALU.mult).then_inc(b_h, 1)
                    dve.tensor_tensor(hrow[:, :, 0:D], tmpp[:, :, :], col(smp[:, 3, :], D), ALU.mult).then_inc(b_h, 1)

                def body(j, front, post, ahead):
                    keep_weights(j)
                    if post:
                        norm_x2(j - 1)
                    if front:
                        mean(j + 1)
                    if ahead:
                        one_hot(j + 2, 0)
                    add_expert(j, 0)
                    if post:
                        extras(j - 1)
                    if ahead:
                        one_hot(j + 2, 1)
                    add_expert(j, 1)
                    if front:
                        x1(j + 1)
                    add_expert(j, 2)
                    if post:
                        squares(j - 1)
                    add_expert(j, 3)
                    if post:
                        scaled_h(j - 1)
                    add_expert(j, 4)
                    if front:
                        router(j + 1)
                    add_expert(j, 5)
                    add_expert(j, 6)
                    if front:
                        add_biases(j + 1)
                    add_expert(j, 7)

                one_hot(0, 0)
                one_hot(0, 1)
                mean(0)
                x1(0)
                router(0)
                add_biases(0)
                one_hot(1, 0)
                one_hot(1, 1)
                pipeline(dve, body)
                norm_x2(LAST)
                extras(LAST)
                squares(LAST)
                scaled_h(LAST)

        M_SLOTS = 5
        wo_flat = Wo[:, :, :, :].rearrange("p e k d -> p (e k d)")
        ek = wo_flat[:, 0:M_SLOTS * TP].rearrange("p (s n) -> p s n", s=M_SLOTS)
        ekT = wo_flat[0:T, 1280:1280 + M_SLOTS * 2 * HID1].rearrange("p (s d) -> p s d", s=M_SLOTS)
        ctxs = wo_flat[:, 2560:2560 + P]
        ctxT = wo_flat[:, 2688:2688 + P]
        g1 = wo_flat[:, 2816:2816 + D]
        m_banks = (0, 3, 4, 5, 6)
        c_x = again(b_x)
        c_xT = again(b_xT)
        c_base = again(b_base)
        c_idx = again(b_idx)
        c_rows = [sem("c_rows_gathered_0"), sem("c_rows_gathered_1")]
        c_hot = again(b_hot)
        c_xb = again(b_xb)
        c_hk = again(b_seg)
        c_V = again(b_cnt)
        c_vm = again(b_router)
        c_vT = again(b_mag)
        c_chain = again(b_hn)
        c_dg = again(b_hnTp)
        c_row = again(b_hnT)
        c_E = again(b_lin)
        c_P = again(b_x1)
        c_agg = again(b_xf)
        c_se = again(b_norm)
        c_hc = again(b_nb)
        c_ss = again(b_u)
        c_ball = again(b_uTp)
        c_th = again(b_uT)
        c_lin = again(b_lg)
        c_x3 = again(b_zs)
        c_norm = again(b_w)
        c_nb = again(b_wE)
        c_u = again(b_wTp)
        c_uTp = again(b_wT)
        c_uT = again(b_bo)
        c_lg = again(b_A)
        c_zs = again(b_h1)
        c_e = again(b_B)
        c_top = again(b_h2)
        c_w = again(b_Y)
        c_w2 = again(b_acc)
        c_wTp = again(b_x2s)
        c_wT = again(b_normp)
        c_b2 = again(b_nbp)
        c_A = again(b_up)
        c_g = again(b_x2Tp)
        c_Y = again(b_x2T)
        c_acc = again(b_x2Ts)
        c_out = again(b_hr)
        c_in = again(b_s1)
        c_wE = again(b_in)
        BALL_NORM = ROOT_STEPS + 2
        BALL_STEPS = ROOT_STEPS + 10
        TOP_STEPS = 18
        m_max = sem("m_k_max")
        m_e = sem("m_k_exp")
        m_t = sem("m_k_turned")
        m_c = sem("m_k_turned_copied")
        m_ctx = sem("m_context")
        m_copied = sem("m_copied")
        m_product = sem("m_product")
        def gather_h(pool, i):
            for u in range(2):
                t = i * 2 + u
                wait(pool, c_agg, t - 1)
                wait(pool, c_rows[u], 16 * CH * i)
                pool.tensor_copy(idx[:, u, :], srcw[:, bass.ds(t * CH, CH)]).then_inc(c_idx, 1)
                wait_apart(pool, c_idx, t + 1)
                for c in range(CH):
                    pool.indirect_dma_start(
                        ring[:, u, c, :], None, htab,
                        bass.IndirectOffsetOnAxis(ap=idx[:, u, c:c + 1], axis=0)).then_inc(c_rows[u], 16)

        with nc.Block() as block:
            @block.sync
            def _(sp):
                sp.dma_start(wout1, a["L1_mix_W_out"]).then_inc(load_experts1, 16)
                sp.dma_start(bias1, a["L1_mix_b_out"].rearrange("(o n) -> o n", o=1).to_broadcast([T, D]))\
                    .then_inc(load_experts1, 16)
                for w, name in ((W1, "L1_ffn_w1"), (W2, "L1_ffn_w2")):
                    sp.dma_start(w[:, :, :, :], a[name].rearrange("e (k p) d -> p e k d", p=P))\
                        .then_inc(load_experts1, 16)

            @block.gpsimd
            def _(pool):
                for semaphore in reused:
                    pool.sem_clear(semaphore)
                gather_h(pool, 0)
                for u in range(2):
                    wait_apart(pool, c_rows[u], 16 * CH)

            @block.vector
            def _(dve):
                dve.memset(zeros[:, 0:P], 0.0).then_inc(m_copied, 1)
                dve.memset(ctxs, 0.0).then_inc(m_copied, 1)
                dve.tensor_reduce(fl[:, 0:1], kT_all[:, :], AX, ALU.max).then_inc(m_max, 1)
                dve.wait_ge(m_max, 1)
                dve.tensor_scalar(fl[:, 1:2], fl[:, 0:1], -1.0, None, ALU.mult).then_inc(m_max, 1)

                def body(i):
                    for s in range(M_SLOTS):
                        n = M_SLOTS * i + s
                        wait(dve, m_t, n + 1)
                        wait(dve, m_ctx, M_SLOTS * (i - 1) + s + 1)
                        dve.tensor_copy(ekT[:, s, :], ps[m_banks[s]][0:T, 0:2 * HID1]).then_inc(m_c, 1)
                body(0)
                with dve.Fori(1, PAIRS // M_SLOTS) as i:
                    body(i)
                dve.wait_ge(m_ctx, PAIRS)
                dve.reciprocal(fl[:, 2:3], ps[2][:, 0:1]).then_inc(m_copied, 1)
                dve.wait_ge(m_copied, 3)
                for h in range(HEADS1):
                    r = slice(HD1 * h, HD1 * h + HD1)
                    dve.tensor_scalar(ctxs[r, r], ps[1][r, r], fl[r, 2:3], HD1 ** -0.5, ALU.mult, ALU.mult)\
                        .then_inc(m_copied, 1)
                dve.wait_ge(m_product, 1)
                dve.tensor_copy(ctxT, ps[3][:, 0:P]).then_inc(m_copied, 1)
                dve.wait_ge(m_product, 2)
                dve.tensor_copy(g1, ps[4][:, 0:D]).then_inc(m_copied, 1)
                dve.wait_ge(m_product, 3)
                dve.tensor_copy(M1[:, :, :], ps[5][:, :].rearrange("p (k d) -> p k d", k=KD)).then_inc(m_copied, 1)

            @block.scalar
            def _(act):
                act.wait_ge(m_max, 2)

                def body(i):
                    for s in range(M_SLOTS):
                        n = M_SLOTS * i + s
                        wait(act, m_t, M_SLOTS * (i - 1) + s + 1)
                        act.activation(ek[:, s, :], kT_all[:, bass.ds(n * TP, TP)], ACT.Exp,
                                       bias=fl[:, 1:2]).then_inc(m_e, 1)
                body(0)
                with act.Fori(1, PAIRS // M_SLOTS) as i:
                    body(i)

            @block.tensor
            def _(pe):
                pe.wait_ge(m_copied, 1)
                pe.matmul(ps[1][:, 0:HID1], zeros[:, 0:P], zeros[:, 0:HID1], start=True, stop=False,
                          skip_group_check=True)
                pe.matmul(ps[2][:, 0:1], zeros[:, 0:P], zeros[:, 0:1], start=True, stop=False,
                          skip_group_check=True)

                def turn(n, s):
                    wait(pe, m_e, n + 1)
                    wait(pe, m_c, n - M_SLOTS + 1)
                    for u in range(2):
                        last = pe.transpose(ps[m_banks[s]][0:T, u * HID1:(u + 1) * HID1],
                                            ek[:, s, u * T:u * T + T], ident[:, :])
                    last.then_inc(m_t, 1)

                def add(n, s):
                    wait(pe, m_c, n + 1)
                    for u in range(2):
                        pe.matmul(ps[1][:, 0:HID1], ekT[:, s, u * HID1:(u + 1) * HID1],
                                  v_all[:, bass.ds(n * 2 + u, 1), :], start=False, stop=False, skip_group_check=True)
                        last = pe.matmul(ps[2][:, 0:1], ekT[:, s, u * HID1:(u + 1) * HID1], ones[0:T, 0:1],
                                         start=False, stop=False, skip_group_check=True)
                    last.then_inc(m_ctx, 1)

                def body(i):
                    for s in range(M_SLOTS + 2):
                        if s < M_SLOTS:
                            turn(M_SLOTS * i + s, s)
                        if s >= 2:
                            add(M_SLOTS * i + s - 2, s - 2)
                body(0)
                with pe.Fori(1, PAIRS // M_SLOTS) as i:
                    body(i)
                pe.wait_ge(m_copied, 3 + HEADS1)
                pe.transpose(ps[3][:, 0:P], ctxs, ident[:, :]).then_inc(m_product, 1)
                pe.wait_ge(m_copied, 4 + HEADS1)
                pe.wait_ge(load_experts1, 64)
                pe.matmul(ps[4][:, 0:D], ctxT, wout1[:, :], start=True, stop=True).then_inc(m_product, 1)
                pe.wait_ge(m_copied, 5 + HEADS1)
                for k in range(KD):
                    last = pe.matmul(ps[5][:, k * D:k * D + D], wq1T[:, k, :], g1, start=True, stop=True)
                last.then_inc(m_product, 1)

        i_seen = sem("i_edges_seen")
        i_load = sem("i_edges_loaded")
        i_rows = sem("i_rows_gathered")
        i_pe = sem("i_tensor_steps")
        i_act = sem("i_scalar_steps")
        i_dve = sem("i_vector_steps")
        i_out = sem("i_h_stored")
        i_base = sem("i_h_loaded")
        I_CLEAR, I_STEP, I_END = 4, 17, 3
        I_TILE = I_CLEAR + SWEEPS * I_STEP + I_END
        I_MAXIMA, I_SHIFT, I_DIAG, I_WEIGHTS = 5, 13, 14, 15
        vm = lay[:, 0:2 * T].rearrange("p (u d) -> p u d", u=2)
        dg = lay[0:T, 2 * T:4 * T].rearrange("p (u d) -> p u d", u=2)
        hk = sb("hk", [P, 2, CH])
        hot1 = hot[0:T, 0, 0:SWEEP_CH, :]
        edge1 = big[0:T, 0, 0:SWEEP_CH, :]
        sums1 = tmp[:, :, :].rearrange("p u d -> p (u d)")[:, 0:D + 1]

        with nc.Block() as block:
            @block.sync
            def _(sp):
                with flagged(sp):
                    with sp.Fori(0, NT) as t:
                        sp.wait_ge(made, 1)
                        sp.wait_ge(i_out, 16 * t)
                        sp.dma_start(base[:, 0, :], hbase_d[bass.ds(t * T, T), :]).then_inc(i_base, 16)
                        with sp.Fori(0, SWEEPS) as w:
                            sp.wait_ge(made, 1)
                            sp.wait_ge(i_pe, 3 * (t * SWEEPS + w))
                            sweep_loads(sp, w, i_load)
                        sp.wait_ge(made, 1)
                        sp.wait_ge(i_dve, I_TILE * (t + 1))
                        sp.dma_start(hbase_d[bass.ds(t * T, T), :], hn[:, 0, :]).then_inc(i_out, 16)
                    sp.wait_ge(i_out, 16 * NT)

            @block.gpsimd
            def _(pool):
                with flagged(pool):
                    with pool.Fori(0, NT) as t:
                        with pool.Fori(0, SWEEPS) as w:
                            n = t * SWEEPS + w
                            pool.wait_ge(i_seen, 2 * n)
                            wait_apart(pool, i_load, 32 * (n + 1)).then_inc(i_seen, 1)
                            for c in range(SWEEP_CH):
                                pool.indirect_dma_start(
                                    ring[0:T, 0, c, :], None, htab,
                                    bass.IndirectOffsetOnAxis(ap=sweep_e[:, 0, c:c + 1], axis=0)).then_inc(i_rows, 16)
                            wait_apart(pool, i_pe, 3 * (n + 1)).then_inc(i_seen, 1)
                            wait_apart(pool, i_seen, 2 * n + 2)
                            pool.inc_swdge_sem([i_rows], [16 * SWEEP_CH], mode="sub")

            @block.scalar
            def _(act):
                with flagged(act):
                    with act.Fori(0, NT) as t:
                        with act.Fori(0, SWEEPS) as w:
                            n = t * SWEEPS + w
                            act.wait_ge(i_dve, t * I_TILE + I_CLEAR + w * I_STEP + I_SHIFT)
                            act.activation(sm[:, 7, 0:1], sm[:, 6, 0:1], ACT.Exp).then_inc(i_act, 1)
                            act.wait_ge(i_pe, 3 * n + 2)
                            for c in range(SWEEP_CH):
                                last = act.activation(big[0:T, 0, c, :], ps[3][0:T, 0:T], ACT.Exp,
                                                      bias=ring[0:T, 0, c, D + 1:D + 2])
                            last.then_inc(i_act, 1)

            @block.vector
            def _(dve):
                with flagged(dve):
                    with dve.Fori(0, NT) as t:
                        done = [0]

                        def step(ins, before=t * I_TILE):
                            done[0] += 1
                            ins.then_inc(i_dve, 1)
                            dve.wait_ge(i_dve, before + done[0])

                        step(dve.memset(tmp[:, :, :], 0.0))
                        step(dve.memset(sm[:, 0, :], 0.0))
                        step(dve.memset(sm[:, 5, :], 0.0))
                        step(dve.tensor_copy(sm[:, 8, 0:1], ht_all[:, bass.ds(t, 1)]))
                        assert done[0] == I_CLEAR
                        carry(dve)
                        with dve.Fori(0, SWEEPS) as w:
                            done[0] = 0
                            n = t * SWEEPS + w
                            before = t * I_TILE + I_CLEAR + w * I_STEP
                            dve.wait_ge(i_load, 32 * (n + 1))
                            dve.wait_ge(i_seen, 2 * n + 1)
                            step(dve.tensor_scalar(sweep_r[:, :], sweep_e[:, 1, :], thr[0:T, bass.ds(t, 1)], None,
                                                   ALU.subtract), before)
                            step(dve.tensor_tensor(hot1, col(sweep_r[:, :], T), mid(iota[0:T, :], SWEEP_CH),
                                                   ALU.is_equal), before)
                            dve.wait_ge(i_rows, 16 * SWEEP_CH)
                            step(dve.tensor_scalar(hk[0:T, 0, 0:SWEEP_CH], ring[0:T, 0, 0:SWEEP_CH, D + 1],
                                                   hbound[0:T, 0:1], None, ALU.add), before)
                            step(dve.tensor_tensor(edge1, hot1, col(hk[0:T, 0, 0:SWEEP_CH], T), ALU.mult), before)
                            step(dve.tensor_reduce(vm[0:T, 0, :], edge1.rearrange("p c d -> p d c"), AX, ALU.max),
                                 before)
                            assert done[0] == I_MAXIMA
                            dve.wait_ge(i_pe, 3 * n + 1)
                            step(dve.tensor_reduce(sm[:, 1, 0:1], ps[7][0:T, 0:T], AX, ALU.max), before)
                            step(dve.tensor_tensor(sm[:, 0, 0:1], sm[:, 0, 0:1], sm[:, 1, 0:1], ALU.max), before)
                            step(dve.tensor_scalar(sm[:, 2, 0:1], sm[:, 0, 0:1], nbound[0:T, 0:1], sm[:, 8, 0:1],
                                                   ALU.add, ALU.add), before)
                            step(dve.tensor_scalar(sm[:, 3, 0:1], sm[:, 2, 0:1], -1e9, None, ALU.max), before)
                            step(dve.tensor_tensor(sm[:, 4, 0:1], sm[:, 8, 0:1], sm[:, 3, 0:1], ALU.subtract), before)
                            step(dve.scalar_tensor_tensor(sm[:, 4, 0:1], sm[:, 0, 0:1], 0.0, sm[:, 4, 0:1],
                                                          ALU.is_gt, ALU.mult), before)
                            step(dve.tensor_tensor(sm[:, 6, 0:1], sm[:, 4, 0:1], sm[:, 5, 0:1], ALU.subtract), before)
                            step(dve.tensor_scalar(sm[:, 6, 0:1], sm[:, 6, 0:1], 0.0, None, ALU.min), before)
                            assert done[0] == I_SHIFT
                            step(dve.tensor_scalar(dg[:, 0, :], ident[0:T, 0:T], sm[:, 4, 0:1], None, ALU.mult),
                                 before)
                            assert done[0] == I_DIAG
                            dve.wait_ge(i_act, 2 * n + 2)
                            step(dve.scalar_tensor_tensor(edge1, edge1, FAR, hot1, ALU.min, ALU.mult), before)
                            assert done[0] == I_WEIGHTS
                            dve.wait_ge(i_pe, 3 * n + 3)
                            step(dve.scalar_tensor_tensor(sums1, sums1, sm[:, 7, 0:1], ps[0][0:T, 0:D + 1],
                                                          ALU.mult, ALU.add), before)
                            step(dve.tensor_copy(sm[:, 5, 0:1], sm[:, 4, 0:1]), before)
                            assert done[0] == I_STEP
                        done[0] = 0
                        before = t * I_TILE + I_CLEAR + SWEEPS * I_STEP
                        step(dve.tensor_scalar(sm[:, 9, 0:1], tmp[:, 1, 0:1], 1e-10, None, ALU.add), before)
                        step(dve.reciprocal(sm[:, 9, 0:1], sm[:, 9, 0:1]), before)
                        dve.wait_ge(i_base, 16 * (t + 1))
                        dve.wait_ge(i_out, 16 * t)
                        step(dve.scalar_tensor_tensor(hn[:, 0, :], tmp[:, 0, :], sm[:, 9, 0:1], base[:, 0, :],
                                                      ALU.mult, ALU.add), before)
                        assert done[0] == I_END

            @block.tensor
            def _(pe):
                with flagged(pe):
                    with pe.Fori(0, NT) as t:
                        with pe.Fori(0, SWEEPS) as w:
                            before = t * I_TILE + I_CLEAR + w * I_STEP
                            pe.wait_ge(i_dve, before + I_MAXIMA)
                            pe.transpose(ps[7][0:T, 0:T], vm[0:T, 0, :], ident[0:T, 0:T]).then_inc(i_pe, 1)
                            pe.wait_ge(i_dve, before + I_DIAG)
                            pe.matmul(ps[3][0:T, 0:T], ones[0:T, 0:T], dg[:, 0, :], start=True, stop=True)\
                                .then_inc(i_pe, 1)
                            pe.wait_ge(i_dve, before + I_WEIGHTS)
                            for c in range(SWEEP_CH):
                                last = pe.matmul(ps[0][0:T, 0:D + 1], big[0:T, 0, c, :], ring[0:T, 0, c, 0:D + 1],
                                                 start=(c == 0), stop=(c == SWEEP_CH - 1))
                            last.then_inc(i_pe, 1)

        v_flat = v_all[:, :, :].rearrange("p t d -> p (t d)")
        xf1, x4, squared = (v_flat[:, n * 2 * D:(n + 1) * 2 * D].rearrange("p (u d) -> p u d", u=2)
                            for n in range(3))

        with nc.Block() as block:
            @block.sync
            def _(sp):
                def load_front(i):
                    wait(sp, made, 1)
                    wait(sp, c_xb, i)
                    sp.dma_start(xin[:, :, :], pair_rows(x2_d, i)).then_inc(c_x, 16)
                    wait(sp, made, 1)
                    wait(sp, c_hc, 2 * i)
                    sp.dma_start(base[:, :, :], pair_rows(hbase_d, i)).then_inc(c_base, 16)
                    wait(sp, made, 1)
                    wait(sp, c_lin, i)
                    sp.dma_start(xT[:, :, :], xn2T_d[:, :, bass.ds(i * TP, TP)]).then_inc(c_xT, 16)

                def store(p):
                    wait(sp, made, 1)
                    wait(sp, c_acc, 2 * EX * (p + 1))
                    sp.dma_start(pair_rows(out, p), x4).then_inc(c_out, 16)

                def body(j, front, post, ahead):
                    if post:
                        store(j - 1)
                    if ahead:
                        load_front(j + 2)

                load_front(0)
                load_front(1)
                pipeline(sp, body)
                store(LAST)
                sp.wait_ge(c_out, 16 * PAIRS)

            @block.gpsimd
            def _(pool):
                with pool.Fori(1, PAIRS) as i:
                    gather_h(pool, i)

            @block.tensor
            def _(pe):
                def turn_max(i, u):
                    t = 2 * i + u
                    wait(pe, c_vm, t + 1)
                    wait(pe, c_E, CH * t)
                    pe.transpose(ps[3][0:T, 0:P], vm[:, u, :], ident[:, :]).then_inc(c_vT, 1)

                def shift_row(i, u):
                    wait(pe, c_dg, 2 * i + u + 1)
                    pe.matmul(ps[3][:, P:P + T], ones[0:T, :], dg[:, u, :], start=True, stop=True).then_inc(c_row, 1)

                def weighted_sums(i, u):
                    t = 2 * i + u
                    wait(pe, c_P, t + 1)
                    wait(pe, c_hc, t - 1)
                    for c in range(CH):
                        last = pe.matmul(ps[u][0:T, 0:D + 1], big[:, u, c, :], ring[:, u, c, 0:D + 1],
                                         start=(c == 0), stop=(c == CH - 1))
                    last.then_inc(c_agg, 1)

                def mixer(i):
                    wait(pe, c_xT, 16 * (i + 1))
                    wait(pe, c_x3, 5 * i)
                    for u in range(2):
                        for k in range(KD):
                            last = pe.matmul(ps[7][0:T, u * D:u * D + D], xT[:, k, u * T:u * T + T], M1[:, k, :],
                                             start=(k == 0), stop=(k == KD - 1))
                    last.then_inc(c_lin, 1)

                def turn_x3(i):
                    wait(pe, c_u, 2 * i + 2)
                    wait(pe, c_x3, 5 * i + 1)
                    transpose_pair(pe, 7, xn).then_inc(c_uTp, 1)

                def logits(i):
                    wait(pe, c_uT, i + 1)
                    for u in range(2):
                        for k in range(KD):
                            last = pe.matmul(ps[7][0:T, EX * u:EX * u + EX], uTf[:, k, u * T:u * T + T],
                                             rwT[:, k, :], start=(k == 0), stop=(k == KD - 1))
                    last.then_inc(c_lg, 1)

                def turn_weights(i):
                    wait(pe, c_w, i + 1)
                    for u in range(2):
                        last = pe.transpose(ps[7][0:EX, u * T:u * T + T], lg[:, 5, u, :], ident[0:T, 0:T])
                    last.then_inc(c_wTp, 1)

                def expert_biases(i):
                    wait(pe, c_wT, i + 1)
                    for u in range(2):
                        last = pe.matmul(ps[7][0:T, u * D:u * D + D], wT[:, u * T:u * T + T], b2[:, :],
                                         start=True, stop=True)
                    last.then_inc(c_b2, 1)

                def hidden(j, e):
                    wait(pe, c_g, 2 * (EX * j + e) - 2)
                    bank = 2 if e % 2 == 0 else 6
                    for m in range(KD):
                        for k in range(KD):
                            last = pe.matmul(ps[bank][:, m * D:m * D + TP], W1[:, e, k, m * P:m * P + P],
                                             uT[:, k, :], start=(k == 0), stop=(k == KD - 1))
                    last.then_inc(c_A, 1)

                def body(j, front, post, ahead):
                    wait(pe, c_in, j + 1)
                    hidden(j, 0)
                    hidden(j, 1)
                    turn_weights(j)
                    expert_biases(j)
                    if front:
                        weighted_sums(j + 1, 1)
                    for e in range(EX):
                        n = EX * j + e
                        src = h1 if e % 2 == 0 else h2
                        wait(pe, c_g, 2 * n + 2)
                        wait(pe, c_acc, 2 * (n - 1))
                        for u in range(2):
                            for k in range(KD):
                                last = pe.matmul(ps[4 + e % 2][0:T, u * D:u * D + D], src[:, k, u * T:u * T + T],
                                                 W2[:, e, k, :], start=(k == 0), stop=(k == KD - 1))
                        last.then_inc(c_Y, 1)
                        if e == 0 and ahead:
                            turn_max(j + 2, 0)
                        if e + 2 < EX:
                            hidden(j, e + 2)
                        if e == 0 and front:
                            mixer(j + 1)
                        if e == 0 and ahead:
                            shift_row(j + 2, 0)
                        if e == 3 and ahead:
                            weighted_sums(j + 2, 0)
                        if e == 3 and front:
                            turn_x3(j + 1)
                        if e == 4 and front:
                            logits(j + 1)
                        if e == 4 and ahead:
                            turn_max(j + 2, 1)
                        if e == 5 and ahead:
                            shift_row(j + 2, 1)

                turn_max(0, 0)
                shift_row(0, 0)
                turn_max(0, 1)
                weighted_sums(0, 0)
                shift_row(0, 1)
                weighted_sums(0, 1)
                mixer(0)
                turn_x3(0)
                turn_max(1, 0)
                shift_row(1, 0)
                logits(0)
                weighted_sums(1, 0)
                turn_max(1, 1)
                shift_row(1, 1)
                pe.wait_ge(load_experts1, 64)
                pipeline(pe, body)

            @block.scalar
            def _(act):
                def edge_exp(i, u):
                    t = 2 * i + u
                    wait(act, c_row, t + 1)
                    wait(act, c_vm, t + 1)
                    for c in range(CH):
                        act.activation(big[:, u, c, :], ps[3][:, P:P + T], ACT.Exp,
                                       bias=ring[:, u, c, D + 1:D + 2]).then_inc(c_E, 1)

                def tanh(i):
                    wait(act, c_ball, BALL_STEPS * i + BALL_NORM)
                    act.activation(sm[:, 12, :], sm[:, 11, :], ACT.Tanh).then_inc(c_th, 1)

                def normalize_x3(i):
                    wait(act, c_nb, i + 1)
                    wait(act, c_x3, 5 * i)
                    for u in range(2):
                        act.activation(xn[:, u, :], xf1[:, u, :], ACT.Identity, bias=nb[:, u:u + 1],
                                       scale=rs[:, u:u + 1]).then_inc(c_u, 1)

                def copy_x3(i):
                    wait(act, c_uTp, i + 1)
                    wait(act, c_in, i)
                    act.copy(uTf[:, :, :], turned_pair(7)).then_inc(c_uT, 1)

                def router_exp(i):
                    wait(act, c_zs, i + 1)
                    act.activation(lg[:, 2, :, :], lg[:, 1, :, :], ACT.Exp).then_inc(c_e, 1)

                def hand_on(i):
                    wait(act, c_uT, i + 1)
                    wait(act, c_A, EX * i)
                    act.copy(uT[:, :, :], uTf[:, :, :]).then_inc(c_in, 1)

                def copy_weights(i):
                    wait(act, c_wTp, i + 1)
                    act.copy(wT[:, :], ps[7][0:EX, 0:TP]).then_inc(c_wT, 1)

                def gelu(j, e):
                    n = EX * j + e
                    wait(act, c_A, n + 1)
                    wait(act, c_Y, n - 1)
                    bank = 2 if e % 2 == 0 else 6
                    target = h1 if e % 2 == 0 else h2
                    for m in range(KD):
                        act.activation(target[:, m, :], ps[bank][:, m * D:m * D + TP], ACT.Gelu,
                                       bias=b1c[:, 2 * e + m:2 * e + m + 1]).then_inc(c_g, 1)

                def body(j, front, post, ahead):
                    copy_weights(j)
                    for e in range(3):
                        gelu(j, e)
                    if ahead:
                        edge_exp(j + 2, 0)
                    if front:
                        tanh(j + 1)
                    for e in range(3, 6):
                        gelu(j, e)
                    if front:
                        normalize_x3(j + 1)
                        copy_x3(j + 1)
                    for e in range(6, EX):
                        gelu(j, e)
                    if front:
                        router_exp(j + 1)
                        hand_on(j + 1)
                    if ahead:
                        edge_exp(j + 2, 1)

                edge_exp(0, 0)
                edge_exp(0, 1)
                for stage in (tanh, normalize_x3, copy_x3):
                    stage(0)
                edge_exp(1, 0)
                router_exp(0)
                hand_on(0)
                edge_exp(1, 1)
                pipeline(act, body)

            @block.vector
            def _(dve):
                def steps(semaphore, before):
                    done = [0]

                    def step(ins):
                        done[0] += 1
                        ins.then_inc(semaphore, 1)
                        dve.wait_ge(semaphore, before + done[0])
                    return step

                def one_hot(i, u):
                    t = i * 2 + u
                    wait(dve, c_P, t - 1)
                    dve.tensor_tensor(hot[:, u, :, :], col(relw[:, bass.ds(t * CH, CH)], T),
                                      mid(iota[:, :], CH), ALU.is_equal).then_inc(c_hot, 1)

                def maxima(i, u):
                    t = i * 2 + u
                    wait(dve, c_rows[u], 16 * CH * (i + 1))
                    dve.tensor_scalar(hk[:, u, :], ring[:, u, :, D + 1], hbound[:, 0:1], None, ALU.add)\
                        .then_inc(c_hk, 1)
                    wait(dve, c_hk, t + 1)
                    wait(dve, c_hot, t + 1)
                    wait(dve, c_agg, t - 1)
                    dve.tensor_tensor(big[:, u, :, :], hot[:, u, :, :], col(hk[:, u, :], T), ALU.mult)\
                        .then_inc(c_V, 1)
                    wait(dve, c_V, t + 1)
                    wait(dve, c_vT, t - 1)
                    dve.tensor_reduce(vm[:, u, :], big[:, u, :, :].rearrange("p c d -> p d c"), AX, ALU.max)\
                        .then_inc(c_vm, 1)

                def shift(i, u):
                    t = i * 2 + u
                    step = steps(c_chain, 4 * t)
                    ht = ht_all[:, bass.ds(t, 1)]
                    m, s = sm[:, 0, u:u + 1], sm[:, 1, u:u + 1]
                    wait(dve, c_vT, t + 1)
                    step(dve.tensor_reduce(m, ps[3][0:T, 0:P], AX, ALU.max))
                    step(dve.tensor_scalar(s, m, nbound[0:T, 0:1], ht, ALU.add, ALU.add))
                    step(dve.tensor_scalar(s, s, -1e9, ht, ALU.max, ALU.subtract))
                    step(dve.scalar_tensor_tensor(s, m, 0.0, s, ALU.is_gt, ALU.mult))
                    wait(dve, c_row, t - 1)
                    dve.tensor_scalar(dg[:, u, :], ident[0:T, 0:T], s, -1.0, ALU.mult, ALU.mult).then_inc(c_dg, 1)

                def edge_weights(i, u):
                    t = i * 2 + u
                    wait(dve, c_E, CH * (t + 1))
                    dve.scalar_tensor_tensor(big[:, u, :, :], big[:, u, :, :], FAR, hot[:, u, :, :],
                                             ALU.min, ALU.mult).then_inc(c_P, 1)

                def combine(i):
                    wait(dve, c_x, 16 * (i + 1))
                    wait(dve, c_x3, 5 * i)
                    dve.tensor_tensor(tmp[:, :, :], xin[:, :, :], mid(bias1[:, :], 2), ALU.add).then_inc(c_xb, 1)
                    for u in range(2):
                        wait(dve, c_agg, 2 * i + u + 1)
                        dve.tensor_scalar(sm[:, 5, u:u + 1], ps[u][0:T, D:D + 1], 1e-10, None, ALU.add).then_inc(c_se, 1)
                    wait(dve, c_se, 3 * i + 2)
                    dve.reciprocal(sm[:, 6, :], sm[:, 5, :]).then_inc(c_se, 1)
                    wait(dve, c_se, 3 * i + 3)
                    wait(dve, c_base, 16 * (i + 1))
                    for u in range(2):
                        dve.scalar_tensor_tensor(hn[:, u, :], ps[u][0:T, 0:D], sm[:, 6, u:u + 1], base[:, u, :],
                                                 ALU.mult, ALU.add).then_inc(c_hc, 1)

                def ball_norm(i):
                    for u in range(2):
                        wait(dve, c_hc, 2 * i + u + 1)
                        dve.tensor_tensor_reduce(squared[:, u, :], hn[:, u, :], hn[:, u, :], 1.0, 0.0, ALU.mult,
                                                 ALU.add, sm[:, 7, u:u + 1]).then_inc(c_ss, 1)
                    wait(dve, c_ss, 2 * i + 2)
                    step = steps(c_ball, BALL_STEPS * i)
                    inverse_root(dve, step, sm[:, 10, :], sm[:, 7, :], sm[:, 13, :])
                    step(dve.tensor_tensor(sm[:, 10, :], sm[:, 10, :], sm[:, 7, :], ALU.mult))
                    step(dve.tensor_scalar(sm[:, 11, :], sm[:, 10, :], 1e-15, None, ALU.max))
                    step(dve.reciprocal(sm[:, 13, :], sm[:, 11, :]))

                def ball_scale(i):
                    step = steps(c_ball, BALL_STEPS * i + BALL_NORM + 1)
                    wait(dve, c_th, i + 1)
                    step(dve.tensor_tensor(sm[:, 14, :], sm[:, 12, :], sm[:, 13, :], ALU.mult))
                    step(dve.tensor_tensor(sm[:, 15, :], sm[:, 14, :], sm[:, 10, :], ALU.mult))
                    step(dve.tensor_scalar(sm[:, 16, :], sm[:, 15, :], 1e-8, None, ALU.add))
                    step(dve.reciprocal(sm[:, 17, :], sm[:, 16, :]))
                    step(dve.tensor_scalar(sm[:, 17, :], sm[:, 17, :], MAX_NORM, 1.0, ALU.mult, ALU.subtract))
                    step(dve.scalar_tensor_tensor(sm[:, 18, :], sm[:, 15, :], MAX_NORM, sm[:, 17, :],
                                                  ALU.is_gt, ALU.mult))
                    step(dve.scalar_tensor_tensor(sm[:, 19, :], sm[:, 18, :], 1.0, sm[:, 14, :], ALU.add, ALU.mult))

                def x3(i):
                    wait(dve, c_lin, i + 1)
                    wait(dve, c_xb, i + 1)
                    if not isinstance(i, int) or i > 0:
                        wait(dve, c_acc, 2 * EX * (i - 1) + 2)
                    dve.tensor_tensor(xf1, tmp[:, :, :], bank2(7), ALU.add).then_inc(c_x3, 1)
                    wait(dve, c_x3, 5 * i + 1)
                    for u in range(2):
                        dve.scalar_tensor_tensor(xf1[:, u, :], hn[:, u, :], sm[:, 19, u:u + 1], xf1[:, u, :],
                                                 ALU.mult, ALU.add).then_inc(c_x3, 1)
                    wait(dve, c_x3, 5 * i + 3)
                    norm(dve, xf1, st, mv, sm[:, 14, :], sm[:, 15, :], rs[:, :], nb[:, :], c_norm, NORM_STEPS * i,
                         (c_u, 2 * i), c_nb)

                def router(i):
                    step = steps(c_top, TOP_STEPS * i)
                    wait(dve, c_lg, i + 1)
                    z = ps[7][0:T, 0:2 * EX].rearrange("p (u e) -> p u e", u=2)
                    step(dve.tensor_reduce(sm[:, 20, :], z, AX, ALU.max))
                    dve.tensor_tensor(lg[:, 1, :, :], z, col(sm[:, 20, :], EX), ALU.subtract).then_inc(c_zs, 1)

                def shares(i):
                    step = steps(c_top, TOP_STEPS * i + 1)
                    io = mid(iota8[:, :], 2)
                    wait(dve, c_e, i + 1)
                    step(dve.tensor_reduce(sm[:, 21, :], lg[:, 2, :, :], AX, ALU.add))
                    step(dve.reciprocal(sm[:, 22, :], sm[:, 21, :]))
                    step(dve.tensor_tensor(lg[:, 3, :, :], lg[:, 2, :, :], col(sm[:, 22, :], EX), ALU.mult))
                    for best in range(2):
                        p = lg[:, 3, :, :] if best == 0 else lg[:, 6, :, :]
                        step(dve.tensor_reduce(sm[:, 8 + best, :], p, AX, ALU.max))
                        step(dve.tensor_tensor(lg[:, 0, :, :], p, col(sm[:, 8 + best, :], EX), ALU.not_equal))
                        step(dve.scalar_tensor_tensor(lg[:, 0, :, :], lg[:, 0, :, :], 99.0, io, ALU.mult, ALU.add))
                        step(dve.tensor_reduce(sm[:, 23, :], lg[:, 0, :, :], AX, ALU.min))
                        if best == 0:
                            step(dve.tensor_tensor(lg[:, 4, :, :], io, col(sm[:, 23, :], EX), ALU.is_equal))
                            step(dve.scalar_tensor_tensor(lg[:, 6, :, :], lg[:, 4, :, :], -2.0, lg[:, 3, :, :],
                                                          ALU.mult, ALU.add))
                        else:
                            dve.tensor_tensor(lg[:, 7, :, :], io, col(sm[:, 23, :], EX), ALU.is_equal).then_inc(c_w2, 1)
                    step(dve.tensor_tensor(sm[:, 20, :], sm[:, 8, :], sm[:, 9, :], ALU.add))
                    wait(dve, c_w2, 2 * i + 1)
                    dve.tensor_tensor(lg[:, 7, :, :], lg[:, 7, :, :], lg[:, 4, :, :], ALU.add).then_inc(c_w2, 1)
                    wait(dve, c_w2, 2 * i + 2)
                    step(dve.tensor_scalar(sm[:, 20, :], sm[:, 20, :], 1e-12, None, ALU.max))
                    step(dve.reciprocal(sm[:, 21, :], sm[:, 20, :]))
                    step(dve.tensor_tensor(lg[:, 7, :, :], lg[:, 7, :, :], lg[:, 3, :, :], ALU.mult))
                    wait(dve, c_wE, i)
                    wait(dve, c_wTp, i)
                    dve.tensor_tensor(lg[:, 5, :, :], lg[:, 7, :, :], col(sm[:, 21, :], EX), ALU.mult).then_inc(c_w, 1)

                def add_input(i):
                    wait(dve, c_u, 2 * i + 2)
                    dve.tensor_tensor(xf1, xf1, xn[:, :, :], ALU.add).then_inc(c_x3, 1)
                    wait(dve, c_x3, 5 * i + 4)
                    wait(dve, c_b2, i + 1)
                    dve.tensor_tensor(xf1, xf1, bank2(7), ALU.add).then_inc(c_x3, 1)

                def keep_weights(j):
                    wait(dve, c_w, j + 1)
                    wait(dve, c_acc, 2 * EX * j)
                    dve.tensor_copy(wE[:, :, :], lg[:, 5, :, :]).then_inc(c_wE, 1)

                def add_expert(j, e):
                    n = EX * j + e
                    wait(dve, c_Y, n + 1)
                    if e == 0:
                        wait(dve, c_wE, j + 1)
                        wait(dve, c_x3, 5 * (j + 1))
                    if e == EX - 1:
                        wait(dve, c_out, 16 * j)
                    source = xf1 if e == 0 else acc
                    target = x4 if e == EX - 1 else acc
                    for u in range(2):
                        wait(dve, c_acc, 2 * n - 1 + u)
                        dve.scalar_tensor_tensor(target[:, u, :], bank2(4 + e % 2)[:, u, :], wE[:, u, e:e + 1],
                                                 source[:, u, :], ALU.mult, ALU.add).then_inc(c_acc, 1)

                def body(j, front, post, ahead):
                    keep_weights(j)
                    add_input(j)
                    if ahead:
                        one_hot(j + 2, 0)
                        maxima(j + 2, 0)
                    if front:
                        combine(j + 1)
                    add_expert(j, 0)
                    if ahead:
                        shift(j + 2, 0)
                    if front:
                        ball_norm(j + 1)
                    add_expert(j, 1)
                    if ahead:
                        edge_weights(j + 2, 0)
                    if front:
                        ball_scale(j + 1)
                    add_expert(j, 2)
                    if front:
                        x3(j + 1)
                    add_expert(j, 3)
                    if ahead:
                        one_hot(j + 2, 1)
                        maxima(j + 2, 1)
                    add_expert(j, 4)
                    if ahead:
                        shift(j + 2, 1)
                    if front:
                        router(j + 1)
                    add_expert(j, 5)
                    if front:
                        shares(j + 1)
                    add_expert(j, 6)
                    if ahead:
                        edge_weights(j + 2, 1)
                    add_expert(j, 7)

                one_hot(0, 0)
                maxima(0, 0)
                shift(0, 0)
                one_hot(0, 1)
                maxima(0, 1)
                edge_weights(0, 0)
                shift(0, 1)
                edge_weights(0, 1)
                one_hot(1, 0)
                for stage in (combine, ball_norm, ball_scale, x3):
                    stage(0)
                maxima(1, 0)
                shift(1, 0)
                one_hot(1, 1)
                router(0)
                shares(0)
                edge_weights(1, 0)
                maxima(1, 1)
                shift(1, 1)
                edge_weights(1, 1)
                pipeline(dve, body)


_INS = ['x', 'src', 'dst', 'L0_gnn_W_left', 'L0_gnn_b_left', 'L0_gnn_W_right', 'L0_mix_w_qkv', 'L0_mix_w_out',
        'L0_mix_b_out', 'L0_ffn_Wr', 'L0_ffn_br', 'L0_ffn_W1', 'L0_ffn_b1', 'L0_ffn_g1', 'L0_ffn_be1', 'L0_ffn_m1',
        'L0_ffn_v1', 'L0_ffn_W2', 'L0_ffn_b2', 'L0_ffn_g2', 'L0_ffn_be2', 'L0_ffn_m2', 'L0_ffn_v2', 'L0_ffn_Wo',
        'L0_ffn_bo', 'L1_gnn_W', 'L1_gnn_b', 'L1_gnn_mag_w', 'L1_gnn_mag_b', 'L1_gnn_attn_w', 'L1_mix_W_qkv',
        'L1_mix_W_out', 'L1_mix_b_out', 'L1_ffn_router_w', 'L1_ffn_w1', 'L1_ffn_b1', 'L1_ffn_w2', 'L1_ffn_b2']


def kernel(**inputs):
    import numpy as _np
    import concourse.bacc as _bacc
    from concourse import mybir as _mybir
    from concourse.bass_utils import run_bass_kernel_spmd as _run

    nc = _bacc.Bacc("TRN2", target_bir_lowering=False, num_devices=1)
    arrays, aps = {}, {}
    for name in _INS:
        arr = _np.ascontiguousarray(inputs[name])
        arrays[f"in_{name}"] = arr
        aps[name] = nc.dram_tensor(f"in_{name}", arr.shape, _mybir.dt.from_np(arr.dtype), kind="ExternalInput").ap()
    out = nc.dram_tensor("out_0", (N, D), F32, kind="ExternalOutput").ap()
    gps_kernel(nc, aps, out)
    r = _run(nc, [arrays], core_ids=[0])
    return r.results[0]["out_0"]
```
